# Optimizing a Trainium2 kernel written in Bass

```python
import numpy as np
import jax
import jax.numpy as jnp

def _softmax(x, axis=-1):
    return jax.nn.softmax(x, axis=axis)

def _gelu(x):
    return jax.nn.gelu(x, approximate=True)

def _silu(x):
    return jax.nn.silu(x)

def _sigmoid(x):
    return jax.nn.sigmoid(x)

def _layernorm(x, axis=-1, eps=1e-05):
    m = jnp.mean(x, axis=axis, keepdims=True)
    v = jnp.var(x, axis=axis, keepdims=True)
    return (x - m) / jnp.sqrt(v + eps)

def _scatter_add(tgt, idx, src, axis=0):
    return tgt.at[idx].add(src)

def _segment_sum(src, seg, n):
    return jax.ops.segment_sum(src, seg, n)
kernel_name = 'mk_gnn_resnorm_d4_gnn_r64_590b6a'

def setup_inputs(seed: int=0):
    np.random.seed(seed)
    _w = jnp.asarray

    def _rec_inputs():
        import jax
        import jax.numpy as jnp
        _gk = jax.random.key(seed)
        x = -0.0002117 + 1 * jax.random.normal(jax.random.fold_in(_gk, 1), (50000, 256), jnp.float32)
        src = jax.random.randint(jax.random.fold_in(_gk, 2), (25000,), 0, 50000, jnp.int32)
        dst = jax.random.randint(jax.random.fold_in(_gk, 3), (25000,), 0, 50000, jnp.int32)
        _o = jnp.argsort(dst, stable=True)
        src = src[_o]
        dst = dst[_o]
        edge_type_16 = jax.random.randint(jax.random.fold_in(_gk, 13), (25000,), 0, 16, jnp.int32)
        edge_type_24 = jax.random.randint(jax.random.fold_in(_gk, 14), (25000,), 0, 24, jnp.int32)
        edge_weight = jax.random.uniform(jax.random.fold_in(_gk, 15), (25000,), jnp.float32, 0.0, 1)
        return (x, src, dst, edge_type_16, edge_type_24, edge_weight)
    x, src, dst, edge_type_16, edge_type_24, edge_weight = _rec_inputs()

    def _L0_gnn_setup():
        import jax, jax.numpy as jnp
        import numpy as np
        N = 100000
        E = 50000
        F = 256
        O = 256
        EPS = 1e-05
        key = jax.random.key(seed)
        k0, k1, k2, k3, k4 = jax.random.split(key, 5)
        x = jax.random.normal(k0, (N, F), dtype=jnp.float32)
        edge_row = jax.random.randint(k1, (E,), 0, N, dtype=jnp.int32)
        edge_col = jax.random.randint(k2, (E,), 0, N, dtype=jnp.int32)
        edge_weight = jax.random.uniform(k3, (E,), dtype=jnp.float32)
        bound = float(np.sqrt(6.0 / (O + 2 * F)))
        W = jax.random.uniform(k4, (O, 2 * F), minval=-bound, maxval=bound, dtype=jnp.float32)
        gamma = jnp.ones((O,), dtype=jnp.float32)
        beta = jnp.zeros((O,), dtype=jnp.float32)
        return {'x': x, 'W': W, 'gamma': gamma, 'beta': beta, 'edge_weight': edge_weight, 'edge_row': edge_row, 'edge_col': edge_col}
    _L0_gnn_all = _L0_gnn_setup()
    _L0_gnn_in = {k: v for k, v in _L0_gnn_all.items() if k in ('W', 'gamma', 'beta')}
    del _L0_gnn_all

    def _L1_gnn_setup():
        import jax, jax.numpy as jnp
        import numpy as np
        NUM_BLOCKS = 64

        def rgcn_layer(x, src, dst, edge_type, W, root, bias):
            N, d = x.shape
            xj = x[src]
            out0 = x @ root + bias

            def body(out, inputs):
                r, Wr = inputs
                mask = (edge_type == r).astype(x.dtype)
                s = jax.ops.segment_sum(xj * mask[:, None], dst, num_segments=N)
                cnt = jax.ops.segment_sum(mask, dst, num_segments=N)
                h = s / jnp.maximum(cnt, 1.0)[:, None]
                hb = h.reshape(N, NUM_BLOCKS, d // NUM_BLOCKS)
                out = out + jnp.einsum('nbi,bio->nbo', hb, Wr).reshape(N, d)
                return (out, None)
            R = W.shape[0]
            out, _ = jax.lax.scan(body, out0, (jnp.arange(R), W))
            return out
        key = jax.random.key(seed)
        ks = jax.random.split(key, 9)
        N, d, R, E = (50000, 256, 16, 12500)
        db = d // NUM_BLOCKS
        return {'node_emb': jax.random.normal(ks[0], (N, d), jnp.float32), 'edge_index': jax.random.randint(ks[1], (2, E), 0, N), 'edge_type': jax.random.randint(ks[2], (E,), 0, R), 'W1': jax.random.normal(ks[3], (R, NUM_BLOCKS, db, db), jnp.float32) * 0.1, 'root1': jax.random.normal(ks[4], (d, d), jnp.float32) * 0.05, 'bias1': jnp.zeros((d,), jnp.float32), 'W2': jax.random.normal(ks[5], (R, NUM_BLOCKS, db, db), jnp.float32) * 0.1, 'root2': jax.random.normal(ks[6], (d, d), jnp.float32) * 0.05, 'bias2': jnp.zeros((d,), jnp.float32)}
    _L1_gnn_all = _L1_gnn_setup()
    _L1_gnn_in = {k: v for k, v in _L1_gnn_all.items() if k in ('W1', 'root1', 'bias1', 'W2', 'root2', 'bias2')}
    del _L1_gnn_all

    def _L2_gnn_setup():
        import jax, jax.numpy as jnp
        import numpy as np
        N_ENT, N_REL, C, E = (100000, 24, 256, 300000)
        key = jax.random.key(seed)
        k1, k2, k3, k4, k5, k6 = jax.random.split(key, 6)
        return {'entity_emb': jax.random.normal(k1, (N_ENT, C), dtype=jnp.float32) * 0.1, 'relation_emb': jax.random.normal(k2, (N_REL, C), dtype=jnp.float32) * 0.1, 'fc_w': jax.random.normal(k3, (C, 2 * C), dtype=jnp.float32) * 0.05, 'fc_b': jax.random.normal(k4, (C,), dtype=jnp.float32) * 0.01, 'edge_index': jax.random.randint(k5, (2, E), 0, N_ENT, dtype=jnp.int32), 'edge_type': jax.random.randint(k6, (E,), 0, N_REL, dtype=jnp.int32), 'n_hops': 2}
    _L2_gnn_all = _L2_gnn_setup()
    _L2_gnn_in = {k: v for k, v in _L2_gnn_all.items() if k in ('relation_emb', 'fc_w', 'fc_b')}
    del _L2_gnn_all

    def _L3_gnn_setup():
        import jax, jax.numpy as jnp
        import numpy as np
        N_NODES = 100000
        N_EDGES = 50000
        DIM = 256
        LEAKY_SLOPE = 0.2
        EPS = 1e-12
        key = jax.random.key(seed)
        ks = jax.random.split(key, 8)
        embeddings = jax.random.normal(ks[0], (N_NODES, DIM), dtype=jnp.float32)
        edge_src = jax.random.randint(ks[1], (N_EDGES,), 0, N_NODES, dtype=jnp.int32)
        edge_dst = jax.random.randint(ks[2], (N_EDGES,), 0, N_NODES, dtype=jnp.int32)
        edge_val = jax.random.uniform(ks[3], (N_EDGES,), dtype=jnp.float32) / 32.0
        scale = 1.0 / np.sqrt(DIM)
        W1 = jax.random.normal(ks[4], (DIM, DIM), dtype=jnp.float32) * scale
        b1 = jax.random.normal(ks[5], (DIM,), dtype=jnp.float32) * 0.01
        W2 = jax.random.normal(ks[6], (DIM, DIM), dtype=jnp.float32) * scale
        b2 = jax.random.normal(ks[7], (DIM,), dtype=jnp.float32) * 0.01
        return {'embeddings': embeddings, 'edge_src': edge_src, 'edge_dst': edge_dst, 'edge_val': edge_val, 'W1': W1, 'b1': b1, 'W2': W2, 'b2': b2}
    _L3_gnn_all = _L3_gnn_setup()
    _L3_gnn_in = {k: v for k, v in _L3_gnn_all.items() if k in ('W1', 'b1', 'W2', 'b2')}
    del _L3_gnn_all
    return {'x': x, 'src': src, 'dst': dst, 'edge_type_16': edge_type_16, 'edge_type_24': edge_type_24, 'edge_weight': edge_weight, 'L0_gnn_W': _L0_gnn_in['W'], 'L0_gnn_gamma': _L0_gnn_in['gamma'], 'L0_gnn_beta': _L0_gnn_in['beta'], 'L1_gnn_W1': _L1_gnn_in['W1'], 'L1_gnn_root1': _L1_gnn_in['root1'], 'L1_gnn_bias1': _L1_gnn_in['bias1'], 'L1_gnn_W2': _L1_gnn_in['W2'], 'L1_gnn_root2': _L1_gnn_in['root2'], 'L1_gnn_bias2': _L1_gnn_in['bias2'], 'L2_gnn_relation_emb': _L2_gnn_in['relation_emb'], 'L2_gnn_fc_w': _L2_gnn_in['fc_w'], 'L2_gnn_fc_b': _L2_gnn_in['fc_b'], 'L3_gnn_W1': _L3_gnn_in['W1'], 'L3_gnn_b1': _L3_gnn_in['b1'], 'L3_gnn_W2': _L3_gnn_in['W2'], 'L3_gnn_b2': _L3_gnn_in['b2']}

def reference(x, src, dst, edge_type_16, edge_type_24, edge_weight, L0_gnn_W, L0_gnn_gamma, L0_gnn_beta, L1_gnn_W1, L1_gnn_root1, L1_gnn_bias1, L1_gnn_W2, L1_gnn_root2, L1_gnn_bias2, L2_gnn_relation_emb, L2_gnn_fc_w, L2_gnn_fc_b, L3_gnn_W1, L3_gnn_b1, L3_gnn_W2, L3_gnn_b2):
    import jax
    import jax.numpy as jnp

    def _L0_gnn_ref(x, W, gamma, beta, edge_weight, edge_row, edge_col):
        import jax, jax.numpy as jnp
        import numpy as np
        N = 100000
        E = 50000
        F = 256
        O = 256
        EPS = 1e-05
        agg = jax.ops.segment_sum(edge_weight[:, None] * x[edge_col], edge_row, num_segments=x.shape[0])
        support = jnp.concatenate([agg, x], axis=1)
        out = support @ W.T
        mu = jnp.mean(out, axis=-1, keepdims=True)
        var = jnp.mean(jnp.square(out - mu), axis=-1, keepdims=True)
        out = (out - mu) * jax.lax.rsqrt(var + EPS) * gamma + beta
        return jax.nn.relu(out)

    def _L1_gnn_ref(node_emb, edge_index, edge_type, W1, root1, bias1, W2, root2, bias2):
        import jax, jax.numpy as jnp
        import numpy as np
        NUM_BLOCKS = 64

        def rgcn_layer(x, src, dst, edge_type, W, root, bias):
            N, d = x.shape
            xj = x[src]
            out0 = x @ root + bias

            def body(out, inputs):
                r, Wr = inputs
                mask = (edge_type == r).astype(x.dtype)
                s = jax.ops.segment_sum(xj * mask[:, None], dst, num_segments=N)
                cnt = jax.ops.segment_sum(mask, dst, num_segments=N)
                h = s / jnp.maximum(cnt, 1.0)[:, None]
                hb = h.reshape(N, NUM_BLOCKS, d // NUM_BLOCKS)
                out = out + jnp.einsum('nbi,bio->nbo', hb, Wr).reshape(N, d)
                return (out, None)
            R = W.shape[0]
            out, _ = jax.lax.scan(body, out0, (jnp.arange(R), W))
            return out
        src, dst = (edge_index[0], edge_index[1])
        x = jax.nn.relu(rgcn_layer(node_emb, src, dst, edge_type, W1, root1, bias1))
        x = rgcn_layer(x, src, dst, edge_type, W2, root2, bias2)
        return x

    def _L2_gnn_ref(entity_emb, relation_emb, fc_w, fc_b, edge_index, edge_type, n_hops):
        import jax, jax.numpy as jnp
        import numpy as np
        N_ENT, N_REL, C, E = (100000, 24, 256, 300000)
        N = entity_emb.shape[0]
        head, tail = (edge_index[0], edge_index[1])
        rel_e = relation_emb[edge_type]

        def agg(x):
            a_input = jnp.concatenate([x[head], x[tail]], axis=-1)
            e = jnp.sum((a_input @ fc_w.T + fc_b) * rel_e, axis=-1)
            e = jnp.where(e > 0, e, 0.2 * e)
            m = jax.ops.segment_max(e, head, num_segments=N)
            ex = jnp.exp(e - jax.lax.stop_gradient(m)[head])
            denom = jax.ops.segment_sum(ex, head, num_segments=N)
            w = ex / denom[head]
            agg_emb = jax.ops.segment_sum(x[tail] * w[:, None], head, num_segments=N)
            return agg_emb + x
        x = entity_emb
        res = entity_emb
        for _ in range(n_hops):
            x = agg(x)
            norm = jnp.maximum(jnp.linalg.norm(x, axis=-1, keepdims=True), 1e-12)
            x = x / norm
            res = res + x
        return x

    def _L3_gnn_ref(embeddings, edge_src, edge_dst, edge_val, W1, b1, W2, b2):
        import jax, jax.numpy as jnp
        import numpy as np
        N_NODES = 100000
        N_EDGES = 50000
        DIM = 256
        LEAKY_SLOPE = 0.2
        EPS = 1e-12
        ego_emb = embeddings @ W1.T + b1
        messages = edge_val[:, None] * embeddings[edge_src]
        neighbor_emb = jax.ops.segment_sum(messages, edge_dst, num_segments=embeddings.shape[0])
        interaction_emb = neighbor_emb * embeddings
        side_emb = (neighbor_emb + interaction_emb) @ W2.T + b2
        out = ego_emb + side_emb
        out = jnp.where(out >= 0, out, LEAKY_SLOPE * out)
        norm = jnp.sqrt(jnp.sum(out * out, axis=1, keepdims=True))
        return out / jnp.maximum(norm, EPS)
    edge_index = jnp.stack([src, dst])
    x = _layernorm(x + _L0_gnn_ref(x, L0_gnn_W, L0_gnn_gamma, L0_gnn_beta, edge_weight, src, dst), axis=-1)
    x = _layernorm(x + _L1_gnn_ref(x, edge_index, edge_type_16, L1_gnn_W1, L1_gnn_root1, L1_gnn_bias1, L1_gnn_W2, L1_gnn_root2, L1_gnn_bias2), axis=-1)
    x = _layernorm(x + _L2_gnn_ref(x, L2_gnn_relation_emb, L2_gnn_fc_w, L2_gnn_fc_b, edge_index, edge_type_24, 2), axis=-1)
    x = _layernorm(x + _L3_gnn_ref(x, src, dst, edge_weight, L3_gnn_W1, L3_gnn_b1, L3_gnn_W2, L3_gnn_b2), axis=-1)
    return x

_drawn_inputs = setup_inputs


def setup_inputs(seed=0):
    import zlib

    import numpy as np

    out = dict(_drawn_inputs(seed))
    spreads = {'L0_gnn_gamma': (1.0, 0.2),
     'L0_gnn_beta': (0.0, 0.1),
     'L1_gnn_bias1': (0.0, 0.1),
     'L1_gnn_bias2': (0.0, 0.1)}
    factors = {'L2_gnn_relation_emb': 200.0,
     'L2_gnn_fc_w': 200.0,
     'L2_gnn_fc_b': 200.0,
     'L3_gnn_b1': 64.0,
     'L3_gnn_b2': 64.0,
     'L3_gnn_W2': 2.97}
    for name, (base, spread) in spreads.items():
        noise = np.random.default_rng([zlib.crc32(name.encode()), seed]).standard_normal(out[name].shape)
        drawn = base * np.exp(spread * noise) if base else spread * noise
        out[name] = jnp.asarray(drawn.astype(out[name].dtype))
    for name, factor in factors.items():
        out[name] = (out[name] * factor).astype(out[name].dtype)
    return out
```

```python
from contextlib import ExitStack

import numpy as np

import concourse.bass as bass
from concourse import mybir

F32 = mybir.dt.float32
BF16 = mybir.dt.bfloat16
F16 = mybir.dt.float16
I32 = mybir.dt.int32
ALU = mybir.AluOpType
ACT = mybir.ActivationFunctionType
AX = mybir.AxisListType

P = 128
N_NODES, D, N_EDGES = 50000, 256, 25000
TILES = -(-N_NODES // P)
ROWS = TILES * P
RING = 8
ALL_ROWS = ROWS + RING * P
EP, EC = 125, 200
MAX_ITEMS = TILES + N_EDGES // P
ITEM_CHUNKS = -(-(MAX_ITEMS + 3 * RING) // P)
ITEMS = ITEM_CHUNKS * P
SORTED = N_EDGES + P
R1, R2 = 16, 24
GROUP = 32
K3 = 3 * GROUP
EPS = 1e-5
FAR = float(1 << 20)
assert EP * EC == N_EDGES and max(R1, R2) < GROUP
OTHER, NODE, KIND, WEIGHT = range(4)
START, LOAD, STORE = range(3)


class Graph:

    def __init__(self, sb, name):
        self.meta = sb(f"{name}_meta", [P, ITEMS, 4], F32)
        self.keep = sb(f"{name}_keep", [P, ITEMS], F32)
        self.share = sb(f"{name}_share", [P, ITEMS], F32)
        self.table = sb(f"{name}_table", [1, 3, ITEMS], I32)
        self.groups = sb(f"{name}_groups", [1, 1], I32)


    def prepare(self, sb, name):
        self.first_row = sb(f"{name}_first_row", [P, ITEMS], F32)
        self.buckets = {k: sb(f"{name}_{k}", [P, TILES + 1], I32 if k.startswith("int") else F32)
                        for k in ("count", "start", "end", "base", "int", "int2")}


def at(group, offset):
    return group * RING + offset, offset % RING, group + offset // RING


class Phase:

    def __init__(self, nc, name):
        self.nc, self.name, self.sems, self.ctx = nc, name, [], ExitStack()

    def __enter__(self):
        self.ctx.__enter__()
        return self

    def sem(self, name):
        s = self.ctx.enter_context(self.nc.semaphore(f"{self.name}_{name}"))
        self.sems.append(s)
        return s

    def pool_dma_sem(self, name):
        return self.nc.alloc_semaphore(f"{self.name}_{name}")

    def sb(self, name, shape, dt):
        return self.ctx.enter_context(self.nc.sbuf_tensor(f"{self.name}_{name}", shape, dt))

    def ps(self, name, shape, dt=F32):
        return self.ctx.enter_context(self.nc.psum_tensor(f"{self.name}_ps_{name}", shape, dt))

    def __exit__(self, *error):
        if error[0] is None:
            for s in self.sems:
                self.nc.gpsimd.sem_clear(s)
            self.nc.all_engine_barrier()
        return self.ctx.__exit__(*error)


def row_of(eng, graph, field, item):
    return eng.value_load(graph.table[0:1, field, bass.ds(item, 1)], min_val=0, max_val=ALL_ROWS - P)


def load_groups(eng, graph):
    return eng.value_load(graph.groups[0:1, 0:1], min_val=1, max_val=(ITEMS - 2 * RING) // RING)


def move_tiles(sp, graph, s, tiles, source, result, target, residual=None):
    def load(item, slot):
        row = row_of(sp, graph, LOAD, item)
        sp.dma_start(tiles[:, slot, :], source[bass.ds(row, P), :]).then_inc(s["in_x"][slot], 16)
        if residual is not None:
            sp.dma_start(residual[0][:, slot, :], residual[1][bass.ds(row, P), :]).then_inc(s["in_res"][slot], 16)

    sp.wait_ge(s["zeroed"], 2)
    for slot in range(RING):
        sp.dma_start(target[ROWS + slot * P:ROWS + (slot + 1) * P, :], result[:, slot, :]).then_inc(s["stored"][slot], 16)
    for k in range(RING):
        load(k, k)
    groups = load_groups(sp, graph)
    with sp.Fori(0, groups) as g:
        for k in range(RING):
            item, slot, _ = at(g, k)
            row = row_of(sp, graph, STORE, item)
            sp.wait_ge(s["out_ready"], item + 1)
            sp.dma_start(target[bass.ds(row, P), :], result[:, slot, :]).then_inc(s["stored"][slot], 16)
            nrow = row_of(sp, graph, LOAD, item + RING)
            sp.wait_ge(s[s["x_done"]], item + 1)
            sp.dma_start(tiles[:, slot, :], source[bass.ds(nrow, P), :]).then_inc(s["in_x"][slot], 16)
            if residual is not None:
                sp.wait_ge(s["res_done"], item + 1)
                sp.dma_start(residual[0][:, slot, :], residual[1][bass.ds(nrow, P), :])\
                    .then_inc(s["in_res"][slot], 16)
    for slot in range(RING):
        sp.wait_ge(s["stored"][slot], (groups + 1) * 16)
        sp.sem_inc(s["passed"], 1)
        sp.wait_ge(s["in_x"][slot], (groups + 1) * 16)
        sp.sem_inc(s["passed"], 1)
        if residual is not None:
            sp.wait_ge(s["in_res"][slot], (groups + 1) * 16)
            sp.sem_inc(s["passed"], 1)


def gather_rows(pool, graph, s, index, gathered, source):
    limit = pool.alloc_register(f"limit_{s['name']}")
    pool.reg_mov(limit, N_NODES - 1)
    for slot in range(RING):
        pool.memset(gathered[:, slot, :], 0.0).then_inc(s["g_zeroed"], 1)
    pool.wait_ge(s["g_zeroed"], RING)
    if gathered.shape[2] > D:
        for slot in range(RING):
            pool.memset(gathered[:, slot, D:], 1.0).then_inc(s["g_zeroed"], 1)
        pool.wait_ge(s["g_zeroed"], 2 * RING)

    def gather(item, slot):
        pool.tensor_copy(index[:, slot, :], graph.meta[:, bass.ds(item, 1), OTHER].bitcast(I32))\
            .then_inc(s["index_copied"], 1)
        pool.wait_ge(s["index_copied"], item + 1)
        pool.sem_inc(s["passed"], 1)
        pool.indirect_dma_start(gathered[:, slot, 0:D], None, source[0:N_NODES, :],
                                bass.IndirectOffsetOnAxis(ap=index[:, slot, :], axis=0),
                                bounds_check=limit, oob_is_err=False).then_inc(s["in_g"][slot], 16)

    for k in range(RING):
        gather(k, k)
    groups = load_groups(pool, graph)
    with pool.Fori(0, groups) as g:
        for k in range(RING):
            item, slot, _ = at(g, k)
            pool.wait_ge(s[s["g_last"]], item + 1)
            pool.sem_inc(s["passed"], 1)
            gather(item + RING, slot)
    for slot in range(RING):
        pool.wait_ge(s["in_g"][slot], (groups + 1) * 16)
        pool.sem_inc(s["passed"], 1)


def ring_sems(ph, x_done, g_done="g_done", residual=False):
    s = {k: ph.sem(k) for k in ("zeroed", "out_ready", "passed", "g_zeroed", "index_copied")}
    s["in_x"] = [ph.sem(f"in_x{k}") for k in range(RING)]
    s["in_g"] = [ph.pool_dma_sem(f"in_g{k}") for k in range(RING)]
    s["stored"] = [ph.sem(f"stored{k}") for k in range(RING)]
    if residual:
        s["in_res"] = [ph.sem(f"in_res{k}") for k in range(RING)]
        s["res_done"] = ph.sem("res_done")
    s["name"], s["x_done"], s["g_last"] = ph.name, x_done, g_done
    return s


class Chain:

    def __init__(self, eng, sem):
        self.eng, self.sem, self.count = eng, sem, 0

    def step(self, instruction):
        self.count += 1
        instruction.then_inc(self.sem, 1)
        self.eng.wait_ge(self.sem, self.count)


class Constants:
    def __init__(self, sb):
        self.iota16 = sb("iota16", [P, TILES + 1], F16)
        self.iota = sb("iota", [P, TILES + 1], F32)
        self.iota_kind = sb("iota_kind", [P, K3], F32)
        self.item_id = sb("item_id", [P, ITEM_CHUNKS], F32)
        self.spare_i = sb("spare_i", [P, ITEM_CHUNKS], I32)
        self.spare = sb("spare", [P, ITEM_CHUNKS], F32)
        self.ones_row = sb("ones_row", [P, TILES + 1], F32)
        self.zero_row = sb("zero_row", [P, TILES + 1], BF16)
        self.ones = sb("ones", [P, P], F32)
        self.ones_b = sb("ones_b", [P, P], BF16)
        self.zeros_b = sb("zeros_b", [P, P], BF16)
        self.ident = sb("ident", [P, P], F32)
        self.ident_b = sb("ident_b", [P, P], BF16)
        self.before = sb("before", [P, P], BF16)
        self.not_before = sb("not_before", [P, P], BF16)


def make_constants(nc, c):
    with Phase(nc, "const") as ph:
        made, numbered, spared = ph.sem("made"), ph.sem("numbered"), ph.sem("spared")
        with nc.Block() as block:
            @block.vector
            def _(dve):
                chain = Chain(dve, spared)
                dve.wait_ge(numbered, 1)
                chain.step(dve.tensor_single_scalar(c.spare_i[:], c.spare_i[:], RING - 1, op=ALU.bitwise_and))
                chain.step(dve.tensor_scalar(c.spare[:], c.spare_i[:], float(P), float(ROWS), ALU.mult, ALU.add))

            @block.gpsimd
            def _(pool):
                chain = Chain(pool, made)
                loose = dict(allow_small_or_imprecise_dtypes=True, channel_multiplier=0)
                pool.iota(c.iota16[:], [[1, TILES + 1]], 0, **loose)
                pool.iota(c.iota[:], [[1, TILES + 1]], 0, **loose)
                pool.iota(c.iota_kind[:], [[0, 3], [1, GROUP]], 0, **loose)
                pool.iota(c.item_id[:], [[P, ITEM_CHUNKS]], 0, channel_multiplier=1,
                          allow_small_or_imprecise_dtypes=True)
                chain.step(pool.iota(c.spare_i[:], [[P, ITEM_CHUNKS]], 0, channel_multiplier=1))
                pool.sem_inc(numbered, 1)
                for t in (c.ident, c.ident_b, c.before, c.zeros_b, c.zero_row):
                    chain.step(pool.memset(t[:], 0.0))
                for t in (c.ones, c.ones_b, c.not_before, c.ones_row):
                    chain.step(pool.memset(t[:], 1.0))
                for t in (c.ident, c.ident_b):
                    chain.step(pool.affine_select(out=t[:], in_=t[:], compare_op=ALU.not_equal, fill=1.0, base=0,
                                                  pattern=[[-1, P]], channel_multiplier=1))
                chain.step(pool.affine_select(out=c.before[:], in_=c.before[:], compare_op=ALU.is_ge, fill=1.0,
                                              base=0, pattern=[[-1, P]], channel_multiplier=1))
                chain.step(pool.affine_select(out=c.not_before[:], in_=c.not_before[:], compare_op=ALU.is_ge,
                                              fill=0.0, base=0, pattern=[[-1, P]], channel_multiplier=1))


def sort_edges(nc, c, arrays, graphs, sorted_records):
    src, dst, kind16, kind24, weight = arrays
    with Phase(nc, "sort") as ph:
        raw = ph.sb("raw", [EP, 4, EC], I32)
        wt = ph.sb("wt", [EP, EC], F32)
        rec = ph.sb("rec", [EP, 2, EC, 5], F32)
        bucket_i = ph.sb("bucket_i", [EP, 2, EC], I32)
        bucket = ph.sb("bucket", [EP, 2, EC + 1], F32)
        place = ph.sb("place", [EP, 2, EC + RING], F32)
        onehot = ph.sb("onehot", [P, 2, RING, TILES + 1], BF16)
        junk = ph.sb("junk", [P, TILES + 1], F32)
        slot_rec = ph.sb("slot_rec", [P, 2, RING, 5], F32)
        none = ph.sb("none", [P, 4], F32)
        hist = [ph.ps(f"hist{o}", [P, TILES + 1]) for o in range(2)]
        rank = [ph.ps(f"rank{o}", [P, TILES + 1]) for o in range(2)]
        s_in, s_dve, s_keys = ph.sem("in"), ph.sem("dve"), ph.sem("keys")
        s_hot, s_hist, s_start = ph.sem("hot"), ph.sem("hist"), ph.sem("start")
        s_hot2, s_rank, s_read, s_rest = ph.sem("hot2"), ph.sem("rank"), ph.sem("read"), ph.sem("rest")
        s_place, s_copied, s_none, s_passed = ph.sem("place"), ph.sem("copied"), ph.sem("none"), ph.sem("passed")
        s_out = [[ph.pool_dma_sem(f"out{o}{k}") for k in range(RING)] for o in range(2)]
        pads = ph.sem("pads")
        with nc.Block() as block:
            @block.sync
            def _(sp):
                for k, a in enumerate((src, dst, kind16, kind24)):
                    sp.dma_start(raw[:, k, :], a.rearrange("(p c) -> p c", p=EP)).then_inc(s_in, 16)
                sp.dma_start(wt[:], weight.rearrange("(p c) -> p c", p=EP)).then_inc(s_in, 16)
                sp.wait_ge(s_none, 1)
                for o in range(2):
                    sp.dma_start(sorted_records[o][N_EDGES:SORTED, :], none[:]).then_inc(pads, 16)
                sp.wait_ge(pads, 32)

            @block.vector
            def _(dve):
                chain = Chain(dve, s_dve)
                chain.step(dve.memset(none[:], 0.0))
                dve.memset(none[:, NODE:NODE + 1], -1.0).then_inc(s_none, 1)
                dve.memset(bucket[:, :, EC:], 0.0)
                dve.wait_ge(s_in, 80)
                for o in range(2):
                    chain.step(dve.tensor_single_scalar(bucket_i[:, o, :], raw[:, o, :], 7, op=ALU.logical_shift_right))
                    dve.tensor_copy(bucket[:, o, 0:EC], bucket_i[:, o, :]).then_inc(s_keys, 1)
                    dve.tensor_copy(rec[:, o, :, OTHER].bitcast(I32), raw[:, 1 - o, :])
                    dve.tensor_copy(rec[:, o, :, NODE], raw[:, o, :])
                dve.tensor_copy(rec[:, 1, :, KIND], raw[:, 2, :])
                dve.tensor_copy(rec[:, 0, :, KIND], raw[:, 3, :])
                for o in range(2):
                    chain.step(dve.tensor_copy(rec[:, o, :, WEIGHT], wt[:]))
                dve.wait_ge(s_keys, 2)
                with dve.Fori(0, EC // RING) as g:
                    for k in range(RING):
                        column = g * RING + k
                        for o in range(2):
                            a = dve.snap(column + o * (EC + 1))
                            dve.wait_ge(s_hist, column * 2 + (o + 1))
                            dve.tensor_scalar(onehot[0:EP, o, k, :], c.iota16[0:EP, :],
                                              bucket[:].rearrange("p o c -> p (o c)")[:, bass.ds(a, 1)], None,
                                              ALU.is_equal).then_inc(s_hot, 1)
                dve.wait_ge(s_hist, 2 * (EC + RING))
                for o in range(2):
                    b = graphs[o].buckets
                    chain.step(dve.tensor_copy(b["count"][:], hist[o][:]))
                    chain.step(dve.tensor_tensor_scan(b["start"][:], c.ones_row[:], b["count"][:], 0.0, ALU.mult, ALU.add))
                    chain.step(dve.tensor_tensor(b["start"][:], b["start"][:], b["count"][:], ALU.subtract))
                    chain.step(dve.tensor_scalar(b["int"][:], b["count"][:], float(P - 1), None, ALU.add))
                    chain.step(dve.tensor_single_scalar(b["int2"][:], b["int"][:], 7, op=ALU.logical_shift_right))
                    chain.step(dve.tensor_scalar(b["count"][:], b["int2"][:], 1.0, None, ALU.max))
                    chain.step(dve.tensor_tensor_scan(b["end"][:], c.ones_row[:], b["count"][:], 0.0, ALU.mult, ALU.add))
                    chain.step(dve.tensor_tensor(b["base"][:], b["end"][:], b["count"][:], ALU.subtract))
                dve.drain().then_inc(s_start, 1)

                def make(column, k):
                    for o in range(2):
                        a = dve.snap(column + o * (EC + 1)) if not isinstance(column, int) else column + o * (EC + 1)
                        dve.tensor_scalar(onehot[0:EP, o, k, :], c.iota16[0:EP, :],
                                          bucket[:].rearrange("p o c -> p (o c)")[:, bass.ds(a, 1)], None,
                                          ALU.is_equal).then_inc(s_hot2, 1)
                make(0, 0)
                with dve.Fori(0, EC // RING) as g:
                    for k in range(RING):
                        column = g * RING + k
                        make(column + 1, (k + 1) % RING)
                        for o in range(2):
                            a = dve.snap(column + o * (EC + 1))
                            p = dve.snap(column + o * (EC + RING))
                            dve.wait_ge(s_rank, column * 2 + (o + 1))
                            dve.scalar_tensor_tensor(junk[0:EP, :], c.iota[0:EP, :],
                                                     bucket[:].rearrange("p o c -> p (o c)")[:, bass.ds(a, 1)],
                                                     rank[o][0:EP, :], ALU.is_equal, ALU.mult,
                                                     accum_out=place[:].rearrange("p o c -> p (o c)")[:, bass.ds(p, 1)])\
                                .then_inc(s_read, 1)
                            dve.wait_ge(s_read, column * 2 + (o + 1))
                for o in range(2):
                    dve.tensor_copy(rec[:, o, :, 4].bitcast(I32), place[:, o, 0:EC]).then_inc(s_place, 1)

            @block.tensor
            def _(pe):
                pe.wait_ge(s_keys, 2)
                for _ in range(RING):
                    for o in range(2):
                        pe.matmul(hist[o][:], c.zeros_b[0:EP, :], c.zero_row[0:EP, :], start=True, stop=True)\
                            .then_inc(s_hist, 1)
                with pe.Fori(0, EC // RING) as g:
                    for k in range(RING):
                        for o in range(2):
                            pe.wait_ge(s_hot, (g * RING + k) * 2 + (o + 1))
                            pe.matmul(hist[o][:], c.ones_b[0:EP, :], onehot[0:EP, o, k, :], start=False, stop=True,
                                      skip_group_check=True).then_inc(s_hist, 1)
                pe.wait_ge(s_start, 1)
                for o in range(2):
                    pe.matmul(rank[o][0:EP, :], c.ones[0:1, 0:EP], graphs[o].buckets["start"][0:1, :],
                              start=True, stop=True)
                with pe.Fori(0, EC // RING) as g:
                    for k in range(RING):
                        column = g * RING + k
                        for o in range(2):
                            pe.wait_ge(s_hot2, column * 2 + (o + 1))
                            pe.matmul(rank[o][0:EP, :], c.before[0:EP, 0:EP], onehot[0:EP, o, k, :], start=False,
                                      stop=True, skip_group_check=True).then_inc(s_rank, 1)
                        for o in range(2):
                            pe.wait_ge(s_read, column * 2 + (o + 1))
                            pe.matmul(rank[o][0:EP, :], c.not_before[0:EP, 0:EP], onehot[0:EP, o, k, :], start=False,
                                      stop=True, skip_group_check=True)

            @block.gpsimd
            def _(pool):
                pool.wait_ge(s_place, 2)
                pool.sem_inc(s_passed, 1)

                def scatter(column, k, o, n):
                    a = column + o * EC if isinstance(column, int) else pool.snap(column + o * EC)
                    pool.tensor_copy(slot_rec[0:EP, o, k, :],
                                     rec[:].rearrange("p o c f -> p (o c) f")[:, bass.ds(a, 1), :].rearrange("p c f -> p (c f)"))\
                        .then_inc(s_copied, 1)
                    pool.wait_ge(s_copied, n)
                    pool.sem_inc(s_passed, 1)
                    pool.indirect_dma_start(sorted_records[o][0:N_EDGES, :],
                                            bass.IndirectOffsetOnAxis(ap=slot_rec[0:EP, o, k, 4:5].bitcast(I32), axis=0),
                                            slot_rec[0:EP, o, k, 0:4], None).then_inc(s_out[o][k], 16)

                for k in range(RING):
                    for o in range(2):
                        scatter(k, k, o, 2 * k + o + 1)
                with pool.Fori(1, EC // RING) as g:
                    for k in range(RING):
                        for o in range(2):
                            pool.wait_ge(s_out[o][k], g * 16)
                            pool.sem_inc(s_passed, 1)
                            scatter(g * RING + k, k, o, (g * RING + k) * 2 + (o + 1))
                for k in range(RING):
                    for o in range(2):
                        pool.wait_ge(s_out[o][k], EC // RING * 16)


def make_items(nc, c, graphs, sorted_records, item_rows):
    with Phase(nc, "items") as ph:
        ints = ph.sb("ints", [P, 2, 3, ITEM_CHUNKS], I32)
        vals = ph.sb("vals", [P, 2, 5, ITEM_CHUNKS], F32)
        tile_id = ph.sb("tile_id", [P, 2, ITEM_CHUNKS], F32)
        base = ph.sb("base", [P, ITEM_CHUNKS], F32)
        end = ph.sb("end", [P, ITEM_CHUNKS], F32)
        begin = ph.sb("begin", [P, ITEM_CHUNKS], F32)
        tmp = ph.sb("tmp", [P, ITEM_CHUNKS], F32)
        tmp2 = ph.sb("tmp2", [P, ITEM_CHUNKS], F32)
        junk = ph.sb("junk", [P, TILES + 1], F32)
        valid = ph.sb("valid", [P, ITEMS], F32)
        other = ph.sb("other", [P, ITEMS], F32)
        gi = ph.sb("gi", [P, 2], I32)
        s_v, s_tab, s_out, s_in, s_zero = ph.sem("v"), ph.sem("tab"), ph.sem("out"), ph.sem("in"), ph.sem("zero")
        s_passed = ph.sem("passed")
        s_win = [[ph.sem(f"win{o}{k}") for k in range(RING)] for o in range(2)]
        KEEP, FIRST_ROW = 3, 4
        with nc.Block() as block:
            @block.vector
            def _(dve):
                chain = Chain(dve, s_v)
                for o in range(2):
                    b = graphs[o].buckets
                    n = TILES
                    for q in range(ITEM_CHUNKS):
                        item = c.item_id[:, q:q + 1]
                        chain.step(dve.tensor_scalar(junk[:, 0:n], b["end"][:, 0:n], item, 0.0, ALU.is_le, ALU.add,
                                                     accum_out=tile_id[:, o, q:q + 1]))
                        for what, out in (("base", base), ("end", end), ("start", begin)):
                            chain.step(dve.scalar_tensor_tensor(junk[:, 0:n], c.iota[:, 0:n], tile_id[:, o, q:q + 1],
                                                                b[what][:, 0:n], ALU.is_equal, ALU.mult,
                                                                accum_out=out[:, q:q + 1]))
                    v = vals[:, o]
                    chain.step(dve.tensor_tensor(tmp[:], c.item_id[:], base[:], ALU.subtract))
                    chain.step(dve.scalar_tensor_tensor(tmp2[:], tmp[:], float(P), begin[:], ALU.mult, ALU.add))
                    chain.step(dve.tensor_scalar(v[:, START, :], tmp2[:], float(N_EDGES), None, ALU.min))
                    chain.step(dve.tensor_scalar(v[:, KEEP, :], tmp[:], 0.0, None, ALU.not_equal))
                    chain.step(dve.tensor_scalar(v[:, LOAD, :], tile_id[:, o, :], float(TILES - 1), float(P), ALU.min, ALU.mult))
                    chain.step(dve.tensor_scalar(v[:, FIRST_ROW, :], tile_id[:, o, :], float(P), None, ALU.mult))
                    chain.step(dve.tensor_tensor(tmp[:], end[:], c.item_id[:], ALU.subtract))
                    chain.step(dve.tensor_scalar(tmp[:], tmp[:], 1.0, None, ALU.is_equal))
                    chain.step(dve.tensor_tensor(tmp2[:], v[:, LOAD, :], c.spare[:], ALU.subtract))
                    chain.step(dve.tensor_tensor(tmp2[:], tmp2[:], tmp[:], ALU.mult))
                    chain.step(dve.tensor_tensor(v[:, STORE, :], tmp2[:], c.spare[:], ALU.add))
                    chain.step(dve.tensor_copy(ints[:, o, :, :], v[:, 0:3, :]))
                    chain.step(dve.tensor_scalar(gi[:, o:o + 1], b["end"][:, n - 1:n], float(RING - 1), None, ALU.add))
                    chain.step(dve.tensor_single_scalar(graphs[o].groups[0:1, 0:1], gi[0:1, o:o + 1], RING.bit_length() - 1,
                                                        op=ALU.logical_shift_right))
                    dve.memset(graphs[o].meta[:], 0.0).then_inc(s_zero, 1)
                dve.drain().then_inc(s_tab, 1)
                for o in range(2):
                    g = graphs[o]
                    dve.wait_ge(s_in, 96 + 16 * (o + 1))
                    node = g.meta[:, :, NODE]
                    chain.step(dve.tensor_tensor(node, node, g.first_row[:], ALU.subtract))
                    chain.step(dve.tensor_scalar(valid[:], node, 0.0, None, ALU.is_ge))
                    chain.step(dve.scalar_tensor_tensor(valid[:], node, float(P), valid[:], ALU.is_lt, ALU.mult))
                    chain.step(dve.tensor_copy(other[:], g.meta[:, :, OTHER].bitcast(I32)))
                    chain.step(dve.tensor_scalar(valid[:], valid[:], -FAR, FAR, ALU.mult, ALU.add))
                    chain.step(dve.tensor_tensor(g.meta[:, :, OTHER].bitcast(I32), other[:], valid[:], ALU.add))

            @block.sync
            def _(sp):
                sp.wait_ge(s_tab, 1)
                with nc.allow_non_contiguous_dma(reason="small tables turned once"):
                    for o in range(2):
                        rows_i, rows_f = item_rows[o]
                        for f in range(3):
                            sp.dma_start(rows_i[f].rearrange("(q p) -> p q", p=P), ints[:, o, f, :]).then_inc(s_out, 16)
                        for f in range(2):
                            sp.dma_start(rows_f[f].rearrange("(q p) -> p q", p=P), vals[:, o, 3 + f, :]).then_inc(s_out, 16)
                sp.wait_ge(s_out, 160)
                for o in range(2):
                    g = graphs[o]
                    rows_i, rows_f = item_rows[o]
                    sp.dma_start(g.table[:], rows_i.rearrange("(a f) i -> a f i", a=1)).then_inc(s_in, 16)
                    sp.dma_start(g.keep[:], rows_f[0].partition_broadcast(P)).then_inc(s_in, 16)
                    sp.dma_start(graphs[o].first_row[:], rows_f[1].partition_broadcast(P)).then_inc(s_in, 16)
                sp.wait_ge(s_in, 96)
                for o in range(2):
                    g = graphs[o]
                    sp.wait_ge(s_zero, 2)
                    groups = load_groups(sp, g)
                    with sp.Fori(0, groups + 2) as it:
                        for k in range(RING):
                            item = sp.snap(it * RING + k, min_val=0, max_val=ITEMS - 1)
                            first = sp.value_load(g.table[0:1, START, bass.ds(item, 1)], min_val=0, max_val=N_EDGES)
                            sp.dma_start(g.meta[:, bass.ds(item, 1), :], sorted_records[o][bass.ds(first, P), :])\
                                .then_inc(s_win[o][k], 16)
                    for k in range(RING):
                        sp.wait_ge(s_win[o][k], (groups + 2) * 16)
                        sp.sem_inc(s_passed, 1)
                    sp.sem_inc(s_in, 16)


def pass_wait(eng, s, sem, value):
    eng.wait_ge(sem, value)
    eng.sem_inc(s["passed"], 1)


def one_hot(dve, c, graph, out, item, weight, sem):
    dve.tensor_scalar(out, c.iota[:, 0:P], graph.meta[:, bass.ds(item, 1), NODE],
                      weight, ALU.is_equal, ALU.mult).then_inc(sem, 1)


def mean_layer(nc, c, graph, w, gamma, beta, eps, x_in, x_out):
    with Phase(nc, "l0") as ph:
        x = ph.sb("x", [P, RING, D], F32)
        gathered = ph.sb("gathered", [P, RING, D], F32)
        index = ph.sb("index", [P, RING, 1], I32)
        hot = ph.sb("hot", [P, 2, P], F32)
        agg_t = ph.sb("agg_t", [P, 2, D], F32)
        x_t = ph.sb("x_t", [P, 2, D], F32)
        stats = ph.sb("stats", [P, 2, 2, 6], F32)
        mv = ph.sb("mv", [P, 2, 2, 2], F32)
        sd = ph.sb("sd", [P, 2, 2], F32)
        rs = ph.sb("rs", [P, 2, 2], F32)
        scaled = ph.sb("scaled", [P, D], F32)
        shifted = ph.sb("shifted", [P, D], F32)
        summed = ph.sb("summed", [P, 2, D], F32)
        result = ph.sb("result", [P, RING, D], F32)
        ps_a = [ph.ps(f"a{k}", [P, 2 * D])[:, 0:D] for k in range(2)]
        ps_x = [ph.ps(f"x{k}", [P, 2 * D])[:, 0:D] for k in range(2)]
        ps_b = [ph.ps(f"b{k}", [P, 2 * D])[:, 0:D] for k in range(2)]
        s = ring_sems(ph, "summed")
        for k in ("g_done", "made", "a_done", "acc", "xt", "b_done", "st1", "ag1", "sd1", "rs1", "scaled", "shifted",
                  "summed", "st2", "ag2", "sd2", "rs2"):
            s[k] = ph.sem(k)
        with nc.Block() as block:
            @block.sync
            def _(sp):
                move_tiles(sp, graph, s, x, x_in, result, x_out)

            @block.gpsimd
            def _(pool):
                gather_rows(pool, graph, s, index, gathered, x_in)

            @block.vector
            def _(dve):
                def make(j, k, lap):
                    one_hot(dve, c, graph, hot[:, k % 2, :], j, graph.meta[:, bass.ds(j, 1), WEIGHT], s["made"])

                def accumulate(j, k, lap):
                    dve.wait_ge(s["a_done"], j + 1)
                    dve.scalar_tensor_tensor(agg_t[:, k % 2, :], agg_t[:, (k + 1) % 2, :],
                                             graph.keep[:, bass.ds(j, 1)], ps_a[k % 2][:, 0:D],
                                             ALU.mult, ALU.add).then_inc(s["acc"], 1)

                def inner(j, k, lap):
                    p = k % 2
                    dve.wait_ge(s["b_done"], j + 1)
                    dve.bn_stats(stats[:, p, 0, :], ps_b[p][:]).then_inc(s["st1"], 1)
                    pass_wait(dve, s, s["st1"], j + 1)
                    dve.bn_aggr(mv[:, p, 0, :], stats[:, p, 0, :]).then_inc(s["ag1"], 1)
                    dve.wait_ge(s["ag1"], j + 1)
                    dve.scalar_tensor_tensor(scaled[:], ps_b[p][:], mv[:, p, 0, 0:1], gamma[:],
                                             ALU.subtract, ALU.mult).then_inc(s["scaled"], 1)
                    dve.wait_ge(s["sd1"], j + 1)
                    dve.reciprocal(rs[:, p, 0:1], sd[:, p, 0:1]).then_inc(s["rs1"], 1)
                    dve.wait_ge(s["scaled"], j + 1)
                    dve.wait_ge(s["rs1"], j + 1)
                    dve.scalar_tensor_tensor(shifted[:], scaled[:], rs[:, p, 0:1], beta[:],
                                             ALU.mult, ALU.add).then_inc(s["shifted"], 1)
                    dve.wait_ge(s["in_x"][k], (lap + 1) * 16)
                    dve.wait_ge(s["shifted"], j + 1)
                    dve.scalar_tensor_tensor(summed[:, p, :], shifted[:], 0.0, x[:, k, :],
                                             ALU.max, ALU.add).then_inc(s["summed"], 1)
                    dve.wait_ge(s["summed"], j + 1)
                    dve.bn_stats(stats[:, p, 1, :], summed[:, p, :]).then_inc(s["st2"], 1)
                    pass_wait(dve, s, s["st2"], j + 1)
                    dve.bn_aggr(mv[:, p, 1, :], stats[:, p, 1, :]).then_inc(s["ag2"], 1)

                def outer(j, k, lap):
                    p = k % 2
                    dve.wait_ge(s["sd2"], j + 1)
                    dve.reciprocal(rs[:, p, 1:2], sd[:, p, 1:2]).then_inc(s["rs2"], 1)
                    dve.wait_ge(s["stored"][k], (lap + 1) * 16)
                    dve.wait_ge(s["rs2"], j + 1)
                    dve.tensor_scalar(result[:, k, :], summed[:, p, :], mv[:, p, 1, 0:1], rs[:, p, 1:2],
                                      ALU.subtract, ALU.mult).then_inc(s["out_ready"], 1)

                dve.memset(agg_t[:], 0.0).then_inc(s["zeroed"], 1)
                dve.memset(result[:], 0.0).then_inc(s["zeroed"], 1)
                dve.wait_ge(s["zeroed"], 2)
                groups = load_groups(dve, graph)
                make(*at(0, 0))
                make(*at(0, 1))
                accumulate(*at(0, 0))
                make(*at(0, 2))
                dve.wait_ge(s["acc"], 1)
                accumulate(*at(0, 1))
                make(*at(0, 3))
                inner(*at(0, 0))
                with dve.Fori(0, groups) as g:
                    for k in range(RING):
                        dve.wait_ge(s["acc"], g * RING + k + 2)
                        accumulate(*at(g, k + 2))
                        make(*at(g, k + 4))
                        inner(*at(g, k + 1))
                        outer(*at(g, k))

            @block.scalar
            def _(act):
                def evacuate(j, k, lap):
                    act.wait_ge(s["a_done"], j + 1)
                    act.copy(x_t[:, k % 2, :], ps_x[k % 2][:, 0:D]).then_inc(s["xt"], 1)

                def deviation(j, k, which, ready, done):
                    act.wait_ge(ready, j + 1)
                    act.activation(sd[:, k % 2, which:which + 1], mv[:, k % 2, which, 1:2], ACT.Sqrt, bias=eps[:])\
                        .then_inc(done, 1)

                groups = load_groups(act, graph)
                evacuate(*at(0, 0))
                evacuate(*at(0, 1))
                deviation(0, 0, 0, s["ag1"], s["sd1"])
                with act.Fori(0, groups) as g:
                    for k in range(RING):
                        j = g * RING + k
                        deviation(j, k, 1, s["ag2"], s["sd2"])
                        evacuate(*at(g, k + 2))
                        deviation(j + 1, k + 1, 0, s["ag1"], s["sd1"])

            @block.tensor
            def _(pe):
                def gather_sum(j, k, lap):
                    pe.wait_ge(s["in_g"][k], (lap + 1) * 16)
                    pe.wait_ge(s["made"], j + 1)
                    for f in range(2):
                        last = pe.matmul(ps_a[k % 2][:, f * P:(f + 1) * P], gathered[:, k, f * P:(f + 1) * P],
                                         hot[:, k % 2, :], start=True, stop=True)
                    last.then_inc(s["g_done"], 1)
                    pe.wait_ge(s["in_x"][k], (lap + 1) * 16)
                    for f in range(2):
                        last = pe.transpose(ps_x[k % 2][:, f * P:(f + 1) * P], x[:, k, f * P:(f + 1) * P],
                                            c.ident[:])
                    last.then_inc(s["a_done"], 1)

                def product(j, k, lap):
                    pe.wait_ge(s["acc"], j + 1)
                    pe.wait_ge(s["xt"], j + 1)
                    for i in range(4):
                        left = agg_t if i < 2 else x_t
                        last = pe.matmul(ps_b[k % 2][:], left[:, k % 2, i % 2 * P:(i % 2 + 1) * P], w[:, i, :],
                                         start=(i == 0), stop=(i == 3))
                    last.then_inc(s["b_done"], 1)

                groups = load_groups(pe, graph)
                gather_sum(*at(0, 0))
                gather_sum(*at(0, 1))
                product(*at(0, 0))
                with pe.Fori(0, groups) as g:
                    for k in range(RING):
                        gather_sum(*at(g, k + 2))
                        product(*at(g, k + 1))


class Norm:

    def __init__(self, ph, s, name):
        self.stats = ph.sb(f"{name}_stats", [P, 2, 6], F32)
        self.mv = ph.sb(f"{name}_mv", [P, 2, 2], F32)
        self.sd = ph.sb(f"{name}_sd", [P, 2], F32)
        self.rs = ph.sb(f"{name}_rs", [P, 2], F32)
        self.st, self.ag, self.dev, self.inv = (ph.sem(f"{name}_{k}") for k in ("st", "ag", "dev", "inv"))

    def moments(self, dve, s, values, j, p):
        dve.bn_stats(self.stats[:, p, :], values).then_inc(self.st, 1)
        pass_wait(dve, s, self.st, j + 1)
        dve.bn_aggr(self.mv[:, p, :], self.stats[:, p, :]).then_inc(self.ag, 1)

    def deviation(self, act, eps, j, p):
        act.wait_ge(self.ag, j + 1)
        act.activation(self.sd[:, p:p + 1], self.mv[:, p, 1:2], ACT.Sqrt, bias=eps[:]).then_inc(self.dev, 1)

    def inverse(self, dve, j, p):
        dve.wait_ge(self.dev, j + 1)
        dve.reciprocal(self.rs[:, p:p + 1], self.sd[:, p:p + 1]).then_inc(self.inv, 1)

    def apply(self, dve, out, values, p):
        return dve.tensor_scalar(out, values, self.mv[:, p, 0:1], self.rs[:, p:p + 1], ALU.subtract, ALU.mult)


def count_edges(nc, c, graph, counts):
    with Phase(nc, "count") as ph:
        hot = ph.sb("hot", [P, 2, P], BF16)
        kind = ph.sb("kind", [P, 2, R1], BF16)
        total = ph.sb("total", [P, RING, R1], F32)
        back = ph.sb("back", [P, RING, R1], F32)
        hot2 = ph.sb("hot2", [P, 2, P], F32)
        hot_t = ph.sb("hot_t", [P, 2, P], F32)
        junk = ph.sb("junk", [P, 2, R1], F32)
        ps_c = [ph.ps(f"c{k}", [P, 2 * D])[:, 0:R1] for k in range(2)]
        ps_t = [ph.ps(f"t{k}", [P, 2 * D])[:, 0:P] for k in range(2)]
        ps_e = [ph.ps(f"e{k}", [P, 2 * D])[:, 0:R1] for k in range(2)]
        s = {k: ph.sem(k) for k in ("made", "counted", "summed", "zeroed", "passed", "made2", "turned", "turned_sb",
                                    "looked", "read", "written", "chain")}
        out = [ph.sem(f"out{k}") for k in range(RING)]
        back_in = [ph.sem(f"back{k}") for k in range(RING)]
        with nc.Block() as block:
            @block.sync
            def _(sp):
                sp.wait_ge(s["zeroed"], 2)
                for k in range(RING):
                    sp.dma_start(counts[ROWS + k * P:ROWS + (k + 1) * P, :], total[:, k, :]).then_inc(out[k], 16)
                groups = load_groups(sp, graph)
                with sp.Fori(0, groups) as g:
                    for k in range(RING):
                        row = row_of(sp, graph, STORE, g * RING + k)
                        sp.wait_ge(s["summed"], g * RING + k + 2)
                        sp.dma_start(counts[bass.ds(row, P), :], total[:, k, :]).then_inc(out[k], 16)
                for k in range(RING):
                    sp.wait_ge(out[k], (groups + 1) * 16)
                    sp.sem_inc(s["passed"], 1)
                sp.sem_inc(s["written"], 1)
                for k in range(RING):
                    row = row_of(sp, graph, LOAD, k)
                    sp.dma_start(back[:, k, :], counts[bass.ds(row, P), :]).then_inc(back_in[k], 16)
                with sp.Fori(0, groups) as g:
                    for k in range(RING):
                        row = row_of(sp, graph, LOAD, (g + 1) * RING + k)
                        sp.wait_ge(s["looked"], g * RING + k + 1)
                        sp.dma_start(back[:, k, :], counts[bass.ds(row, P), :]).then_inc(back_in[k], 16)
                for k in range(RING):
                    sp.wait_ge(back_in[k], (groups + 1) * 16)
                    sp.sem_inc(s["passed"], 1)

            @block.vector
            def _(dve):
                def make(j, k):
                    dve.tensor_scalar(hot[:, k % 2, :], c.iota[:, 0:P], graph.meta[:, bass.ds(j, 1), NODE], None,
                                      ALU.is_equal)
                    dve.tensor_scalar(kind[:, k % 2, :], c.iota[:, 0:R1], graph.meta[:, bass.ds(j, 1), KIND], None,
                                      ALU.is_equal).then_inc(s["made"], 1)

                dve.memset(total[:], 0.0).then_inc(s["zeroed"], 1)
                dve.memset(graph.share[:], 1.0).then_inc(s["zeroed"], 1)
                dve.wait_ge(s["zeroed"], 2)
                make(0, 0)
                make(1, 1)
                dve.sem_inc(s["summed"], 1)
                groups = load_groups(dve, graph)
                with dve.Fori(0, groups) as g:
                    for k in range(RING):
                        j = g * RING + k
                        dve.wait_ge(s["counted"], j + 1)
                        dve.wait_ge(out[k], (g + 1) * 16)
                        dve.wait_ge(s["summed"], j + 1)
                        dve.scalar_tensor_tensor(total[:, k, :], total[:, (k - 1) % RING, :],
                                                 graph.keep[:, bass.ds(j, 1)], ps_c[k % 2], ALU.mult, ALU.add)\
                            .then_inc(s["summed"], 1)
                        make(j + 2, k)

                def make2(j, k):
                    dve.tensor_scalar(hot2[:, k % 2, :], c.iota[:, 0:P], graph.meta[:, bass.ds(j, 1), NODE], None,
                                      ALU.is_equal).then_inc(s["made2"], 1)

                make2(0, 0)
                make2(1, 1)
                with dve.Fori(0, groups) as g:
                    for k in range(RING):
                        j = g * RING + k
                        dve.wait_ge(s["looked"], j + 1)
                        dve.scalar_tensor_tensor(junk[:, k % 2, :], c.iota[:, 0:R1], graph.meta[:, bass.ds(j, 1), KIND],
                                                 ps_e[k % 2], ALU.is_equal, ALU.mult,
                                                 accum_out=graph.share[:, bass.ds(j, 1)]).then_inc(s["read"], 1)
                        dve.wait_ge(s["read"], j + 1)
                        make2(j + 2, k)
                dve.wait_ge(s["read"], 1)
                dve.tensor_scalar(graph.share[:], graph.share[:], 1.0, None, ALU.max).then_inc(s["chain"], 1)
                dve.wait_ge(s["chain"], 1)
                dve.reciprocal(graph.share[:], graph.share[:])

            @block.scalar
            def _(act):
                groups = load_groups(act, graph)

                def copy(j, k):
                    act.wait_ge(s["turned"], j + 1)
                    act.copy(hot_t[:, k % 2, :], ps_t[k % 2]).then_inc(s["turned_sb"], 1)

                copy(0, 0)
                with act.Fori(0, groups) as g:
                    for k in range(RING):
                        copy(g * RING + k + 1, k + 1)

            @block.tensor
            def _(pe):
                groups = load_groups(pe, graph)
                with pe.Fori(0, groups) as g:
                    for k in range(RING):
                        j = g * RING + k
                        pe.wait_ge(s["made"], j + 1)
                        pe.matmul(ps_c[k % 2], hot[:, k % 2, :], kind[:, k % 2, :], start=True, stop=True)\
                            .then_inc(s["counted"], 1)

                def turn(j, k):
                    pe.wait_ge(s["made2"], j + 1)
                    pe.transpose(ps_t[k % 2], hot2[:, k % 2, :], c.ident[:]).then_inc(s["turned"], 1)

                turn(0, 0)
                with pe.Fori(0, groups) as g:
                    for k in range(RING):
                        j = g * RING + k
                        turn(j + 1, k + 1)
                        pe.wait_ge(back_in[k], (g + 1) * 16)
                        pe.wait_ge(s["turned_sb"], j + 1)
                        pe.matmul(ps_e[k % 2], hot_t[:, k % 2, :], back[:, k, :], start=True, stop=True)\
                            .then_inc(s["looked"], 1)


def relation_layer(nc, c, graph, name, root, table, bias, eps, x_in, x_out, residual=None):
    with Phase(nc, name) as ph:
        x = ph.sb("x", [P, RING, D], F32)
        res = None if residual is None else ph.sb("res", [P, RING, D], F32)
        gathered = ph.sb("gathered", [P, RING, D], F32)
        index = ph.sb("index", [P, RING, 1], I32)
        hot = ph.sb("hot", [P, 2, P], F32)
        kind = ph.sb("kind", [P, RING, K3], BF16)
        first = ph.sb("first", [P, RING], F32)
        kind_t = ph.sb("kind_t", [K3, 2, P], BF16)
        x_t = ph.sb("x_t", [P, 2, D], F32)
        part = ph.sb("part", [P, 4, D], F32)
        message = ph.sb("message", [P, 2, 2, D], F32)
        total = ph.sb("total", [P, 2, D], F32)
        biased = ph.sb("biased", [P, 4, D], F32)
        summed = ph.sb("summed", [P, 2, D], F32)
        result = ph.sb("result", [P, RING, D], F32)
        ps_x = [ph.ps(f"x{k}", [P, 2 * D])[:, 0:D] for k in range(2)]
        ps_k = ph.ps("k", [P, 4 * D], BF16)
        ps_w = ph.ps("w", [P, 4 * D])
        ps_b = [ph.ps(f"b{k}", [P, 2 * D])[:, 0:D] for k in range(2)]
        s = ring_sems(ph, "a_done", "multiplied", residual is not None)
        for k in ("made_kind", "made_hot", "a_done", "xt", "kt", "w_done", "multiplied", "message", "b_done", "total",
                  "biased"):
            s[k] = ph.sem(k)
        norm = Norm(ph, s, "norm") if residual is not None else None
        with nc.Block() as block:
            @block.sync
            def _(sp):
                move_tiles(sp, graph, s, x, x_in, result, x_out, None if residual is None else (res, residual))

            @block.gpsimd
            def _(pool):
                gather_rows(pool, graph, s, index, gathered, x_in)

            @block.vector
            def _(dve):
                def make_kind(j, k, lap):
                    dve.tensor_scalar(first[:, k:k + 1], graph.keep[:, bass.ds(j, 1)], -1.0, 1.0, ALU.mult, ALU.add)
                    dve.tensor_scalar(kind[:, k, :], c.iota_kind[:], graph.meta[:, bass.ds(j, 1), KIND], None,
                                      ALU.is_equal).then_inc(s["made_kind"], 1)

                def make_hot(j, k, lap):
                    one_hot(dve, c, graph, hot[:, k % 2, :], j, graph.share[:, bass.ds(j, 1)], s["made_hot"])

                def multiply(j, k, lap):
                    dve.wait_ge(s["in_g"][k], (lap + 1) * 16)
                    dve.wait_ge(s["w_done"], j + 1)
                    rows = gathered[:, k, :].rearrange("p (b i) -> p i b", i=4).unsqueeze(3).broadcast_to([P, 4, 64, 4])
                    dve.tensor_tensor(part[:].rearrange("p i (b o) -> p i b o", o=4), rows,
                                      ps_w[:].rearrange("p (i b o) -> p i b o", i=4, o=4), ALU.mult)\
                        .then_inc(s["multiplied"], 1)
                    dve.wait_ge(s["multiplied"], j + 1)
                    dve.tensor_tensor(message[:, k % 2, :, :], part[:, 0:2, :], part[:, 2:4, :], ALU.add)\
                        .then_inc(s["message"], 1)

                def finish(j, k, lap):
                    p = k % 2
                    dve.wait_ge(s["b_done"], j + 1)
                    dve.scalar_tensor_tensor(total[:, p, :], total[:, 1 - p, :], graph.keep[:, bass.ds(j, 1)],
                                             ps_b[p], ALU.mult, ALU.add).then_inc(s["total"], 1)
                    make_hot(*at_plus(j, k, lap, 2))
                    dve.wait_ge(s["total"], j + 1)
                    dve.tensor_tensor(biased[:, k % 4, :], total[:, p, :], bias[:], ALU.add).then_inc(s["biased"], 1)
                    if residual is not None:
                        dve.wait_ge(s["in_res"][k], (lap + 1) * 16)
                        dve.wait_ge(s["biased"], j + 1)
                        dve.tensor_tensor(summed[:, p, :], biased[:, k % 4, :], res[:, k, :], ALU.add)\
                            .then_inc(s["res_done"], 1)
                        dve.wait_ge(s["res_done"], j + 1)
                        norm.moments(dve, s, summed[:, p, :], j, p)

                def normalise(j, k, lap):
                    norm.inverse(dve, j, k % 2)
                    dve.wait_ge(s["stored"][k], (lap + 1) * 16)
                    dve.wait_ge(norm.inv, j + 1)
                    norm.apply(dve, result[:, k, :], summed[:, k % 2, :], k % 2).then_inc(s["out_ready"], 1)

                dve.memset(total[:], 0.0).then_inc(s["zeroed"], 1)
                dve.memset(result[:], 0.0).then_inc(s["zeroed"], 1)
                dve.wait_ge(s["zeroed"], 2)
                groups = load_groups(dve, graph)
                for k in range(RING):
                    make_kind(*at(0, k))
                make_hot(*at(0, 0))
                make_hot(*at(0, 1))
                multiply(*at(0, 0))
                multiply(*at(0, 1))
                finish(*at(0, 0))
                with dve.Fori(0, groups) as g:
                    for k in range(RING):
                        multiply(*at(g, k + 2))
                        finish(*at(g, k + 1))
                        if residual is not None:
                            normalise(*at(g, k))
                        make_kind(*at(g + 1, k))

            @block.scalar
            def _(act):
                def evacuate(j, k, lap):
                    act.wait_ge(s["a_done"], j + 1)
                    act.copy(kind_t[:, k % 2, :], ps_k[0:K3, 0:P]).then_inc(s["kt"], 1)
                    act.activation(x_t[:, k % 2, :], ps_x[k % 2], ACT.Copy, scale=first[:, k:k + 1])\
                        .then_inc(s["xt"], 1)

                groups = load_groups(act, graph)
                evacuate(*at(0, 0))
                evacuate(*at(0, 1))
                evacuate(*at(0, 2))
                if residual is not None:
                    norm.deviation(act, eps, 0, 0)
                with act.Fori(0, groups) as g:
                    for k in range(RING):
                        j = g * RING + k
                        evacuate(*at(g, k + 3))
                        if residual is not None:
                            norm.deviation(act, eps, j + 1, (k + 1) % 2)
                        else:
                            act.wait_ge(s["stored"][k], (g + 1) * 16)
                            act.wait_ge(s["biased"], j + 1)
                            act.activation(result[:, k, :], biased[:, k % 4, :], ACT.Relu).then_inc(s["out_ready"], 1)

            @block.tensor
            def _(pe):
                def turn(j, k, lap):
                    pe.wait_ge(s["made_kind"], j + 1)
                    pe.transpose(ps_k[0:K3, 0:P], kind[:, k, :], c.ident_b[:])
                    pe.wait_ge(s["in_x"][k], (lap + 1) * 16)
                    for f in range(2):
                        last = pe.transpose(ps_x[k % 2][:, f * P:(f + 1) * P], x[:, k, f * P:(f + 1) * P], c.ident[:])
                    last.then_inc(s["a_done"], 1)

                def blocks(j, k, lap):
                    pe.wait_ge(s["kt"], j + 1)
                    if not isinstance(j, int) or j > 0:
                        pe.wait_ge(s["multiplied"], j)
                    for h in range(2):
                        last = pe.matmul(ps_w[:, h * 2 * D:(h + 1) * 2 * D], kind_t[:, k % 2, :],
                                         table[:, h * 2 * D:(h + 1) * 2 * D], start=True, stop=True)
                    last.then_inc(s["w_done"], 1)

                def products(j, k, lap):
                    pe.wait_ge(s["made_hot"], j + 1)
                    pe.wait_ge(s["xt"], j + 1)
                    for f in range(2):
                        pe.matmul(ps_b[k % 2], x_t[:, k % 2, f * P:(f + 1) * P], root[:, f, :], start=(f == 0), stop=False)
                    pe.wait_ge(s["message"], j + 1)
                    for i in range(2):
                        last = pe.matmul(ps_b[k % 2], hot[:, k % 2, :], message[:, k % 2, i, :], start=False, stop=(i == 1))
                    last.then_inc(s["b_done"], 1)

                groups = load_groups(pe, graph)
                turn(*at(0, 0))
                blocks(*at(0, 0))
                turn(*at(0, 1))
                products(*at(0, 0))
                blocks(*at(0, 1))
                turn(*at(0, 2))
                with pe.Fori(0, groups) as g:
                    for k in range(RING):
                        products(*at(g, k + 1))
                        blocks(*at(g, k + 2))
                        turn(*at(g, k + 3))


def at_plus(j, k, lap, more):
    return j + more, (k + more) % RING, lap + (k + more) // RING


def interaction_layer(nc, c, graph, w1, w2, bias, eps, x_in, x_out):
    with Phase(nc, "l3") as ph:
        x = ph.sb("x", [P, RING, D], F32)
        gathered = ph.sb("gathered", [P, RING, D], F32)
        index = ph.sb("index", [P, RING, 1], I32)
        hot = ph.sb("hot", [P, 2, P], F32)
        agg_t = ph.sb("agg_t", [P, 2, D], F32)
        mix_t = ph.sb("mix_t", [P, 2, D], F32)
        x_t = ph.sb("x_t", [P, 2, D], F32)
        biased = ph.sb("biased", [P, 2, D], F32)
        leaky = ph.sb("leaky", [P, 2, D], F32)
        squares = ph.sb("squares", [P, D], F32)
        length = ph.sb("length", [P, 3, 2], F32)
        summed = ph.sb("summed", [P, 2, D], F32)
        result = ph.sb("result", [P, RING, D], F32)
        ps_a = [ph.ps(f"a{k}", [P, 2 * D])[:, 0:D] for k in range(2)]
        ps_x = [ph.ps(f"x{k}", [P, 2 * D])[:, 0:D] for k in range(2)]
        ps_b = [ph.ps(f"b{k}", [P, 2 * D])[:, 0:D] for k in range(2)]
        s = ring_sems(ph, "summed")
        for k in ("made", "a_done", "g_done", "acc", "xt", "mix", "b_done", "biased", "leaky", "squared", "rooted",
                  "guarded", "inverted", "summed"):
            s[k] = ph.sem(k)
        norm = Norm(ph, s, "norm")
        with nc.Block() as block:
            @block.sync
            def _(sp):
                move_tiles(sp, graph, s, x, x_in, result, x_out)

            @block.gpsimd
            def _(pool):
                gather_rows(pool, graph, s, index, gathered, x_in)

            @block.vector
            def _(dve):
                def make(j, k, lap):
                    one_hot(dve, c, graph, hot[:, k % 2, :], j, graph.meta[:, bass.ds(j, 1), WEIGHT], s["made"])

                def accumulate(j, k, lap):
                    p = k % 2
                    dve.wait_ge(s["a_done"], j + 1)
                    dve.scalar_tensor_tensor(agg_t[:, p, :], agg_t[:, 1 - p, :], graph.keep[:, bass.ds(j, 1)], ps_a[p],
                                             ALU.mult, ALU.add).then_inc(s["acc"], 1)
                    make(*at_plus(j, k, lap, 2))
                    dve.wait_ge(s["xt"], j + 1)
                    dve.wait_ge(s["acc"], j + 1)
                    dve.scalar_tensor_tensor(mix_t[:, p, :], x_t[:, p, :], 1.0, agg_t[:, p, :], ALU.add, ALU.mult)\
                        .then_inc(s["mix"], 1)

                def activate(j, k, lap):
                    p = k % 2
                    dve.wait_ge(s["b_done"], j + 1)
                    dve.tensor_tensor(biased[:, p, :], ps_b[p], bias[:], ALU.add).then_inc(s["biased"], 1)
                    dve.wait_ge(s["biased"], j + 1)
                    dve.scalar_tensor_tensor(leaky[:, p, :], biased[:, p, :], 0.2, biased[:, p, :], ALU.mult, ALU.max)\
                        .then_inc(s["leaky"], 1)

                def add(j, k, lap):
                    p = k % 2
                    dve.wait_ge(s["rooted"], j + 1)
                    dve.tensor_scalar(length[:, 1, p:p + 1], length[:, 1, p:p + 1], 1e-12, None, ALU.max)\
                        .then_inc(s["guarded"], 1)
                    dve.wait_ge(s["guarded"], j + 1)
                    dve.reciprocal(length[:, 2, p:p + 1], length[:, 1, p:p + 1]).then_inc(s["inverted"], 1)
                    dve.wait_ge(s["inverted"], j + 1)
                    dve.scalar_tensor_tensor(summed[:, p, :], leaky[:, p, :], length[:, 2, p:p + 1], x[:, k, :],
                                             ALU.mult, ALU.add).then_inc(s["summed"], 1)
                    dve.wait_ge(s["summed"], j + 1)
                    norm.moments(dve, s, summed[:, p, :], j, p)

                def normalise(j, k, lap):
                    norm.inverse(dve, j, k % 2)
                    dve.wait_ge(s["stored"][k], (lap + 1) * 16)
                    dve.wait_ge(norm.inv, j + 1)
                    norm.apply(dve, result[:, k, :], summed[:, k % 2, :], k % 2).then_inc(s["out_ready"], 1)

                dve.memset(agg_t[:], 0.0).then_inc(s["zeroed"], 1)
                dve.memset(result[:], 0.0).then_inc(s["zeroed"], 1)
                dve.wait_ge(s["zeroed"], 2)
                groups = load_groups(dve, graph)
                make(*at(0, 0))
                make(*at(0, 1))
                accumulate(*at(0, 0))
                accumulate(*at(0, 1))
                activate(*at(0, 0))
                accumulate(*at(0, 2))
                activate(*at(0, 1))
                add(*at(0, 0))
                with dve.Fori(0, groups) as g:
                    for k in range(RING):
                        accumulate(*at(g, k + 3))
                        activate(*at(g, k + 2))
                        add(*at(g, k + 1))
                        normalise(*at(g, k))

            @block.scalar
            def _(act):
                def evacuate(j, k, lap):
                    act.wait_ge(s["a_done"], j + 1)
                    act.copy(x_t[:, k % 2, :], ps_x[k % 2]).then_inc(s["xt"], 1)

                def measure(j, k, lap):
                    p = k % 2
                    act.wait_ge(s["leaky"], j + 1)
                    act.activation(squares[:], leaky[:, p, :], ACT.Square, accum_out=length[:, 0, p:p + 1])\
                        .then_inc(s["squared"], 1)
                    act.wait_ge(s["squared"], j + 1)
                    act.activation(length[:, 1, p:p + 1], length[:, 0, p:p + 1], ACT.Sqrt).then_inc(s["rooted"], 1)

                groups = load_groups(act, graph)
                evacuate(*at(0, 0))
                evacuate(*at(0, 1))
                measure(*at(0, 0))
                evacuate(*at(0, 2))
                measure(*at(0, 1))
                norm.deviation(act, eps, 0, 0)
                with act.Fori(0, groups) as g:
                    for k in range(RING):
                        evacuate(*at(g, k + 3))
                        measure(*at(g, k + 2))
                        norm.deviation(act, eps, g * RING + k + 1, (k + 1) % 2)

            @block.tensor
            def _(pe):
                def gather_sum(j, k, lap):
                    pe.wait_ge(s["in_g"][k], (lap + 1) * 16)
                    pe.wait_ge(s["made"], j + 1)
                    for f in range(2):
                        last = pe.matmul(ps_a[k % 2][:, f * P:(f + 1) * P], gathered[:, k, f * P:(f + 1) * P],
                                         hot[:, k % 2, :], start=True, stop=True)
                    last.then_inc(s["g_done"], 1)
                    pe.wait_ge(s["in_x"][k], (lap + 1) * 16)
                    for f in range(2):
                        last = pe.transpose(ps_x[k % 2][:, f * P:(f + 1) * P], x[:, k, f * P:(f + 1) * P], c.ident[:])
                    last.then_inc(s["a_done"], 1)

                def product(j, k, lap):
                    pe.wait_ge(s["acc"], j + 1)
                    pe.wait_ge(s["xt"], j + 1)
                    for i in range(2):
                        pe.matmul(ps_b[k % 2], x_t[:, k % 2, i * P:(i + 1) * P], w1[:, i, :], start=(i == 0), stop=False)
                    pe.wait_ge(s["mix"], j + 1)
                    for i in range(2):
                        last = pe.matmul(ps_b[k % 2], mix_t[:, k % 2, i * P:(i + 1) * P], w2[:, i, :], start=False,
                                         stop=(i == 1))
                    last.then_inc(s["b_done"], 1)

                groups = load_groups(pe, graph)
                gather_sum(*at(0, 0))
                gather_sum(*at(0, 1))
                product(*at(0, 0))
                gather_sum(*at(0, 2))
                product(*at(0, 1))
                with pe.Fori(0, groups) as g:
                    for k in range(RING):
                        gather_sum(*at(g, k + 3))
                        product(*at(g, k + 2))


MASK = -1e30
FLOOR = -1e29
TINY = 1e-24
LN_SCALE = 16


class InverseRoot:

    def __init__(self, ph, name):
        self.v = ph.sb(f"{name}_v", [P, 2], F32)
        self.log = ph.sb(f"{name}_log", [P, 2], F32)
        self.y = ph.sb(f"{name}_y", [P, 2], F32)
        self.a = ph.sb(f"{name}_a", [P, 2], F32)
        self.b = ph.sb(f"{name}_b", [P, 2], F32)
        self.root = ph.sb(f"{name}_root", [P, 2], F32)
        self.have_v, self.logged, self.first, self.s_a, self.s_b, self.done = (
            ph.sem(f"{name}_{k}") for k in ("have_v", "logged", "first", "s_a", "s_b", "done"))

    def guess(self, act, shift, j, p):
        act.wait_ge(self.have_v, j + 1)
        act.activation(self.log[:, p:p + 1], self.v[:, p:p + 1], ACT.Ln, scale=float(2 ** LN_SCALE)).then_inc(self.logged, 1)
        act.wait_ge(self.logged, j + 1)
        act.activation(self.y[:, p:p + 1], self.log[:, p:p + 1], ACT.Exp, scale=-0.5, bias=shift[:])\
            .then_inc(self.first, 1)

    def refine(self, dve, j, p):
        y, q = self.y[:, p:p + 1], slice(p, p + 1)
        dve.wait_ge(self.first, j + 1)
        dve.scalar_tensor_tensor(self.a[:, q], y, y, self.v[:, q], ALU.mult, ALU.mult).then_inc(self.s_a, 1)
        dve.wait_ge(self.s_a, j + 1)
        dve.tensor_scalar(self.b[:, q], self.a[:, q], -0.5, 1.5, ALU.mult, ALU.add).then_inc(self.s_b, 1)
        dve.wait_ge(self.s_b, j + 1)
        dve.tensor_tensor(self.root[:, q], self.b[:, q], y, ALU.mult).then_inc(self.done, 1)


def attention_hop(nc, c, graph, name, head_w, tail_w, shift, x_in, x_out, residual=None):
    last_hop = residual is not None
    with Phase(nc, name) as ph:
        x = ph.sb("x", [P, RING, D], F32)
        res = ph.sb("res", [P, RING, D], F32) if last_hop else None
        gathered = ph.sb("gathered", [P, RING, D + 1], F32)
        index = ph.sb("index", [P, RING, 1], I32)
        kind = ph.sb("kind", [P, RING, GROUP], F32)
        mask = ph.sb("mask", [P, RING, P], BF16)
        kind_t = ph.sb("kind_t", [GROUP, 2, P], F32)
        x_t = ph.sb("x_t", [P, 2, D], F32)
        head_t = ph.sb("head_t", [GROUP, 2, P], F32)
        tail = ph.sb("tail", [P, 2], F32)
        junk = ph.sb("junk", [P, D + 1], F32)
        diag = ph.sb("diag", [P, 2, P], F32)
        fifth = ph.sb("fifth", [P, 2, P], F32)
        minus = ph.sb("minus", [P, 2, P + 1], F32)
        small = ph.sb("small", [P, 8, 2], F32)
        minus_max = ph.sb("minus_max", [P, 2], F32)
        expo = ph.sb("expo", [P, 4, P + 1], F32)
        sums = ph.sb("sums", [P, 4], F32)
        expo_t = ph.sb("expo_t", [P, 2, P], F32)
        scale_old = ph.sb("scale_old", [P, 2], F32)
        denom = ph.sb("denom", [P, 2], F32)
        agg = ph.sb("agg", [P, 2, D], F32)
        y = ph.sb("y", [P, 2, D], F32)
        squares = ph.sb("squares", [P, D], F32)
        total_sq = ph.sb("total_sq", [P, 2], F32)
        summed = ph.sb("summed", [P, 2, D], F32) if last_hop else None
        result = ph.sb("result", [P, RING, D], F32)
        restart = ph.sb("restart", [P, ITEMS], F32)
        ps_x = ph.ps("x", [P, 2 * D])
        ps_k = ph.ps("k", [P, 2 * D])
        ps_h = ph.ps("h", [P, 2 * D])
        ps_w = ph.ps("w", [P, 2 * D])
        ps_e = ph.ps("e", [P, 2 * D])
        ps_t = ph.ps("t", [P, 2 * D])
        ps_g = ph.ps("g", [P, 2 * D])
        s = ring_sems(ph, "y", "agg_done", last_hop)
        for k in ("made", "turned", "kt", "xt", "hw_done", "ht", "tail", "diag", "e_done", "fifth", "minus", "mx", "lk",
                  "old", "mm", "expo", "t_done", "expo_t", "agg_done", "c1", "c2", "den", "agg", "dmax", "rden", "y",
                  "squared"):
            s[k] = ph.sem(k)
        inv = InverseRoot(ph, "inv")
        if last_hop:
            s["summed"] = ph.sem("summed")
            norm, inv2 = Norm(ph, s, "norm"), InverseRoot(ph, "inv2")
        with nc.Block() as block:
            @block.sync
            def _(sp):
                move_tiles(sp, graph, s, x, x_in, result, x_out, (res, residual) if last_hop else None)

            @block.gpsimd
            def _(pool):
                gather_rows(pool, graph, s, index, gathered, x_in)

            @block.vector
            def _(dve):
                def make(j, k, lap):
                    dve.tensor_scalar(kind[:, k, :], c.iota[:, 0:GROUP], graph.meta[:, bass.ds(j, 1), KIND], None,
                                      ALU.is_equal)
                    dve.tensor_scalar(mask[:, k, :], c.iota[:, 0:P], graph.meta[:, bass.ds(j, 1), NODE], MASK,
                                      ALU.not_equal, ALU.mult).then_inc(s["made"], 1)

                def score(j, k, lap):
                    p = k % 2
                    dve.wait_ge(s["hw_done"], j + 1)
                    dve.tensor_tensor_reduce(out=junk[:], in0=gathered[:, k, :], in1=ps_w[:, 0:D + 1], scale=1.0,
                                             scalar=0.0, op0=ALU.mult, op1=ALU.add, accum_out=tail[:, p:p + 1])\
                        .then_inc(s["tail"], 1)
                    dve.wait_ge(s["tail"], j + 1)
                    dve.tensor_scalar(diag[:, p, :], c.ident[:], tail[:, p:p + 1], None, ALU.mult).then_inc(s["diag"], 1)

                def maximum(j, k, lap):
                    p = k % 2
                    q = slice(p, p + 1)
                    old = minus[:, p, P:P + 1]
                    dve.scalar_tensor_tensor(old, minus_max[:, 1 - p:2 - p], graph.keep[:, bass.ds(j, 1)],
                                             restart[:, bass.ds(j, 1)], ALU.mult, ALU.add).then_inc(s["old"], 1)
                    dve.wait_ge(s["fifth"], j + 1)
                    dve.tensor_reduce(small[:, 0, q], ps_e[:, 0:P], AX.X, ALU.max).then_inc(s["mx"], 1)
                    dve.scalar_tensor_tensor(minus[:, p, 0:P], ps_e[:, 0:P], -1.0, fifth[:, p, :], ALU.mult, ALU.min)\
                        .then_inc(s["minus"], 1)
                    dve.wait_ge(s["mx"], j + 1)
                    dve.scalar_tensor_tensor(small[:, 1, q], small[:, 0, q], 0.2, small[:, 0, q], ALU.mult, ALU.max)\
                        .then_inc(s["lk"], 1)
                    dve.wait_ge(s["lk"], j + 1)
                    dve.wait_ge(s["old"], j + 1)
                    dve.scalar_tensor_tensor(minus_max[:, q], small[:, 1, q], -1.0, old, ALU.mult, ALU.min)\
                        .then_inc(s["mm"], 1)

                def combine(j, k, lap):
                    p = k % 2
                    q = slice(p, p + 1)
                    corr = expo[:, k % 4, P:P + 1]
                    dve.wait_ge(s["expo"], j + 1)
                    dve.tensor_scalar(scale_old[:, q], corr, graph.keep[:, bass.ds(j, 1)], None, ALU.mult)\
                        .then_inc(s["c1"], 1)
                    dve.tensor_tensor(small[:, 2, q], sums[:, k % 4:k % 4 + 1], corr, ALU.subtract).then_inc(s["c2"], 1)
                    dve.wait_ge(s["c1"], j + 1)
                    dve.wait_ge(s["c2"], j + 1)
                    dve.scalar_tensor_tensor(denom[:, q], denom[:, 1 - p:2 - p], scale_old[:, q], small[:, 2, q],
                                             ALU.mult, ALU.add).then_inc(s["den"], 1)
                    dve.wait_ge(s["agg_done"], j + 1)
                    dve.scalar_tensor_tensor(agg[:, p, :], agg[:, 1 - p, :], scale_old[:, q], ps_g[:, 0:D],
                                             ALU.mult, ALU.add).then_inc(s["agg"], 1)
                    dve.wait_ge(s["den"], j + 1)
                    dve.tensor_scalar(small[:, 3, q], denom[:, q], 1e-30, None, ALU.max).then_inc(s["dmax"], 1)
                    dve.wait_ge(s["dmax"], j + 1)
                    dve.reciprocal(small[:, 4, q], small[:, 3, q]).then_inc(s["rden"], 1)
                    dve.wait_ge(s["rden"], j + 1)
                    dve.wait_ge(s["agg"], j + 1)
                    dve.scalar_tensor_tensor(y[:, p, :], agg[:, p, :], small[:, 4, q], x[:, k, :], ALU.mult, ALU.add)\
                        .then_inc(s["y"], 1)
                    dve.wait_ge(s["squared"], j + 1)
                    dve.tensor_scalar(inv.v[:, q], total_sq[:, q], TINY, None, ALU.max).then_inc(inv.have_v, 1)

                def scale_rows(j, k, lap):
                    p = k % 2
                    inv.refine(dve, j, p)
                    if not last_hop:
                        dve.wait_ge(s["stored"][k], (lap + 1) * 16)
                        dve.wait_ge(inv.done, j + 1)
                        dve.tensor_scalar(result[:, k, :], y[:, p, :], inv.root[:, p:p + 1], None, ALU.mult)\
                            .then_inc(s["out_ready"], 1)
                        return
                    dve.wait_ge(s["in_res"][k], (lap + 1) * 16)
                    dve.wait_ge(inv.done, j + 1)
                    dve.scalar_tensor_tensor(summed[:, p, :], y[:, p, :], inv.root[:, p:p + 1], res[:, k, :],
                                             ALU.mult, ALU.add).then_inc(s["res_done"], 1)
                    dve.wait_ge(s["res_done"], j + 1)
                    norm.moments(dve, s, summed[:, p, :], j, p)
                    dve.wait_ge(norm.ag, j + 1)
                    dve.tensor_scalar(inv2.v[:, p:p + 1], norm.mv[:, p, 1:2], EPS, None, ALU.add).then_inc(inv2.have_v, 1)

                def normalise(j, k, lap):
                    p = k % 2
                    inv2.refine(dve, j, p)
                    dve.wait_ge(s["stored"][k], (lap + 1) * 16)
                    dve.wait_ge(inv2.done, j + 1)
                    dve.tensor_scalar(result[:, k, :], summed[:, p, :], norm.mv[:, p, 0:1], inv2.root[:, p:p + 1],
                                      ALU.subtract, ALU.mult).then_inc(s["out_ready"], 1)

                def transposed(j, k, lap):
                    dve.wait_ge(s["t_done"], j + 1)
                    dve.tensor_copy(expo_t[:, k % 2, :], ps_t[:, 0:P]).then_inc(s["expo_t"], 1)

                for t in (agg, denom, minus_max):
                    dve.memset(t[:], 0.0)
                dve.tensor_scalar(restart[:], graph.keep[:], FLOOR, -FLOOR, ALU.mult, ALU.add).then_inc(s["zeroed"], 1)
                dve.memset(result[:], 0.0).then_inc(s["zeroed"], 1)
                dve.wait_ge(s["zeroed"], 2)
                groups = load_groups(dve, graph)
                for k in range(RING):
                    make(*at(0, k))
                for n in range(-5, 0):
                    for step, ahead in ((maximum, 4), (score, 5), (combine, 2), (scale_rows, 1), (transposed, 3)):
                        if n + ahead >= 0:
                            step(*at(0, n + ahead))
                with dve.Fori(0, groups) as g:
                    for k in range(RING):
                        maximum(*at(g, k + 4))
                        score(*at(g, k + 5))
                        combine(*at(g, k + 2))
                        scale_rows(*at(g, k + 1))
                        if last_hop:
                            normalise(*at(g, k))
                        transposed(*at(g, k + 3))
                        make(*at(g + 1, k))

            @block.scalar
            def _(act):
                def leak(j, k, lap):
                    act.wait_ge(s["e_done"], j + 1)
                    act.activation(fifth[:, k % 2, :], ps_e[:, 0:P], ACT.Copy, scale=-0.2).then_inc(s["fifth"], 1)

                def heads(j, k, lap):
                    act.wait_ge(s["hw_done"], j + 1)
                    act.copy(head_t[0:R2, k % 2, :], ps_h[0:R2, 0:P]).then_inc(s["ht"], 1)

                def evacuate(j, k, lap):
                    act.wait_ge(s["turned"], j + 1)
                    act.copy(x_t[:, k % 2, :], ps_x[:, 0:D]).then_inc(s["xt"], 1)
                    act.copy(kind_t[:, k % 2, :], ps_k[0:GROUP, 0:P]).then_inc(s["kt"], 1)

                def exponentials(j, k, lap):
                    act.wait_ge(s["minus"], j + 1)
                    act.wait_ge(s["mm"], j + 1)
                    act.activation(expo[:, k % 4, :], minus[:, k % 2, :], ACT.Exp, scale=-1.0,
                                   bias=minus_max[:, k % 2:k % 2 + 1], accum_out=sums[:, k % 4:k % 4 + 1])\
                        .then_inc(s["expo"], 1)

                def measure(j, k, lap):
                    act.wait_ge(s["y"], j + 1)
                    act.activation(squares[:], y[:, k % 2, :], ACT.Square, accum_out=total_sq[:, k % 2:k % 2 + 1])\
                        .then_inc(s["squared"], 1)
                    inv.guess(act, shift, j, k % 2)

                def outer(j, k, lap):
                    inv2.guess(act, shift, j, k % 2)

                steps = [(leak, 4), (heads, 5), (evacuate, 6), (exponentials, 4), (measure, 2)]
                if last_hop:
                    steps.append((outer, 1))
                groups = load_groups(act, graph)
                for n in range(-6, 0):
                    for step, ahead in steps:
                        if n + ahead >= 0:
                            step(*at(0, n + ahead))
                with act.Fori(0, groups) as g:
                    for k in range(RING):
                        for step, ahead in steps:
                            step(*at(g, k + ahead))

            @block.tensor
            def _(pe):
                def turn(j, k, lap):
                    pe.wait_ge(s["made"], j + 1)
                    pe.transpose(ps_k[0:GROUP, 0:P], kind[:, k, :], c.ident[:])
                    pe.wait_ge(s["in_x"][k], (lap + 1) * 16)
                    for f in range(2):
                        last = pe.transpose(ps_x[:, f * P:(f + 1) * P], x[:, k, f * P:(f + 1) * P], c.ident[:])
                    last.then_inc(s["turned"], 1)

                def project(j, k, lap):
                    p = k % 2
                    pe.wait_ge(s["kt"], j + 1)
                    pe.wait_ge(s["in_g"][k], (lap + 1) * 16)
                    pe.matmul(ps_w[:, 0:D + 1], kind_t[0:R2, p, :], tail_w[0:R2, :], start=True, stop=True)
                    pe.wait_ge(s["xt"], j + 1)
                    for f in range(2):
                        last = pe.matmul(ps_h[0:R2, 0:P], head_w[:, f, 0:R2], x_t[:, p, f * P:(f + 1) * P],
                                         start=(f == 0), stop=(f == 1))
                    last.then_inc(s["hw_done"], 1)

                def scores(j, k, lap):
                    p = k % 2
                    pe.wait_ge(s["minus"], j) if not isinstance(j, int) or j > 0 else None
                    pe.matmul(ps_e[:, 0:P], mask[:, k, :], c.ident_b[:], start=True, stop=False)
                    pe.wait_ge(s["ht"], j + 1)
                    pe.matmul(ps_e[:, 0:P], head_t[0:R2, p, :], kind_t[0:R2, p, :], start=False, stop=False)
                    pe.wait_ge(s["diag"], j + 1)
                    pe.matmul(ps_e[:, 0:P], c.ones[:], diag[:, p, :], start=False, stop=True).then_inc(s["e_done"], 1)

                def transpose(j, k, lap):
                    pe.wait_ge(s["expo"], j + 1)
                    pe.transpose(ps_t[:, 0:P], expo[:, k % 4, 0:P], c.ident[:]).then_inc(s["t_done"], 1)

                def aggregate(j, k, lap):
                    pe.wait_ge(s["expo_t"], j + 1)
                    if not isinstance(j, int) or j > 0:
                        pe.wait_ge(s["agg"], j)
                    pe.matmul(ps_g[:, 0:D], expo_t[:, k % 2, :], gathered[:, k, 0:D], start=True, stop=True)\
                        .then_inc(s["agg_done"], 1)

                steps = [(scores, 4), (project, 5), (turn, 6), (aggregate, 2), (transpose, 3)]
                groups = load_groups(pe, graph)
                for n in range(-6, 0):
                    for step, ahead in steps:
                        if n + ahead >= 0:
                            step(*at(0, n + ahead))
                with pe.Fori(0, groups) as g:
                    for k in range(RING):
                        for step, ahead in steps:
                            step(*at(g, k + ahead))


class Weights:
    def __init__(self, sb):
        self.l0 = sb("l0_w", [P, 4, D], F32)
        self.gamma, self.beta = sb("gamma", [P, D], F32), sb("beta", [P, D], F32)
        self.root = [sb(f"root{k}", [P, 2, D], F32) for k in range(2)]
        self.table = [sb(f"blocks{k}", [K3, 4 * D], BF16) for k in range(2)]
        self.bias = [sb(f"l1_bias{k}", [P, D], F32) for k in range(2)]
        self.head = sb("head_w", [P, 2, GROUP], F32)
        self.tail = sb("tail_w", [GROUP, D + 1], F32)
        self.l3 = [sb(f"l3_w{k}", [P, 2, D], F32) for k in range(2)]
        self.l3_bias = sb("l3_bias", [P, D], F32)
        self.eps = sb("eps", [P, 1], F32)
        self.shift = sb("shift", [P, 1], F32)


def load_weights(nc, c, w, a):
    with Phase(nc, "weights") as ph:
        full = [ph.sb(f"full{k}", [K3, 4 * D], F32) for k in range(2)]
        rest = [ph.sb(f"rest{k}", [K3, 4 * D], F32) for k in range(2)]
        piece = [ph.sb(f"piece{k}", [K3, 4 * D], BF16) for k in range(2)]
        fc = ph.sb("fc", [P, 2, 2 * D + 1], F32)
        rel = ph.sb("rel", [P, 2, R2], F32)
        bias2 = ph.sb("bias2", [P, D], F32)
        ps_h = ph.ps("h", [P, 2 * D])
        ps_t = ph.ps("t", [P, 2 * D])
        s_in, s_zero, s_v, s_fc = ph.sem("in"), ph.sem("zero"), ph.sem("v"), ph.sem("fc")
        with nc.Block() as block:
            @block.sync
            def _(sp):
                n = 0
                halves = "(b p) o -> p b o"
                for dst, src in ((w.l0[:], a["L0_gnn_W"].rearrange(halves, p=P)),
                                 (w.root[0][:], a["L1_gnn_root1"].rearrange(halves, p=P)),
                                 (w.root[1][:], a["L1_gnn_root2"].rearrange(halves, p=P)),
                                 (w.l3[0][:], a["L3_gnn_W1"].rearrange(halves, p=P)),
                                 (w.l3[1][:], a["L3_gnn_W2"].rearrange(halves, p=P)),
                                 (fc[:, :, 0:2 * D], a["L2_gnn_fc_w"].rearrange(halves, p=P)),
                                 (rel[:], a["L2_gnn_relation_emb"].rearrange(halves, p=P)),
                                 (w.gamma[:], a["L0_gnn_gamma"].partition_broadcast(P)),
                                 (w.beta[:], a["L0_gnn_beta"].partition_broadcast(P)),
                                 (w.bias[0][:], a["L1_gnn_bias1"].partition_broadcast(P)),
                                 (w.bias[1][:], a["L1_gnn_bias2"].partition_broadcast(P)),
                                 (w.l3_bias[:], a["L3_gnn_b1"].partition_broadcast(P)),
                                 (bias2[:], a["L3_gnn_b2"].partition_broadcast(P))):
                    sp.dma_start(dst, src).then_inc(s_in, 16)
                    n += 16
                with nc.allow_non_contiguous_dma(reason="256 values once"):
                    sp.dma_start(fc[:, :, 2 * D:], a["L2_gnn_fc_b"].rearrange("(b p o) -> p b o", p=P, o=1)).then_inc(s_in, 16)
                n += 16
                sp.wait_ge(s_zero, 1)
                for k in range(2):
                    for part in range(3):
                        sp.dma_start(full[k][part * GROUP:part * GROUP + R1, :], a[f"L1_gnn_W{k + 1}"]).then_inc(s_in, 16)
                        n += 16
                assert n == 20 * 16
                sp.wait_ge(s_in, n)

            @block.vector
            def _(dve):
                chain = Chain(dve, s_v)
                for k in range(2):
                    chain.step(dve.memset(full[k][:], 0.0))
                dve.memset(w.eps[:], EPS).then_inc(s_zero, 1)
                dve.memset(w.shift[:], float(np.log(2.0) * LN_SCALE / 2))
                dve.wait_ge(s_in, 20 * 16)
                for k in range(2):
                    source = full[k]
                    for part in range(3):
                        rows = slice(part * GROUP, (part + 1) * GROUP)
                        chain.step(dve.tensor_copy(piece[k][:], source[:]))
                        chain.step(dve.tensor_copy(w.table[k][rows, :], piece[k][rows, :]))
                        chain.step(dve.tensor_tensor(rest[k][:], source[:], piece[k][:], ALU.subtract))
                        source = rest[k]
                chain.step(dve.tensor_tensor(w.l3_bias[:], w.l3_bias[:], bias2[:], ALU.add))
                dve.wait_ge(s_fc, 1)
                for f in range(2):
                    chain.step(dve.tensor_copy(w.head[:, f, 0:R2], ps_h[:, f * GROUP:f * GROUP + R2]))
                chain.step(dve.tensor_copy(w.tail[0:R2, :], ps_t[0:R2, 0:D + 1]))

            @block.tensor
            def _(pe):
                pe.wait_ge(s_in, 20 * 16)
                for f in range(2):
                    for b in range(2):
                        pe.matmul(ps_h[:, f * GROUP:f * GROUP + R2], fc[:, b, f * P:(f + 1) * P], rel[:, b, :],
                                  start=(b == 0), stop=(b == 1))
                for b in range(2):
                    last = pe.matmul(ps_t[0:R2, 0:D + 1], rel[:, b, :], fc[:, b, D:], start=(b == 0), stop=(b == 1))
                last.then_inc(s_fc, 1)


def build(nc, a, out):
    def dram(name, shape, dt=F32):
        return nc.dram_tensor(name, shape, dt).ap()

    with ExitStack() as ctx:
        def sb(name, shape, dt):
            return ctx.enter_context(nc.sbuf_tensor(name, shape, dt))

        c, w = Constants(sb), Weights(sb)
        graphs = [Graph(sb, "by_src"), Graph(sb, "by_dst")]
        sorted_records = [dram(f"sorted{o}", (SORTED, 4)) for o in range(2)]
        item_rows = [(dram(f"rows_i{o}", (3, ITEMS), I32), dram(f"rows_f{o}", (2, ITEMS))) for o in range(2)]
        counts = dram("counts", (ALL_ROWS, R1))
        x1, h, x2, z, x3 = (dram(n, (ALL_ROWS, D)) for n in ("x1", "h", "x2", "z", "x3"))
        make_constants(nc, c)
        with ExitStack() as prep:
            def sb_prep(name, shape, dt):
                return prep.enter_context(nc.sbuf_tensor(name, shape, dt))
            for g, n in zip(graphs, ("src", "dst")):
                g.prepare(sb_prep, n)
            sort_edges(nc, c, [a[n] for n in ("src", "dst", "edge_type_16", "edge_type_24", "edge_weight")],
                       graphs, sorted_records)
            make_items(nc, c, graphs, sorted_records, item_rows)
        load_weights(nc, c, w, a)
        by_src, by_dst = graphs
        count_edges(nc, c, by_dst, counts)
        mean_layer(nc, c, by_src, w.l0, w.gamma, w.beta, w.eps, a["x"], x1)
        relation_layer(nc, c, by_dst, "l1a", w.root[0], w.table[0], w.bias[0], w.eps, x1, h)
        relation_layer(nc, c, by_dst, "l1b", w.root[1], w.table[1], w.bias[1], w.eps, h, x2, residual=x1)
        attention_hop(nc, c, by_src, "l2a", w.head, w.tail, w.shift, x2, z)
        attention_hop(nc, c, by_src, "l2b", w.head, w.tail, w.shift, z, x3, residual=x2)
        interaction_layer(nc, c, by_dst, w.l3[0], w.l3[1], w.l3_bias, w.eps, x3, out)


def laid_out(inputs):
    a = {k: np.asarray(v) for k, v in inputs.items()}
    x = np.zeros((ALL_ROWS, D), np.float32)
    x[:N_NODES] = a["x"]
    a["x"] = x
    for k in ("L0_gnn_W", "L2_gnn_relation_emb", "L3_gnn_W1", "L3_gnn_W2"):
        a[k] = a[k].T
    for k in ("L1_gnn_W1", "L1_gnn_W2"):
        a[k] = a[k].transpose(0, 2, 1, 3).reshape(R1, 4 * D)
    return {k: np.ascontiguousarray(v) for k, v in a.items()}


def kernel(**inputs):
    import concourse.bacc as bacc
    from concourse.bass_utils import run_bass_kernel_spmd

    nc = bacc.Bacc("TRN2", target_bir_lowering=False, num_devices=1)
    arrays = {f"in_{k}": v for k, v in laid_out(inputs).items()}
    aps = {k[3:]: nc.dram_tensor(k, v.shape, mybir.dt.from_np(v.dtype), kind="ExternalInput").ap()
           for k, v in arrays.items()}
    out = nc.dram_tensor("out", (ALL_ROWS, D), F32, kind="ExternalOutput").ap()
    build(nc, aps, out)
    r = run_bass_kernel_spmd(nc, [arrays], core_ids=[0])
    return r.results[0]["out"][:N_NODES]
```

```python
from contextlib import ExitStack

import numpy as np

import concourse.bass as bass
from concourse import mybir

F32 = mybir.dt.float32
BF16 = mybir.dt.bfloat16
F16 = mybir.dt.float16
I32 = mybir.dt.int32
ALU = mybir.AluOpType
ACT = mybir.ActivationFunctionType
AX = mybir.AxisListType

P = 128
N_NODES, D, N_EDGES = 50000, 256, 25000
TILES = -(-N_NODES // P)
ROWS = TILES * P
RING = 8
ALL_ROWS = ROWS + RING * P
EP, EC = 125, 200
MAX_ITEMS = TILES + N_EDGES // P
ITEM_CHUNKS = -(-(MAX_ITEMS + 3 * RING) // P)
ITEMS = ITEM_CHUNKS * P
R1, R2 = 16, 24
GROUP = 32
K3 = 3 * GROUP
EPS = 1e-5
FAR = 1 << 20
assert EP * EC == N_EDGES and max(R1, R2) < GROUP
OTHER, NODE, KIND, WEIGHT = range(4)
LOAD, STORE, LAST = range(3)


class Graph:

    def __init__(self, sb, name):
        self.meta = sb(f"{name}_meta", [P, ITEMS, 4], F32)
        self.keep = sb(f"{name}_keep", [P, ITEMS], F32)
        self.share = sb(f"{name}_share", [P, ITEMS], F32)
        self.table = sb(f"{name}_table", [1, 3, ITEMS], I32)
        self.groups = sb(f"{name}_groups", [1, 1], I32)


    def prepare(self, sb, name):
        self.buckets = {k: sb(f"{name}_{k}", [P, TILES + 1], I32 if k.startswith("int") else F32)
                        for k in ("count", "end", "base", "seed", "int", "int2")}


def at(group, offset):
    return group * RING + offset, offset % RING, group + offset // RING


class Phase:

    def __init__(self, nc, name):
        self.nc, self.name, self.sems, self.ctx = nc, name, [], ExitStack()

    def __enter__(self):
        self.ctx.__enter__()
        return self

    def sem(self, name):
        s = self.ctx.enter_context(self.nc.semaphore(f"{self.name}_{name}"))
        self.sems.append(s)
        return s

    def pool_dma_sem(self, name):
        return self.nc.alloc_semaphore(f"{self.name}_{name}")

    def sb(self, name, shape, dt):
        return self.ctx.enter_context(self.nc.sbuf_tensor(f"{self.name}_{name}", shape, dt))

    def ps(self, name, shape, dt=F32):
        return self.ctx.enter_context(self.nc.psum_tensor(f"{self.name}_ps_{name}", shape, dt))

    def __exit__(self, *error):
        if error[0] is None:
            for s in self.sems:
                self.nc.gpsimd.sem_clear(s)
            self.nc.all_engine_barrier()
        return self.ctx.__exit__(*error)


def row_of(eng, graph, field, item):
    return eng.value_load(graph.table[0:1, field, bass.ds(item, 1)], min_val=0, max_val=ALL_ROWS - P)


def load_groups(eng, graph):
    return eng.value_load(graph.groups[0:1, 0:1], min_val=1, max_val=-(-MAX_ITEMS // RING))


def move_tiles(sp, graph, s, tiles, source, result, target, residual=None):
    load_regs, store_regs = ([sp.alloc_register(f"{s['name']}_{n}{k}") for k in range(RING)] for n in ("load", "store"))

    def rows_of(regs, field, first_item):
        sp.load(regs, graph.table[0:1, field, bass.ds(first_item, RING)])
        return [sp.snap(r, min_val=0, max_val=ALL_ROWS - P) for r in regs]

    first_rows = rows_of(load_regs, LOAD, 0)

    def load(item, slot):
        row = first_rows[item]
        sp.dma_start(tiles[:, slot, :], source[bass.ds(row, P), :]).then_inc(s["in_x"][slot], 16)
        if residual is not None:
            sp.dma_start(residual[0][:, slot, :], residual[1][bass.ds(row, P), :]).then_inc(s["in_res"][slot], 16)

    sp.wait_ge(s["zeroed"], 2)
    for slot in range(RING):
        sp.dma_start(target[ROWS + slot * P:ROWS + (slot + 1) * P, :], result[:, slot, :]).then_inc(s["stored"][slot], 16)
    for k in range(RING):
        load(k, k)
    groups = load_groups(sp, graph)
    with sp.Fori(0, groups) as g:
        rows, next_rows = rows_of(store_regs, STORE, g * RING), rows_of(load_regs, LOAD, (g + 1) * RING)
        for k in range(RING):
            item, slot, _ = at(g, k)
            row, nrow = rows[k], next_rows[k]
            sp.wait_ge(s["out_ready"], item + 1)
            sp.dma_start(target[bass.ds(row, P), :], result[:, slot, :]).then_inc(s["stored"][slot], 16)
            sp.wait_ge(s[s["x_done"]], item + 1)
            sp.dma_start(tiles[:, slot, :], source[bass.ds(nrow, P), :]).then_inc(s["in_x"][slot], 16)
            if residual is not None:
                sp.wait_ge(s["res_done"], item + 1)
                sp.dma_start(residual[0][:, slot, :], residual[1][bass.ds(nrow, P), :])\
                    .then_inc(s["in_res"][slot], 16)
    for slot in range(RING):
        sp.wait_ge(s["stored"][slot], (groups + 1) * 16)
        sp.sem_inc(s["passed"], 1)
        sp.wait_ge(s["in_x"][slot], (groups + 1) * 16)
        sp.sem_inc(s["passed"], 1)
        if residual is not None:
            sp.wait_ge(s["in_res"][slot], (groups + 1) * 16)
            sp.sem_inc(s["passed"], 1)


def gather_rows(pool, graph, s, index, gathered, source):
    limit = pool.alloc_register(f"limit_{s['name']}")
    pool.reg_mov(limit, N_NODES - 1)
    for slot in range(RING):
        pool.memset(gathered[:, slot, :], 0.0).then_inc(s["g_zeroed"], 1)
    pool.wait_ge(s["g_zeroed"], RING)
    if gathered.shape[2] > D:
        for slot in range(RING):
            pool.memset(gathered[:, slot, D:], 1.0).then_inc(s["g_zeroed"], 1)
        pool.wait_ge(s["g_zeroed"], 2 * RING)

    def gather(item, slot):
        pool.tensor_copy(index[:, slot, :], graph.meta[:, bass.ds(item, 1), OTHER].bitcast(I32))\
            .then_inc(s["index_copied"], 1)
        pool.wait_ge(s["index_copied"], item + 1)
        pool.sem_inc(s["passed"], 1)
        pool.indirect_dma_start(gathered[:, slot, 0:D], None, source[0:N_NODES, :],
                                bass.IndirectOffsetOnAxis(ap=index[:, slot, :], axis=0),
                                bounds_check=limit, oob_is_err=False).then_inc(s["in_g"][slot], 16)

    for k in range(RING):
        gather(k, k)
    groups = load_groups(pool, graph)
    with pool.Fori(0, groups) as g:
        for k in range(RING):
            item, slot, _ = at(g, k)
            pool.wait_ge(s[s["g_last"]], item + 1)
            pool.sem_inc(s["passed"], 1)
            gather(item + RING, slot)
    for slot in range(RING):
        pool.wait_ge(s["in_g"][slot], (groups + 1) * 16)
        pool.sem_inc(s["passed"], 1)


def ring_sems(ph, x_done, g_done="g_done", residual=False):
    s = {k: ph.sem(k) for k in ("zeroed", "out_ready", "passed", "g_zeroed", "index_copied")}
    s["in_x"] = [ph.sem(f"in_x{k}") for k in range(RING)]
    s["in_g"] = [ph.pool_dma_sem(f"in_g{k}") for k in range(RING)]
    s["stored"] = [ph.sem(f"stored{k}") for k in range(RING)]
    if residual:
        s["in_res"] = [ph.sem(f"in_res{k}") for k in range(RING)]
        s["res_done"] = ph.sem("res_done")
    s["name"], s["x_done"], s["g_last"] = ph.name, x_done, g_done
    return s


class Chain:

    def __init__(self, eng, sem):
        self.eng, self.sem, self.count = eng, sem, 0

    def step(self, instruction):
        self.count += 1
        instruction.then_inc(self.sem, 1)
        self.eng.wait_ge(self.sem, self.count)


class Constants:
    def __init__(self, sb):
        self.iota16 = sb("iota16", [P, TILES + 1], F16)
        self.iota = sb("iota", [P, TILES + 1], F32)
        self.iota_kind = sb("iota_kind", [P, K3], F32)
        self.item_id = sb("item_id", [P, ITEM_CHUNKS], F32)
        self.spare_i = sb("spare_i", [P, ITEM_CHUNKS], I32)
        self.spare = sb("spare", [P, ITEM_CHUNKS], F32)
        self.ones_row = sb("ones_row", [P, TILES + 1], F32)
        self.zero_row = sb("zero_row", [P, TILES + 1], BF16)
        self.ones = sb("ones", [P, P], F32)
        self.ones_b = sb("ones_b", [P, P], BF16)
        self.zeros_b = sb("zeros_b", [P, P], BF16)
        self.ident = sb("ident", [P, P], F32)
        self.ident_b = sb("ident_b", [P, P], BF16)
        self.before = sb("before", [P, P], BF16)
        self.not_before = sb("not_before", [P, P], BF16)


def make_constants(nc, c):
    with Phase(nc, "const") as ph:
        made, numbered, spared = ph.sem("made"), ph.sem("numbered"), ph.sem("spared")
        with nc.Block() as block:
            @block.vector
            def _(dve):
                chain = Chain(dve, spared)
                dve.wait_ge(numbered, 1)
                chain.step(dve.tensor_single_scalar(c.spare_i[:], c.spare_i[:], RING - 1, op=ALU.bitwise_and))
                chain.step(dve.tensor_scalar(c.spare[:], c.spare_i[:], float(P), float(ROWS), ALU.mult, ALU.add))

            @block.gpsimd
            def _(pool):
                chain = Chain(pool, made)
                loose = dict(allow_small_or_imprecise_dtypes=True, channel_multiplier=0)
                pool.iota(c.iota16[:], [[1, TILES + 1]], 0, **loose)
                pool.iota(c.iota[:], [[1, TILES + 1]], 0, **loose)
                pool.iota(c.iota_kind[:], [[0, 3], [1, GROUP]], 0, **loose)
                pool.iota(c.item_id[:], [[P, ITEM_CHUNKS]], 0, channel_multiplier=1,
                          allow_small_or_imprecise_dtypes=True)
                chain.step(pool.iota(c.spare_i[:], [[P, ITEM_CHUNKS]], 0, channel_multiplier=1))
                pool.sem_inc(numbered, 1)
                for t in (c.ident, c.ident_b, c.before, c.zeros_b, c.zero_row):
                    chain.step(pool.memset(t[:], 0.0))
                for t in (c.ones, c.ones_b, c.not_before, c.ones_row):
                    chain.step(pool.memset(t[:], 1.0))
                for t in (c.ident, c.ident_b):
                    chain.step(pool.affine_select(out=t[:], in_=t[:], compare_op=ALU.not_equal, fill=1.0, base=0,
                                                  pattern=[[-1, P]], channel_multiplier=1))
                chain.step(pool.affine_select(out=c.before[:], in_=c.before[:], compare_op=ALU.is_ge, fill=1.0,
                                              base=0, pattern=[[-1, P]], channel_multiplier=1))
                chain.step(pool.affine_select(out=c.not_before[:], in_=c.not_before[:], compare_op=ALU.is_ge,
                                              fill=0.0, base=0, pattern=[[-1, P]], channel_multiplier=1))


def sort_edges(nc, c, arrays, graphs, item_records):
    src, dst, kind16, kind24, weight = arrays
    HALF = RING // 2
    with Phase(nc, "sort") as ph:
        raw = ph.sb("raw", [EP, 4, EC], I32)
        wt = ph.sb("wt", [EP, EC], F32)
        rec = ph.sb("rec", [EP, 2, EC, 4], F32)
        bucket_i = ph.sb("bucket_i", [EP, 2, EC], I32)
        local_i = ph.sb("local_i", [EP, 2, EC], I32)
        bucket = ph.sb("bucket", [EP, 2, EC + 1], F32)
        rank_f = ph.sb("rank_f", [EP, 2, 2, HALF], F32)
        rank_i = ph.sb("rank_i", [EP, 2, 2, HALF], I32)
        item_i = ph.sb("item_i", [EP, 2, 2, HALF], I32)
        lane_i = ph.sb("lane_i", [EP, 2, 2, HALF], I32)
        place = ph.sb("place", [EP, 2, 2, HALF], I32)
        onehot = ph.sb("onehot", [P, 2, RING, TILES + 1], BF16)
        junk = ph.sb("junk", [P, 2, TILES + 1], F32)
        slot_rec = ph.sb("slot_rec", [EP, 2, 2, HALF, 4], F32)
        hist = [ph.ps(f"hist{o}", [P, TILES + 1]) for o in range(2)]
        rank = [ph.ps(f"rank{o}", [P, TILES + 1]) for o in range(2)]
        s_in, s_dve, s_keys = ph.sem("in"), ph.sem("dve"), ph.sem("keys")
        s_hot, s_hist, s_start = ph.sem("hot"), ph.sem("hist"), ph.sem("start")
        s_hot2, s_rank, s_read, s_empty = ph.sem("hot2"), ph.sem("rank"), ph.sem("read"), ph.sem("empty")
        s_int, s_split, s_placed = ph.sem("int"), ph.sem("split"), ph.sem("placed")
        s_staged, s_freed, s_passed, s_rec, s_pads = (ph.sem(n) for n in ("staged", "freed", "passed", "rec", "pads"))
        s_out = [ph.pool_dma_sem(f"out{h}") for h in range(2)]
        out_per_half = 2 * HALF * 16

        def flat(t):
            return t[:].rearrange("p o c -> p (o c)")

        with nc.Block() as block:
            @block.sync
            def _(sp):
                for k, a in enumerate((src, dst, kind16, kind24)):
                    sp.dma_start(raw[:, k, :], a.rearrange("(p c) -> p c", p=EP)).then_inc(s_in, 16)
                sp.dma_start(wt[:], weight.rearrange("(p c) -> p c", p=EP)).then_inc(s_in, 16)
                sp.wait_ge(s_empty, 4)
                for o in range(2):
                    sp.dma_start(item_records[o].rearrange("(p i) f -> p i f", p=P), graphs[o].meta[:])\
                        .then_inc(s_pads, 16)
                sp.wait_ge(s_pads, 32)

            @block.vector
            def _(dve):
                chain = Chain(dve, s_dve)
                dve.memset(bucket[:, :, EC:], 0.0)
                dve.wait_ge(s_in, 80)
                for o in range(2):
                    chain.step(dve.tensor_single_scalar(bucket_i[:, o, :], raw[:, o, :], 7, op=ALU.logical_shift_right))
                    dve.tensor_copy(bucket[:, o, 0:EC], bucket_i[:, o, :]).then_inc(s_keys, 1)
                    chain.step(dve.tensor_single_scalar(local_i[:, o, :], raw[:, o, :], P - 1, op=ALU.bitwise_and))
                    dve.tensor_copy(rec[:, o, :, OTHER].bitcast(I32), raw[:, 1 - o, :])
                    dve.tensor_copy(rec[:, o, :, NODE], local_i[:, o, :])
                dve.tensor_copy(rec[:, 1, :, KIND], raw[:, 2, :])
                dve.tensor_copy(rec[:, 0, :, KIND], raw[:, 3, :])
                for o in range(2):
                    chain.step(dve.tensor_copy(rec[:, o, :, WEIGHT], wt[:]))
                dve.drain().then_inc(s_rec, 1)
                dve.wait_ge(s_keys, 2)

                def make(column, k, sem):
                    for o in range(2):
                        a = dve.snap(column + o * (EC + 1)) if not isinstance(column, int) else column + o * (EC + 1)
                        dve.tensor_scalar(onehot[0:EP, o, k, :], c.iota16[0:EP, :], flat(bucket)[:, bass.ds(a, 1)], None,
                                          ALU.is_equal).then_inc(sem, 1)

                with dve.Fori(0, EC // RING) as g:
                    for k in range(RING):
                        dve.wait_ge(s_hist, (g * RING + k) * 2 + 2)
                        make(g * RING + k, k, s_hot)
                dve.wait_ge(s_hist, 2 * (EC + RING))
                for o in range(2):
                    b = graphs[o].buckets
                    chain.step(dve.tensor_scalar(b["int"][:], hist[o][:], float(P - 1), None, ALU.add))
                    chain.step(dve.tensor_single_scalar(b["int2"][:], b["int"][:], 7, op=ALU.logical_shift_right))
                    chain.step(dve.tensor_scalar(b["count"][:], b["int2"][:], 1.0, None, ALU.max))
                    chain.step(dve.tensor_tensor_scan(b["end"][:], c.ones_row[:], b["count"][:], 0.0, ALU.mult, ALU.add))
                    chain.step(dve.tensor_tensor(b["base"][:], b["end"][:], b["count"][:], ALU.subtract))
                    chain.step(dve.tensor_scalar(b["seed"][:], b["base"][:], float(P), None, ALU.mult))
                dve.drain().then_inc(s_start, 1)

                make(0, 0, s_hot2)
                with dve.Fori(0, EC // RING) as g:
                    for half in range(2):
                        step = g * 2 + half
                        for q in range(HALF):
                            k = half * HALF + q
                            column = g * RING + k
                            make(column + 1, (k + 1) % RING, s_hot2)
                            for o in range(2):
                                a = dve.snap(column + o * (EC + 1))
                                dve.wait_ge(s_rank, column * 2 + (o + 1))
                                dve.scalar_tensor_tensor(junk[0:EP, o, :], c.iota[0:EP, :], flat(bucket)[:, bass.ds(a, 1)],
                                                         rank[o][0:EP, :], ALU.is_equal, ALU.mult,
                                                         accum_out=rank_f[:, half, o, q:q + 1]).then_inc(s_read, 1)
                                dve.wait_ge(s_read, column * 2 + (o + 1))
                        dve.tensor_copy(rank_i[:, half], rank_f[:, half]).then_inc(s_int, 1)
                        dve.wait_ge(s_int, step + 1)
                        dve.tensor_single_scalar(item_i[:, half], rank_i[:, half], 7, op=ALU.logical_shift_right)
                        dve.tensor_single_scalar(lane_i[:, half], rank_i[:, half], P - 1, op=ALU.bitwise_and)\
                            .then_inc(s_split, 1)
                        dve.wait_ge(s_freed, step + 1)
                        dve.wait_ge(s_split, step + 1)
                        dve.scalar_tensor_tensor(place[:, half], lane_i[:, half], float(ITEMS), item_i[:, half],
                                                 ALU.mult, ALU.add).then_inc(s_placed, 1)

            @block.scalar
            def _(act):
                act.wait_ge(s_rec, 1)
                with act.Fori(0, EC // RING) as g:
                    for half in range(2):
                        act.wait_ge(s_freed, g * 2 + half + 1)
                        act.sem_inc(s_passed, 1)
                        column = act.snap(g * RING + half * HALF)
                        act.copy(slot_rec[:, half], rec[:, :, bass.ds(column, HALF), :]).then_inc(s_staged, 1)

            @block.tensor
            def _(pe):
                pe.wait_ge(s_keys, 2)
                for _ in range(RING):
                    for o in range(2):
                        pe.matmul(hist[o][:], c.zeros_b[0:EP, :], c.zero_row[0:EP, :], start=True, stop=True)\
                            .then_inc(s_hist, 1)
                with pe.Fori(0, EC // RING) as g:
                    for k in range(RING):
                        for o in range(2):
                            pe.wait_ge(s_hot, (g * RING + k) * 2 + (o + 1))
                            pe.matmul(hist[o][:], c.ones_b[0:EP, :], onehot[0:EP, o, k, :], start=False, stop=True,
                                      skip_group_check=True).then_inc(s_hist, 1)
                pe.wait_ge(s_start, 1)
                for o in range(2):
                    pe.matmul(rank[o][0:EP, :], c.ones[0:1, 0:EP], graphs[o].buckets["seed"][0:1, :],
                              start=True, stop=True)
                with pe.Fori(0, EC // RING) as g:
                    for k in range(RING):
                        column = g * RING + k
                        for o in range(2):
                            pe.wait_ge(s_hot2, column * 2 + (o + 1))
                            pe.matmul(rank[o][0:EP, :], c.before[0:EP, 0:EP], onehot[0:EP, o, k, :], start=False,
                                      stop=True, skip_group_check=True).then_inc(s_rank, 1)
                        for o in range(2):
                            pe.wait_ge(s_read, column * 2 + (o + 1))
                            pe.matmul(rank[o][0:EP, :], c.not_before[0:EP, 0:EP], onehot[0:EP, o, k, :], start=False,
                                      stop=True, skip_group_check=True)

            @block.gpsimd
            def _(pool):
                for g in graphs:
                    pool.memset(g.meta[:, :, KIND:], 0.0).then_inc(s_empty, 1)
                    pool.memset(g.meta[:, :, NODE], -1.0)
                    pool.memset(g.meta[:, :, OTHER].bitcast(I32), FAR).then_inc(s_empty, 1)
                pool.sem_inc(s_freed, 2)
                pool.wait_ge(s_pads, 32)
                pool.sem_inc(s_passed, 1)

                def scatter(step, half):
                    pool.wait_ge(s_staged, step + 1)
                    pool.sem_inc(s_passed, 1)
                    pool.wait_ge(s_placed, step + 1)
                    pool.sem_inc(s_passed, 1)
                    for q in range(HALF):
                        for o in range(2):
                            pool.indirect_dma_start(item_records[o][:],
                                                    bass.IndirectOffsetOnAxis(ap=place[:, half, o, q:q + 1], axis=0),
                                                    slot_rec[:, half, o, q, :], None).then_inc(s_out[half], 16)

                def free(half, lap):
                    pool.wait_ge(s_out[half], lap * out_per_half)
                    pool.sem_inc(s_freed, 1)

                scatter(0, 0)
                with pool.Fori(0, EC // RING - 1) as g:
                    scatter(g * 2 + 1, 1)
                    free(0, g + 1)
                    scatter(g * 2 + 2, 0)
                    free(1, g + 1)
                scatter(2 * (EC // RING) - 1, 1)
                for half in range(2):
                    free(half, EC // RING)


def make_items(nc, c, graphs, item_records, item_rows):
    with Phase(nc, "items") as ph:
        ints = ph.sb("ints", [P, 2, 3, ITEM_CHUNKS], I32)
        vals = ph.sb("vals", [P, 2, 4, ITEM_CHUNKS], F32)
        tile_id = ph.sb("tile_id", [P, 2, ITEM_CHUNKS], F32)
        base = ph.sb("base", [P, ITEM_CHUNKS], F32)
        end = ph.sb("end", [P, ITEM_CHUNKS], F32)
        tmp = ph.sb("tmp", [P, ITEM_CHUNKS], F32)
        tmp2 = ph.sb("tmp2", [P, ITEM_CHUNKS], F32)
        junk = ph.sb("junk", [P, TILES + 1], F32)
        gi = ph.sb("gi", [P, 2], I32)
        s_v, s_tab, s_out, s_in = ph.sem("v"), ph.sem("tab"), ph.sem("out"), ph.sem("in")
        KEEP = 3
        with nc.Block() as block:
            @block.vector
            def _(dve):
                chain = Chain(dve, s_v)
                for o in range(2):
                    b = graphs[o].buckets
                    n = TILES
                    for q in range(ITEM_CHUNKS):
                        item = c.item_id[:, q:q + 1]
                        chain.step(dve.tensor_scalar(junk[:, 0:n], b["end"][:, 0:n], item, 0.0, ALU.is_le, ALU.add,
                                                     accum_out=tile_id[:, o, q:q + 1]))
                        for what, out in (("base", base), ("end", end)):
                            chain.step(dve.scalar_tensor_tensor(junk[:, 0:n], c.iota[:, 0:n], tile_id[:, o, q:q + 1],
                                                                b[what][:, 0:n], ALU.is_equal, ALU.mult,
                                                                accum_out=out[:, q:q + 1]))
                    v = vals[:, o]
                    chain.step(dve.tensor_tensor(tmp[:], c.item_id[:], base[:], ALU.subtract))
                    chain.step(dve.tensor_scalar(v[:, KEEP, :], tmp[:], 0.0, None, ALU.not_equal))
                    chain.step(dve.tensor_scalar(v[:, LOAD, :], tile_id[:, o, :], float(TILES - 1), float(P), ALU.min, ALU.mult))
                    chain.step(dve.tensor_scalar(v[:, LAST, :], end[:], -1.0, 0.0, ALU.add, ALU.max))
                    chain.step(dve.tensor_tensor(tmp[:], end[:], c.item_id[:], ALU.subtract))
                    chain.step(dve.tensor_scalar(tmp[:], tmp[:], 1.0, None, ALU.is_equal))
                    chain.step(dve.tensor_tensor(tmp2[:], v[:, LOAD, :], c.spare[:], ALU.subtract))
                    chain.step(dve.tensor_tensor(tmp2[:], tmp2[:], tmp[:], ALU.mult))
                    chain.step(dve.tensor_tensor(v[:, STORE, :], tmp2[:], c.spare[:], ALU.add))
                    chain.step(dve.tensor_copy(ints[:, o, :, :], v[:, 0:3, :]))
                    chain.step(dve.tensor_scalar(gi[:, o:o + 1], b["end"][:, n - 1:n], float(RING - 1), None, ALU.add))
                    chain.step(dve.tensor_single_scalar(graphs[o].groups[0:1, 0:1], gi[0:1, o:o + 1], RING.bit_length() - 1,
                                                        op=ALU.logical_shift_right))
                dve.drain().then_inc(s_tab, 1)

            @block.sync
            def _(sp):
                for o in range(2):
                    sp.dma_start(graphs[o].meta[:], item_records[o].rearrange("(p i) f -> p i f", p=P)).then_inc(s_in, 16)
                sp.wait_ge(s_tab, 1)
                with nc.allow_non_contiguous_dma(reason="small tables turned once"):
                    for o in range(2):
                        rows_i, rows_f = item_rows[o]
                        for f in range(3):
                            sp.dma_start(rows_i[f].rearrange("(q p) -> p q", p=P), ints[:, o, f, :]).then_inc(s_out, 16)
                        sp.dma_start(rows_f.rearrange("(q p) -> p q", p=P), vals[:, o, KEEP, :]).then_inc(s_out, 16)
                sp.wait_ge(s_out, 128)
                for o in range(2):
                    g = graphs[o]
                    rows_i, rows_f = item_rows[o]
                    sp.dma_start(g.table[:], rows_i.rearrange("(a f) i -> a f i", a=1)).then_inc(s_in, 16)
                    sp.dma_start(g.keep[:], rows_f.partition_broadcast(P)).then_inc(s_in, 16)
                sp.wait_ge(s_in, 96)


def pass_wait(eng, s, sem, value):
    eng.wait_ge(sem, value)
    eng.sem_inc(s["passed"], 1)


def one_hot(dve, c, graph, out, item, weight, sem):
    dve.tensor_scalar(out, c.iota[:, 0:P], graph.meta[:, bass.ds(item, 1), NODE],
                      weight, ALU.is_equal, ALU.mult).then_inc(sem, 1)


def mean_layer(nc, c, graph, w, gamma, beta, eps, x_in, x_out):
    with Phase(nc, "l0") as ph:
        x = ph.sb("x", [P, RING, D], F32)
        gathered = ph.sb("gathered", [P, RING, D], F32)
        index = ph.sb("index", [P, RING, 1], I32)
        hot = ph.sb("hot", [P, 2, P], F32)
        agg_t = ph.sb("agg_t", [P, 2, D], F32)
        x_t = ph.sb("x_t", [P, 2, D], F32)
        stats = ph.sb("stats", [P, 2, 2, 6], F32)
        mv = ph.sb("mv", [P, 2, 2, 2], F32)
        sd = ph.sb("sd", [P, 2, 2], F32)
        rs = ph.sb("rs", [P, 2, 2], F32)
        scaled = ph.sb("scaled", [P, D], F32)
        shifted = ph.sb("shifted", [P, D], F32)
        summed = ph.sb("summed", [P, 2, D], F32)
        result = ph.sb("result", [P, RING, D], F32)
        ps_a = [ph.ps(f"a{k}", [P, 2 * D])[:, 0:D] for k in range(2)]
        ps_x = [ph.ps(f"x{k}", [P, 2 * D])[:, 0:D] for k in range(2)]
        ps_b = [ph.ps(f"b{k}", [P, 2 * D])[:, 0:D] for k in range(2)]
        s = ring_sems(ph, "summed")
        for k in ("g_done", "made", "a_done", "acc", "xt", "b_done", "st1", "ag1", "sd1", "rs1", "scaled", "shifted",
                  "summed", "st2", "ag2", "sd2", "rs2"):
            s[k] = ph.sem(k)
        with nc.Block() as block:
            @block.sync
            def _(sp):
                move_tiles(sp, graph, s, x, x_in, result, x_out)

            @block.gpsimd
            def _(pool):
                gather_rows(pool, graph, s, index, gathered, x_in)

            @block.vector
            def _(dve):
                def make(j, k, lap):
                    one_hot(dve, c, graph, hot[:, k % 2, :], j, graph.meta[:, bass.ds(j, 1), WEIGHT], s["made"])

                def accumulate(j, k, lap):
                    dve.wait_ge(s["a_done"], j + 1)
                    dve.scalar_tensor_tensor(agg_t[:, k % 2, :], agg_t[:, (k + 1) % 2, :],
                                             graph.keep[:, bass.ds(j, 1)], ps_a[k % 2][:, 0:D],
                                             ALU.mult, ALU.add).then_inc(s["acc"], 1)

                def inner(j, k, lap):
                    p = k % 2
                    dve.wait_ge(s["b_done"], j + 1)
                    dve.bn_stats(stats[:, p, 0, :], ps_b[p][:]).then_inc(s["st1"], 1)
                    pass_wait(dve, s, s["st1"], j + 1)
                    dve.bn_aggr(mv[:, p, 0, :], stats[:, p, 0, :]).then_inc(s["ag1"], 1)
                    dve.wait_ge(s["ag1"], j + 1)
                    dve.scalar_tensor_tensor(scaled[:], ps_b[p][:], mv[:, p, 0, 0:1], gamma[:],
                                             ALU.subtract, ALU.mult).then_inc(s["scaled"], 1)
                    dve.wait_ge(s["sd1"], j + 1)
                    dve.reciprocal(rs[:, p, 0:1], sd[:, p, 0:1]).then_inc(s["rs1"], 1)
                    dve.wait_ge(s["scaled"], j + 1)
                    dve.wait_ge(s["rs1"], j + 1)
                    dve.scalar_tensor_tensor(shifted[:], scaled[:], rs[:, p, 0:1], beta[:],
                                             ALU.mult, ALU.add).then_inc(s["shifted"], 1)
                    dve.wait_ge(s["in_x"][k], (lap + 1) * 16)
                    dve.wait_ge(s["shifted"], j + 1)
                    dve.scalar_tensor_tensor(summed[:, p, :], shifted[:], 0.0, x[:, k, :],
                                             ALU.max, ALU.add).then_inc(s["summed"], 1)
                    dve.wait_ge(s["summed"], j + 1)
                    dve.bn_stats(stats[:, p, 1, :], summed[:, p, :]).then_inc(s["st2"], 1)
                    pass_wait(dve, s, s["st2"], j + 1)
                    dve.bn_aggr(mv[:, p, 1, :], stats[:, p, 1, :]).then_inc(s["ag2"], 1)

                def outer(j, k, lap):
                    p = k % 2
                    dve.wait_ge(s["sd2"], j + 1)
                    dve.reciprocal(rs[:, p, 1:2], sd[:, p, 1:2]).then_inc(s["rs2"], 1)
                    dve.wait_ge(s["stored"][k], (lap + 1) * 16)
                    dve.wait_ge(s["rs2"], j + 1)
                    dve.tensor_scalar(result[:, k, :], summed[:, p, :], mv[:, p, 1, 0:1], rs[:, p, 1:2],
                                      ALU.subtract, ALU.mult).then_inc(s["out_ready"], 1)

                dve.memset(agg_t[:], 0.0).then_inc(s["zeroed"], 1)
                dve.memset(result[:], 0.0).then_inc(s["zeroed"], 1)
                dve.wait_ge(s["zeroed"], 2)
                groups = load_groups(dve, graph)
                make(*at(0, 0))
                make(*at(0, 1))
                accumulate(*at(0, 0))
                make(*at(0, 2))
                dve.wait_ge(s["acc"], 1)
                accumulate(*at(0, 1))
                make(*at(0, 3))
                inner(*at(0, 0))
                with dve.Fori(0, groups) as g:
                    for k in range(RING):
                        dve.wait_ge(s["acc"], g * RING + k + 2)
                        accumulate(*at(g, k + 2))
                        make(*at(g, k + 4))
                        inner(*at(g, k + 1))
                        outer(*at(g, k))

            @block.scalar
            def _(act):
                def evacuate(j, k, lap):
                    act.wait_ge(s["a_done"], j + 1)
                    act.copy(x_t[:, k % 2, :], ps_x[k % 2][:, 0:D]).then_inc(s["xt"], 1)

                def deviation(j, k, which, ready, done):
                    act.wait_ge(ready, j + 1)
                    act.activation(sd[:, k % 2, which:which + 1], mv[:, k % 2, which, 1:2], ACT.Sqrt, bias=eps[:])\
                        .then_inc(done, 1)

                groups = load_groups(act, graph)
                evacuate(*at(0, 0))
                evacuate(*at(0, 1))
                deviation(0, 0, 0, s["ag1"], s["sd1"])
                with act.Fori(0, groups) as g:
                    for k in range(RING):
                        j = g * RING + k
                        deviation(j, k, 1, s["ag2"], s["sd2"])
                        evacuate(*at(g, k + 2))
                        deviation(j + 1, k + 1, 0, s["ag1"], s["sd1"])

            @block.tensor
            def _(pe):
                def gather_sum(j, k, lap):
                    pe.wait_ge(s["in_g"][k], (lap + 1) * 16)
                    pe.wait_ge(s["made"], j + 1)
                    for f in range(2):
                        last = pe.matmul(ps_a[k % 2][:, f * P:(f + 1) * P], gathered[:, k, f * P:(f + 1) * P],
                                         hot[:, k % 2, :], start=True, stop=True)
                    last.then_inc(s["g_done"], 1)
                    pe.wait_ge(s["in_x"][k], (lap + 1) * 16)
                    for f in range(2):
                        last = pe.transpose(ps_x[k % 2][:, f * P:(f + 1) * P], x[:, k, f * P:(f + 1) * P],
                                            c.ident[:])
                    last.then_inc(s["a_done"], 1)

                def product(j, k, lap):
                    pe.wait_ge(s["acc"], j + 1)
                    pe.wait_ge(s["xt"], j + 1)
                    for i in range(4):
                        left = agg_t if i < 2 else x_t
                        last = pe.matmul(ps_b[k % 2][:], left[:, k % 2, i % 2 * P:(i % 2 + 1) * P], w[:, i, :],
                                         start=(i == 0), stop=(i == 3))
                    last.then_inc(s["b_done"], 1)

                groups = load_groups(pe, graph)
                gather_sum(*at(0, 0))
                gather_sum(*at(0, 1))
                product(*at(0, 0))
                with pe.Fori(0, groups) as g:
                    for k in range(RING):
                        gather_sum(*at(g, k + 2))
                        product(*at(g, k + 1))


class Norm:

    def __init__(self, ph, s, name):
        self.stats = ph.sb(f"{name}_stats", [P, 2, 6], F32)
        self.mv = ph.sb(f"{name}_mv", [P, 2, 2], F32)
        self.sd = ph.sb(f"{name}_sd", [P, 2], F32)
        self.rs = ph.sb(f"{name}_rs", [P, 2], F32)
        self.st, self.ag, self.dev, self.inv = (ph.sem(f"{name}_{k}") for k in ("st", "ag", "dev", "inv"))

    def moments(self, dve, s, values, j, p):
        dve.bn_stats(self.stats[:, p, :], values).then_inc(self.st, 1)
        pass_wait(dve, s, self.st, j + 1)
        dve.bn_aggr(self.mv[:, p, :], self.stats[:, p, :]).then_inc(self.ag, 1)

    def deviation(self, act, eps, j, p):
        act.wait_ge(self.ag, j + 1)
        act.activation(self.sd[:, p:p + 1], self.mv[:, p, 1:2], ACT.Sqrt, bias=eps[:]).then_inc(self.dev, 1)

    def inverse(self, dve, j, p):
        dve.wait_ge(self.dev, j + 1)
        dve.reciprocal(self.rs[:, p:p + 1], self.sd[:, p:p + 1]).then_inc(self.inv, 1)

    def apply(self, dve, out, values, p):
        return dve.tensor_scalar(out, values, self.mv[:, p, 0:1], self.rs[:, p:p + 1], ALU.subtract, ALU.mult)


def count_edges(nc, c, graph, node_rows):
    HALF = RING // 2
    with Phase(nc, "count") as ph:
        hot = ph.sb("hot", [P, RING, P], BF16)
        kind = ph.sb("kind", [P, RING, R1], BF16)
        window = ph.sb("window", [P, R1, ITEMS], F32)
        total = ph.sb("total", [P, R1, ITEMS], F32)
        names = ph.sb("names", [P, ITEM_CHUNKS, P], F16)
        row = ph.sb("row", [P, 2, RING, P], F16)
        hot_t = ph.sb("hot_t", [P, 2, RING, P], F32)
        kind2 = ph.sb("kind2", [P, 2, RING, R1], F32)
        own = ph.sb("own", [P, 2, RING, R1], F32)
        ps_c = [ph.ps(f"c{h}", [P, 2 * D])[:, 0:HALF * R1] for h in range(2)]
        ps_n = ph.ps("n", [P, 2 * D])[:, 0:P]
        ps_e = [ph.ps(f"e{h}", [P, 2 * D])[:, 0:RING * R1] for h in range(2)]
        s = {k: ph.sem(k) for k in ("made", "counted", "taken", "zeroed", "passed", "turned", "named", "named_out",
                                    "summed", "hot_t", "kind2", "looked", "own", "shared", "chain", "last")}
        row_in = [ph.sem(f"row{h}") for h in range(2)]
        with nc.Block() as block:
            @block.sync
            def _(sp):
                sp.wait_ge(s["named"], ITEM_CHUNKS)
                sp.dma_start(node_rows.rearrange("(q p) n -> p q n", p=P), names[:]).then_inc(s["named_out"], 16)
                sp.wait_ge(s["named_out"], 16)
                groups = load_groups(sp, graph)
                for h in range(2):
                    sp.dma_start(row[:, h], node_rows[h * RING:(h + 1) * RING, :].partition_broadcast(P))\
                        .then_inc(row_in[h], 16)
                with sp.Fori(0, (groups + 1) // 2) as pair:
                    for h in range(2):
                        first = sp.snap((pair + 1) * 2 * RING + h * RING, min_val=0, max_val=ITEMS - RING)
                        sp.wait_ge(s["hot_t"], pair * 2 + (h + 1))
                        sp.dma_start(row[:, h], node_rows[bass.ds(first, RING), :].partition_broadcast(P))\
                            .then_inc(row_in[h], 16)
                for h in range(2):
                    sp.wait_ge(row_in[h], ((groups + 1) // 2 + 1) * 16)
                    sp.sem_inc(s["passed"], 1)

            @block.vector
            def _(dve):
                def kinds(out, item, n):
                    return dve.tensor_tensor(out, graph.meta[:, bass.ds(item, n), KIND].unsqueeze(2).broadcast_to([P, n, R1]),
                                             c.iota[:, 0:R1].unsqueeze(1).broadcast_to([P, n, R1]), ALU.is_equal)

                def make(item, half):
                    for q in range(HALF):
                        dve.tensor_scalar(hot[:, half * HALF + q, :], c.iota16[:, 0:P],
                                          graph.meta[:, bass.ds(item + q, 1), NODE], None, ALU.is_equal)
                    kinds(kind[:, half * HALF:(half + 1) * HALF, :], item, HALF).then_inc(s["made"], 1)

                dve.memset(window[:], 0.0).then_inc(s["zeroed"], 1)
                dve.memset(graph.share[:], 1.0).then_inc(s["chain"], 1)
                groups = load_groups(dve, graph)
                make(0, 0)
                make(HALF, 1)
                with dve.Fori(0, groups) as g:
                    for half in range(2):
                        pass_wait(dve, s, s["counted"], g * 2 + half + 1)
                        make((g + 1) * RING + half * HALF, half)
                dve.wait_ge(s["taken"], groups * 2 + 2)
                dve.sem_inc(s["passed"], 1)
                dve.wait_ge(s["chain"], 1)
                for r in range(R1):
                    last = dve.tensor_tensor_scan(total[:, r, :], graph.keep[:], window[:, r, :], 0.0, ALU.mult, ALU.add)
                last.then_inc(s["summed"], 1)

                def look(j, g, h, lap):
                    dve.wait_ge(row_in[h], (lap + 1) * 16)
                    dve.sem_inc(s["passed"], 1)
                    dve.tensor_scalar(hot_t[:, h], row[:, h], c.item_id[:, 0:1], None, ALU.is_equal).then_inc(s["hot_t"], 1)
                    kinds(kind2[:, h], j, RING).then_inc(s["kind2"], 1)

                def take(j, g, h):
                    dve.wait_ge(s["looked"], g + 1)
                    dve.tensor_tensor(own[:, h], kind2[:, h], ps_e[h].rearrange("p (k r) -> p k r", r=R1), ALU.mult)\
                        .then_inc(s["own"], 1)
                    pass_wait(dve, s, s["own"], g + 1)
                    dve.tensor_reduce(graph.share[:, bass.ds(j, RING)], own[:, h], AX.X, ALU.add).then_inc(s["shared"], 1)

                look(0, 0, 0, 0)
                dve.wait_ge(s["kind2"], 1)
                with dve.Fori(0, (groups + 1) // 2) as pair:
                    for h in range(2):
                        g = pair * 2 + h
                        look((g + 1) * RING, g + 1, 1 - h, pair + h)
                        take(g * RING, g, h)
                        dve.wait_ge(s["kind2"], g + 2)
                dve.drain().then_inc(s["last"], 1)
                dve.wait_ge(s["last"], 1)
                dve.tensor_scalar(graph.share[:], graph.share[:], 1.0, None, ALU.max).then_inc(s["chain"], 1)
                dve.wait_ge(s["chain"], 2)
                dve.reciprocal(graph.share[:], graph.share[:])

            @block.scalar
            def _(act):
                for q in range(ITEM_CHUNKS):
                    act.wait_ge(s["turned"], q + 1)
                    act.copy(names[:, q, :], ps_n).then_inc(s["named"], 1)
                groups = load_groups(act, graph)
                act.wait_ge(s["zeroed"], 1)
                act.sem_inc(s["taken"], 2)
                with act.Fori(0, groups) as g:
                    for half in range(2):
                        pass_wait(act, s, s["counted"], g * 2 + half + 1)
                        act.copy(window[:, :, bass.ds(g * RING + half * HALF, HALF)],
                                 ps_c[half].rearrange("p (k r) -> p r k", r=R1)).then_inc(s["taken"], 1)

            @block.tensor
            def _(pe):
                for q in range(ITEM_CHUNKS):
                    if q:
                        pe.wait_ge(s["named"], q)
                    pe.transpose(ps_n, graph.meta[:, q * P:(q + 1) * P, NODE], c.ident[:]).then_inc(s["turned"], 1)
                groups = load_groups(pe, graph)
                with pe.Fori(0, groups) as g:
                    for half in range(2):
                        pe.wait_ge(s["made"], g * 2 + half + 1)
                        pe.wait_ge(s["taken"], g * 2 + half + 1)
                        for q in range(HALF):
                            k = half * HALF + q
                            last = pe.matmul(ps_c[half][:, q * R1:(q + 1) * R1], hot[:, k, :], kind[:, k, :],
                                             start=True, stop=True)
                        last.then_inc(s["counted"], 1)
                regs = [pe.alloc_register(f"last{k}") for k in range(RING)]
                pe.wait_ge(s["summed"], 1)
                with pe.Fori(0, (groups + 1) // 2) as pair:
                    for h in range(2):
                        g = pair * 2 + h
                        pe.load(regs, graph.table[0:1, LAST, bass.ds(g * RING, RING)])
                        pass_wait(pe, s, s["hot_t"], g + 1)
                        for k in range(RING):
                            item = pe.snap(regs[k], min_val=0, max_val=ITEMS - 1)
                            last = pe.matmul(ps_e[h][:, k * R1:(k + 1) * R1], hot_t[:, h, k, :],
                                             total[:, :, bass.ds(item, 1)].rearrange("p r k -> p (r k)"), start=True, stop=True)
                        last.then_inc(s["looked"], 1)


def relation_layer(nc, c, graph, name, root, table, bias, eps, x_in, x_out, residual=None):
    with Phase(nc, name) as ph:
        x = ph.sb("x", [P, RING, D], F32)
        res = None if residual is None else ph.sb("res", [P, RING, D], F32)
        gathered = ph.sb("gathered", [P, RING, D], F32)
        index = ph.sb("index", [P, RING, 1], I32)
        hot = ph.sb("hot", [P, 2, P], F32)
        kind = ph.sb("kind", [P, RING, K3], BF16)
        first = ph.sb("first", [P, RING], F32)
        kind_t = ph.sb("kind_t", [K3, 2, P], BF16)
        x_t = ph.sb("x_t", [P, 2, D], F32)
        part = ph.sb("part", [P, 4, D], F32)
        message = ph.sb("message", [P, 2, 2, D], F32)
        total = ph.sb("total", [P, 2, D], F32)
        biased = ph.sb("biased", [P, 4, D], F32)
        summed = ph.sb("summed", [P, 2, D], F32)
        result = ph.sb("result", [P, RING, D], F32)
        ps_x = [ph.ps(f"x{k}", [P, 2 * D])[:, 0:D] for k in range(2)]
        ps_k = ph.ps("k", [P, 4 * D], BF16)
        ps_w = ph.ps("w", [P, 4 * D])
        ps_b = [ph.ps(f"b{k}", [P, 2 * D])[:, 0:D] for k in range(2)]
        s = ring_sems(ph, "a_done", "multiplied", residual is not None)
        for k in ("made_kind", "made_hot", "a_done", "xt", "kt", "w_done", "multiplied", "message", "b_done", "total",
                  "biased"):
            s[k] = ph.sem(k)
        norm = Norm(ph, s, "norm") if residual is not None else None
        with nc.Block() as block:
            @block.sync
            def _(sp):
                move_tiles(sp, graph, s, x, x_in, result, x_out, None if residual is None else (res, residual))

            @block.gpsimd
            def _(pool):
                gather_rows(pool, graph, s, index, gathered, x_in)

            @block.vector
            def _(dve):
                def make_kind(j, k, lap):
                    dve.tensor_scalar(first[:, k:k + 1], graph.keep[:, bass.ds(j, 1)], -1.0, 1.0, ALU.mult, ALU.add)
                    dve.tensor_scalar(kind[:, k, :], c.iota_kind[:], graph.meta[:, bass.ds(j, 1), KIND], None,
                                      ALU.is_equal).then_inc(s["made_kind"], 1)

                def make_hot(j, k, lap):
                    one_hot(dve, c, graph, hot[:, k % 2, :], j, graph.share[:, bass.ds(j, 1)], s["made_hot"])

                def multiply(j, k, lap):
                    dve.wait_ge(s["in_g"][k], (lap + 1) * 16)
                    dve.wait_ge(s["w_done"], j + 1)
                    rows = gathered[:, k, :].rearrange("p (b i) -> p i b", i=4).unsqueeze(3).broadcast_to([P, 4, 64, 4])
                    dve.tensor_tensor(part[:].rearrange("p i (b o) -> p i b o", o=4), rows,
                                      ps_w[:].rearrange("p (i b o) -> p i b o", i=4, o=4), ALU.mult)\
                        .then_inc(s["multiplied"], 1)
                    dve.wait_ge(s["multiplied"], j + 1)
                    dve.tensor_tensor(message[:, k % 2, :, :], part[:, 0:2, :], part[:, 2:4, :], ALU.add)\
                        .then_inc(s["message"], 1)

                def finish(j, k, lap):
                    p = k % 2
                    dve.wait_ge(s["b_done"], j + 1)
                    dve.scalar_tensor_tensor(total[:, p, :], total[:, 1 - p, :], graph.keep[:, bass.ds(j, 1)],
                                             ps_b[p], ALU.mult, ALU.add).then_inc(s["total"], 1)
                    make_hot(*at_plus(j, k, lap, 2))
                    dve.wait_ge(s["total"], j + 1)
                    dve.tensor_tensor(biased[:, k % 4, :], total[:, p, :], bias[:], ALU.add).then_inc(s["biased"], 1)
                    if residual is not None:
                        dve.wait_ge(s["in_res"][k], (lap + 1) * 16)
                        dve.wait_ge(s["biased"], j + 1)
                        dve.tensor_tensor(summed[:, p, :], biased[:, k % 4, :], res[:, k, :], ALU.add)\
                            .then_inc(s["res_done"], 1)
                        dve.wait_ge(s["res_done"], j + 1)
                        norm.moments(dve, s, summed[:, p, :], j, p)

                def normalise(j, k, lap):
                    norm.inverse(dve, j, k % 2)
                    dve.wait_ge(s["stored"][k], (lap + 1) * 16)
                    dve.wait_ge(norm.inv, j + 1)
                    norm.apply(dve, result[:, k, :], summed[:, k % 2, :], k % 2).then_inc(s["out_ready"], 1)

                dve.memset(total[:], 0.0).then_inc(s["zeroed"], 1)
                dve.memset(result[:], 0.0).then_inc(s["zeroed"], 1)
                dve.wait_ge(s["zeroed"], 2)
                groups = load_groups(dve, graph)
                for k in range(RING):
                    make_kind(*at(0, k))
                make_hot(*at(0, 0))
                make_hot(*at(0, 1))
                multiply(*at(0, 0))
                multiply(*at(0, 1))
                finish(*at(0, 0))
                with dve.Fori(0, groups) as g:
                    for k in range(RING):
                        multiply(*at(g, k + 2))
                        finish(*at(g, k + 1))
                        if residual is not None:
                            normalise(*at(g, k))
                        make_kind(*at(g + 1, k))

            @block.scalar
            def _(act):
                def evacuate(j, k, lap):
                    act.wait_ge(s["a_done"], j + 1)
                    act.copy(kind_t[:, k % 2, :], ps_k[0:K3, 0:P]).then_inc(s["kt"], 1)
                    act.activation(x_t[:, k % 2, :], ps_x[k % 2], ACT.Copy, scale=first[:, k:k + 1])\
                        .then_inc(s["xt"], 1)

                groups = load_groups(act, graph)
                evacuate(*at(0, 0))
                evacuate(*at(0, 1))
                evacuate(*at(0, 2))
                if residual is not None:
                    norm.deviation(act, eps, 0, 0)
                with act.Fori(0, groups) as g:
                    for k in range(RING):
                        j = g * RING + k
                        evacuate(*at(g, k + 3))
                        if residual is not None:
                            norm.deviation(act, eps, j + 1, (k + 1) % 2)
                        else:
                            act.wait_ge(s["stored"][k], (g + 1) * 16)
                            act.wait_ge(s["biased"], j + 1)
                            act.activation(result[:, k, :], biased[:, k % 4, :], ACT.Relu).then_inc(s["out_ready"], 1)

            @block.tensor
            def _(pe):
                def turn(j, k, lap):
                    pe.wait_ge(s["made_kind"], j + 1)
                    pe.transpose(ps_k[0:K3, 0:P], kind[:, k, :], c.ident_b[:])
                    pe.wait_ge(s["in_x"][k], (lap + 1) * 16)
                    for f in range(2):
                        last = pe.transpose(ps_x[k % 2][:, f * P:(f + 1) * P], x[:, k, f * P:(f + 1) * P], c.ident[:])
                    last.then_inc(s["a_done"], 1)

                def blocks(j, k, lap):
                    pe.wait_ge(s["kt"], j + 1)
                    if not isinstance(j, int) or j > 0:
                        pe.wait_ge(s["multiplied"], j)
                    for h in range(2):
                        last = pe.matmul(ps_w[:, h * 2 * D:(h + 1) * 2 * D], kind_t[:, k % 2, :],
                                         table[:, h * 2 * D:(h + 1) * 2 * D], start=True, stop=True)
                    last.then_inc(s["w_done"], 1)

                def products(j, k, lap):
                    pe.wait_ge(s["made_hot"], j + 1)
                    pe.wait_ge(s["xt"], j + 1)
                    for f in range(2):
                        pe.matmul(ps_b[k % 2], x_t[:, k % 2, f * P:(f + 1) * P], root[:, f, :], start=(f == 0), stop=False)
                    pe.wait_ge(s["message"], j + 1)
                    for i in range(2):
                        last = pe.matmul(ps_b[k % 2], hot[:, k % 2, :], message[:, k % 2, i, :], start=False, stop=(i == 1))
                    last.then_inc(s["b_done"], 1)

                groups = load_groups(pe, graph)
                turn(*at(0, 0))
                blocks(*at(0, 0))
                turn(*at(0, 1))
                products(*at(0, 0))
                blocks(*at(0, 1))
                turn(*at(0, 2))
                with pe.Fori(0, groups) as g:
                    for k in range(RING):
                        products(*at(g, k + 1))
                        blocks(*at(g, k + 2))
                        turn(*at(g, k + 3))


def at_plus(j, k, lap, more):
    return j + more, (k + more) % RING, lap + (k + more) // RING


def interaction_layer(nc, c, graph, w1, w2, bias, eps, x_in, x_out):
    with Phase(nc, "l3") as ph:
        x = ph.sb("x", [P, RING, D], F32)
        gathered = ph.sb("gathered", [P, RING, D], F32)
        index = ph.sb("index", [P, RING, 1], I32)
        hot = ph.sb("hot", [P, 2, P], F32)
        agg_t = ph.sb("agg_t", [P, 2, D], F32)
        mix_t = ph.sb("mix_t", [P, 2, D], F32)
        x_t = ph.sb("x_t", [P, 2, D], F32)
        biased = ph.sb("biased", [P, 2, D], F32)
        leaky = ph.sb("leaky", [P, 2, D], F32)
        squares = ph.sb("squares", [P, D], F32)
        length = ph.sb("length", [P, 3, 2], F32)
        summed = ph.sb("summed", [P, 2, D], F32)
        result = ph.sb("result", [P, RING, D], F32)
        ps_a = [ph.ps(f"a{k}", [P, 2 * D])[:, 0:D] for k in range(2)]
        ps_x = [ph.ps(f"x{k}", [P, 2 * D])[:, 0:D] for k in range(2)]
        ps_b = [ph.ps(f"b{k}", [P, 2 * D])[:, 0:D] for k in range(2)]
        s = ring_sems(ph, "summed")
        for k in ("made", "a_done", "g_done", "acc", "xt", "mix", "b_done", "biased", "leaky", "squared", "rooted",
                  "guarded", "inverted", "summed"):
            s[k] = ph.sem(k)
        norm = Norm(ph, s, "norm")
        with nc.Block() as block:
            @block.sync
            def _(sp):
                move_tiles(sp, graph, s, x, x_in, result, x_out)

            @block.gpsimd
            def _(pool):
                gather_rows(pool, graph, s, index, gathered, x_in)

            @block.vector
            def _(dve):
                def make(j, k, lap):
                    one_hot(dve, c, graph, hot[:, k % 2, :], j, graph.meta[:, bass.ds(j, 1), WEIGHT], s["made"])

                def accumulate(j, k, lap):
                    p = k % 2
                    dve.wait_ge(s["a_done"], j + 1)
                    dve.scalar_tensor_tensor(agg_t[:, p, :], agg_t[:, 1 - p, :], graph.keep[:, bass.ds(j, 1)], ps_a[p],
                                             ALU.mult, ALU.add).then_inc(s["acc"], 1)
                    make(*at_plus(j, k, lap, 2))
                    dve.wait_ge(s["xt"], j + 1)
                    dve.wait_ge(s["acc"], j + 1)
                    dve.scalar_tensor_tensor(mix_t[:, p, :], x_t[:, p, :], 1.0, agg_t[:, p, :], ALU.add, ALU.mult)\
                        .then_inc(s["mix"], 1)

                def activate(j, k, lap):
                    p = k % 2
                    dve.wait_ge(s["b_done"], j + 1)
                    dve.tensor_tensor(biased[:, p, :], ps_b[p], bias[:], ALU.add).then_inc(s["biased"], 1)
                    dve.wait_ge(s["biased"], j + 1)
                    dve.scalar_tensor_tensor(leaky[:, p, :], biased[:, p, :], 0.2, biased[:, p, :], ALU.mult, ALU.max)\
                        .then_inc(s["leaky"], 1)

                def add(j, k, lap):
                    p = k % 2
                    dve.wait_ge(s["rooted"], j + 1)
                    dve.tensor_scalar(length[:, 1, p:p + 1], length[:, 1, p:p + 1], 1e-12, None, ALU.max)\
                        .then_inc(s["guarded"], 1)
                    dve.wait_ge(s["guarded"], j + 1)
                    dve.reciprocal(length[:, 2, p:p + 1], length[:, 1, p:p + 1]).then_inc(s["inverted"], 1)
                    dve.wait_ge(s["inverted"], j + 1)
                    dve.scalar_tensor_tensor(summed[:, p, :], leaky[:, p, :], length[:, 2, p:p + 1], x[:, k, :],
                                             ALU.mult, ALU.add).then_inc(s["summed"], 1)
                    dve.wait_ge(s["summed"], j + 1)
                    norm.moments(dve, s, summed[:, p, :], j, p)

                def normalise(j, k, lap):
                    norm.inverse(dve, j, k % 2)
                    dve.wait_ge(s["stored"][k], (lap + 1) * 16)
                    dve.wait_ge(norm.inv, j + 1)
                    norm.apply(dve, result[:, k, :], summed[:, k % 2, :], k % 2).then_inc(s["out_ready"], 1)

                dve.memset(agg_t[:], 0.0).then_inc(s["zeroed"], 1)
                dve.memset(result[:], 0.0).then_inc(s["zeroed"], 1)
                dve.wait_ge(s["zeroed"], 2)
                groups = load_groups(dve, graph)
                make(*at(0, 0))
                make(*at(0, 1))
                accumulate(*at(0, 0))
                accumulate(*at(0, 1))
                activate(*at(0, 0))
                accumulate(*at(0, 2))
                activate(*at(0, 1))
                add(*at(0, 0))
                with dve.Fori(0, groups) as g:
                    for k in range(RING):
                        accumulate(*at(g, k + 3))
                        activate(*at(g, k + 2))
                        add(*at(g, k + 1))
                        normalise(*at(g, k))

            @block.scalar
            def _(act):
                def evacuate(j, k, lap):
                    act.wait_ge(s["a_done"], j + 1)
                    act.copy(x_t[:, k % 2, :], ps_x[k % 2]).then_inc(s["xt"], 1)

                def measure(j, k, lap):
                    p = k % 2
                    act.wait_ge(s["leaky"], j + 1)
                    act.activation(squares[:], leaky[:, p, :], ACT.Square, accum_out=length[:, 0, p:p + 1])\
                        .then_inc(s["squared"], 1)
                    act.wait_ge(s["squared"], j + 1)
                    act.activation(length[:, 1, p:p + 1], length[:, 0, p:p + 1], ACT.Sqrt).then_inc(s["rooted"], 1)

                groups = load_groups(act, graph)
                evacuate(*at(0, 0))
                evacuate(*at(0, 1))
                measure(*at(0, 0))
                evacuate(*at(0, 2))
                measure(*at(0, 1))
                norm.deviation(act, eps, 0, 0)
                with act.Fori(0, groups) as g:
                    for k in range(RING):
                        evacuate(*at(g, k + 3))
                        measure(*at(g, k + 2))
                        norm.deviation(act, eps, g * RING + k + 1, (k + 1) % 2)

            @block.tensor
            def _(pe):
                def gather_sum(j, k, lap):
                    pe.wait_ge(s["in_g"][k], (lap + 1) * 16)
                    pe.wait_ge(s["made"], j + 1)
                    for f in range(2):
                        last = pe.matmul(ps_a[k % 2][:, f * P:(f + 1) * P], gathered[:, k, f * P:(f + 1) * P],
                                         hot[:, k % 2, :], start=True, stop=True)
                    last.then_inc(s["g_done"], 1)
                    pe.wait_ge(s["in_x"][k], (lap + 1) * 16)
                    for f in range(2):
                        last = pe.transpose(ps_x[k % 2][:, f * P:(f + 1) * P], x[:, k, f * P:(f + 1) * P], c.ident[:])
                    last.then_inc(s["a_done"], 1)

                def product(j, k, lap):
                    pe.wait_ge(s["acc"], j + 1)
                    pe.wait_ge(s["xt"], j + 1)
                    for i in range(2):
                        pe.matmul(ps_b[k % 2], x_t[:, k % 2, i * P:(i + 1) * P], w1[:, i, :], start=(i == 0), stop=False)
                    pe.wait_ge(s["mix"], j + 1)
                    for i in range(2):
                        last = pe.matmul(ps_b[k % 2], mix_t[:, k % 2, i * P:(i + 1) * P], w2[:, i, :], start=False,
                                         stop=(i == 1))
                    last.then_inc(s["b_done"], 1)

                groups = load_groups(pe, graph)
                gather_sum(*at(0, 0))
                gather_sum(*at(0, 1))
                product(*at(0, 0))
                gather_sum(*at(0, 2))
                product(*at(0, 1))
                with pe.Fori(0, groups) as g:
                    for k in range(RING):
                        gather_sum(*at(g, k + 3))
                        product(*at(g, k + 2))


MASK = -1e30
FLOOR = -1e29
TINY = 1e-24
LN_SCALE = 16


class InverseRoot:

    def __init__(self, ph, name):
        self.v = ph.sb(f"{name}_v", [P, 2], F32)
        self.log = ph.sb(f"{name}_log", [P, 2], F32)
        self.y = ph.sb(f"{name}_y", [P, 2], F32)
        self.a = ph.sb(f"{name}_a", [P, 2], F32)
        self.b = ph.sb(f"{name}_b", [P, 2], F32)
        self.root = ph.sb(f"{name}_root", [P, 2], F32)
        self.have_v, self.logged, self.first, self.s_a, self.s_b, self.done = (
            ph.sem(f"{name}_{k}") for k in ("have_v", "logged", "first", "s_a", "s_b", "done"))

    def guess(self, act, shift, j, p):
        act.wait_ge(self.have_v, j + 1)
        act.activation(self.log[:, p:p + 1], self.v[:, p:p + 1], ACT.Ln, scale=float(2 ** LN_SCALE)).then_inc(self.logged, 1)
        act.wait_ge(self.logged, j + 1)
        act.activation(self.y[:, p:p + 1], self.log[:, p:p + 1], ACT.Exp, scale=-0.5, bias=shift[:])\
            .then_inc(self.first, 1)

    def refine(self, dve, j, p):
        y, q = self.y[:, p:p + 1], slice(p, p + 1)
        dve.wait_ge(self.first, j + 1)
        dve.scalar_tensor_tensor(self.a[:, q], y, y, self.v[:, q], ALU.mult, ALU.mult).then_inc(self.s_a, 1)
        dve.wait_ge(self.s_a, j + 1)
        dve.tensor_scalar(self.b[:, q], self.a[:, q], -0.5, 1.5, ALU.mult, ALU.add).then_inc(self.s_b, 1)
        dve.wait_ge(self.s_b, j + 1)
        dve.tensor_tensor(self.root[:, q], self.b[:, q], y, ALU.mult).then_inc(self.done, 1)


def attention_hop(nc, c, graph, name, head_w, tail_w, shift, x_in, x_out, residual=None):
    last_hop = residual is not None
    with Phase(nc, name) as ph:
        x = ph.sb("x", [P, RING, D], F32)
        res = ph.sb("res", [P, RING, D], F32) if last_hop else None
        gathered = ph.sb("gathered", [P, RING, D + 1], F32)
        index = ph.sb("index", [P, RING, 1], I32)
        kind = ph.sb("kind", [P, RING, GROUP], F32)
        mask = ph.sb("mask", [P, RING, P], BF16)
        kind_t = ph.sb("kind_t", [GROUP, 2, P], F32)
        x_t = ph.sb("x_t", [P, 2, D], F32)
        head_t = ph.sb("head_t", [GROUP, 2, P], F32)
        tail = ph.sb("tail", [P, 2], F32)
        junk = ph.sb("junk", [P, D + 1], F32)
        diag = ph.sb("diag", [P, 2, P], F32)
        fifth = ph.sb("fifth", [P, 2, P], F32)
        minus = ph.sb("minus", [P, 2, P + 1], F32)
        small = ph.sb("small", [P, 8, 2], F32)
        minus_max = ph.sb("minus_max", [P, 2], F32)
        expo = ph.sb("expo", [P, 4, P + 1], F32)
        sums = ph.sb("sums", [P, 4], F32)
        expo_t = ph.sb("expo_t", [P, 2, P], F32)
        scale_old = ph.sb("scale_old", [P, 2], F32)
        denom = ph.sb("denom", [P, 2], F32)
        agg = ph.sb("agg", [P, 2, D], F32)
        y = ph.sb("y", [P, 2, D], F32)
        squares = ph.sb("squares", [P, D], F32)
        total_sq = ph.sb("total_sq", [P, 2], F32)
        summed = ph.sb("summed", [P, 2, D], F32) if last_hop else None
        result = ph.sb("result", [P, RING, D], F32)
        restart = ph.sb("restart", [P, ITEMS], F32)
        ps_x = ph.ps("x", [P, 2 * D])
        ps_k = ph.ps("k", [P, 2 * D])
        ps_h = ph.ps("h", [P, 2 * D])
        ps_w = ph.ps("w", [P, 2 * D])
        ps_e = ph.ps("e", [P, 2 * D])
        ps_t = ph.ps("t", [P, 2 * D])
        ps_g = ph.ps("g", [P, 2 * D])
        s = ring_sems(ph, "y", "agg_done", last_hop)
        for k in ("made", "turned", "kt", "xt", "hw_done", "ht", "tail", "diag", "e_done", "fifth", "minus", "mx", "lk",
                  "old", "mm", "expo", "t_done", "expo_t", "agg_done", "c1", "c2", "den", "agg", "dmax", "rden", "y",
                  "squared"):
            s[k] = ph.sem(k)
        inv = InverseRoot(ph, "inv")
        if last_hop:
            s["summed"] = ph.sem("summed")
            norm, inv2 = Norm(ph, s, "norm"), InverseRoot(ph, "inv2")
        with nc.Block() as block:
            @block.sync
            def _(sp):
                move_tiles(sp, graph, s, x, x_in, result, x_out, (res, residual) if last_hop else None)

            @block.gpsimd
            def _(pool):
                gather_rows(pool, graph, s, index, gathered, x_in)

            @block.vector
            def _(dve):
                def make(j, k, lap):
                    dve.tensor_scalar(kind[:, k, :], c.iota[:, 0:GROUP], graph.meta[:, bass.ds(j, 1), KIND], None,
                                      ALU.is_equal)
                    dve.tensor_scalar(mask[:, k, :], c.iota[:, 0:P], graph.meta[:, bass.ds(j, 1), NODE], MASK,
                                      ALU.not_equal, ALU.mult).then_inc(s["made"], 1)

                def score(j, k, lap):
                    p = k % 2
                    dve.wait_ge(s["hw_done"], j + 1)
                    dve.tensor_tensor_reduce(out=junk[:], in0=gathered[:, k, :], in1=ps_w[:, 0:D + 1], scale=1.0,
                                             scalar=0.0, op0=ALU.mult, op1=ALU.add, accum_out=tail[:, p:p + 1])\
                        .then_inc(s["tail"], 1)
                    dve.wait_ge(s["tail"], j + 1)
                    dve.tensor_scalar(diag[:, p, :], c.ident[:], tail[:, p:p + 1], None, ALU.mult).then_inc(s["diag"], 1)

                def maximum(j, k, lap):
                    p = k % 2
                    q = slice(p, p + 1)
                    old = minus[:, p, P:P + 1]
                    dve.scalar_tensor_tensor(old, minus_max[:, 1 - p:2 - p], graph.keep[:, bass.ds(j, 1)],
                                             restart[:, bass.ds(j, 1)], ALU.mult, ALU.add).then_inc(s["old"], 1)
                    dve.wait_ge(s["fifth"], j + 1)
                    dve.tensor_reduce(small[:, 0, q], ps_e[:, 0:P], AX.X, ALU.max).then_inc(s["mx"], 1)
                    dve.scalar_tensor_tensor(minus[:, p, 0:P], ps_e[:, 0:P], -1.0, fifth[:, p, :], ALU.mult, ALU.min)\
                        .then_inc(s["minus"], 1)
                    dve.wait_ge(s["mx"], j + 1)
                    dve.scalar_tensor_tensor(small[:, 1, q], small[:, 0, q], 0.2, small[:, 0, q], ALU.mult, ALU.max)\
                        .then_inc(s["lk"], 1)
                    dve.wait_ge(s["lk"], j + 1)
                    dve.wait_ge(s["old"], j + 1)
                    dve.scalar_tensor_tensor(minus_max[:, q], small[:, 1, q], -1.0, old, ALU.mult, ALU.min)\
                        .then_inc(s["mm"], 1)

                def combine(j, k, lap):
                    p = k % 2
                    q = slice(p, p + 1)
                    corr = expo[:, k % 4, P:P + 1]
                    dve.wait_ge(s["expo"], j + 1)
                    dve.tensor_scalar(scale_old[:, q], corr, graph.keep[:, bass.ds(j, 1)], None, ALU.mult)\
                        .then_inc(s["c1"], 1)
                    dve.tensor_tensor(small[:, 2, q], sums[:, k % 4:k % 4 + 1], corr, ALU.subtract).then_inc(s["c2"], 1)
                    dve.wait_ge(s["c1"], j + 1)
                    dve.wait_ge(s["c2"], j + 1)
                    dve.scalar_tensor_tensor(denom[:, q], denom[:, 1 - p:2 - p], scale_old[:, q], small[:, 2, q],
                                             ALU.mult, ALU.add).then_inc(s["den"], 1)
                    dve.wait_ge(s["agg_done"], j + 1)
                    dve.scalar_tensor_tensor(agg[:, p, :], agg[:, 1 - p, :], scale_old[:, q], ps_g[:, 0:D],
                                             ALU.mult, ALU.add).then_inc(s["agg"], 1)
                    dve.wait_ge(s["den"], j + 1)
                    dve.tensor_scalar(small[:, 3, q], denom[:, q], 1e-30, None, ALU.max).then_inc(s["dmax"], 1)
                    dve.wait_ge(s["dmax"], j + 1)
                    dve.reciprocal(small[:, 4, q], small[:, 3, q]).then_inc(s["rden"], 1)
                    dve.wait_ge(s["rden"], j + 1)
                    dve.wait_ge(s["agg"], j + 1)
                    dve.scalar_tensor_tensor(y[:, p, :], agg[:, p, :], small[:, 4, q], x[:, k, :], ALU.mult, ALU.add)\
                        .then_inc(s["y"], 1)
                    dve.wait_ge(s["squared"], j + 1)
                    dve.tensor_scalar(inv.v[:, q], total_sq[:, q], TINY, None, ALU.max).then_inc(inv.have_v, 1)

                def scale_rows(j, k, lap):
                    p = k % 2
                    inv.refine(dve, j, p)
                    if not last_hop:
                        dve.wait_ge(s["stored"][k], (lap + 1) * 16)
                        dve.wait_ge(inv.done, j + 1)
                        dve.tensor_scalar(result[:, k, :], y[:, p, :], inv.root[:, p:p + 1], None, ALU.mult)\
                            .then_inc(s["out_ready"], 1)
                        return
                    dve.wait_ge(s["in_res"][k], (lap + 1) * 16)
                    dve.wait_ge(inv.done, j + 1)
                    dve.scalar_tensor_tensor(summed[:, p, :], y[:, p, :], inv.root[:, p:p + 1], res[:, k, :],
                                             ALU.mult, ALU.add).then_inc(s["res_done"], 1)
                    dve.wait_ge(s["res_done"], j + 1)
                    norm.moments(dve, s, summed[:, p, :], j, p)
                    dve.wait_ge(norm.ag, j + 1)
                    dve.tensor_scalar(inv2.v[:, p:p + 1], norm.mv[:, p, 1:2], EPS, None, ALU.add).then_inc(inv2.have_v, 1)

                def normalise(j, k, lap):
                    p = k % 2
                    inv2.refine(dve, j, p)
                    dve.wait_ge(s["stored"][k], (lap + 1) * 16)
                    dve.wait_ge(inv2.done, j + 1)
                    dve.tensor_scalar(result[:, k, :], summed[:, p, :], norm.mv[:, p, 0:1], inv2.root[:, p:p + 1],
                                      ALU.subtract, ALU.mult).then_inc(s["out_ready"], 1)

                def transposed(j, k, lap):
                    dve.wait_ge(s["t_done"], j + 1)
                    dve.tensor_copy(expo_t[:, k % 2, :], ps_t[:, 0:P]).then_inc(s["expo_t"], 1)

                for t in (agg, denom, minus_max):
                    dve.memset(t[:], 0.0)
                dve.tensor_scalar(restart[:], graph.keep[:], FLOOR, -FLOOR, ALU.mult, ALU.add).then_inc(s["zeroed"], 1)
                dve.memset(result[:], 0.0).then_inc(s["zeroed"], 1)
                dve.wait_ge(s["zeroed"], 2)
                groups = load_groups(dve, graph)
                for k in range(RING):
                    make(*at(0, k))
                for n in range(-5, 0):
                    for step, ahead in ((maximum, 4), (score, 5), (combine, 2), (scale_rows, 1), (transposed, 3)):
                        if n + ahead >= 0:
                            step(*at(0, n + ahead))
                with dve.Fori(0, groups) as g:
                    for k in range(RING):
                        maximum(*at(g, k + 4))
                        score(*at(g, k + 5))
                        combine(*at(g, k + 2))
                        scale_rows(*at(g, k + 1))
                        if last_hop:
                            normalise(*at(g, k))
                        transposed(*at(g, k + 3))
                        make(*at(g + 1, k))

            @block.scalar
            def _(act):
                def leak(j, k, lap):
                    act.wait_ge(s["e_done"], j + 1)
                    act.activation(fifth[:, k % 2, :], ps_e[:, 0:P], ACT.Copy, scale=-0.2).then_inc(s["fifth"], 1)

                def heads(j, k, lap):
                    act.wait_ge(s["hw_done"], j + 1)
                    act.copy(head_t[0:R2, k % 2, :], ps_h[0:R2, 0:P]).then_inc(s["ht"], 1)

                def evacuate(j, k, lap):
                    act.wait_ge(s["turned"], j + 1)
                    act.copy(x_t[:, k % 2, :], ps_x[:, 0:D]).then_inc(s["xt"], 1)
                    act.copy(kind_t[:, k % 2, :], ps_k[0:GROUP, 0:P]).then_inc(s["kt"], 1)

                def exponentials(j, k, lap):
                    act.wait_ge(s["minus"], j + 1)
                    act.wait_ge(s["mm"], j + 1)
                    act.activation(expo[:, k % 4, :], minus[:, k % 2, :], ACT.Exp, scale=-1.0,
                                   bias=minus_max[:, k % 2:k % 2 + 1], accum_out=sums[:, k % 4:k % 4 + 1])\
                        .then_inc(s["expo"], 1)

                def measure(j, k, lap):
                    act.wait_ge(s["y"], j + 1)
                    act.activation(squares[:], y[:, k % 2, :], ACT.Square, accum_out=total_sq[:, k % 2:k % 2 + 1])\
                        .then_inc(s["squared"], 1)
                    inv.guess(act, shift, j, k % 2)

                def outer(j, k, lap):
                    inv2.guess(act, shift, j, k % 2)

                steps = [(leak, 4), (heads, 5), (evacuate, 6), (exponentials, 4), (measure, 2)]
                if last_hop:
                    steps.append((outer, 1))
                act.preload_act_table_set("natural_log_exp_and_others")
                groups = load_groups(act, graph)
                for n in range(-6, 0):
                    for step, ahead in steps:
                        if n + ahead >= 0:
                            step(*at(0, n + ahead))
                with act.Fori(0, groups) as g:
                    for k in range(RING):
                        for step, ahead in steps:
                            step(*at(g, k + ahead))

            @block.tensor
            def _(pe):
                def turn(j, k, lap):
                    pe.wait_ge(s["made"], j + 1)
                    pe.transpose(ps_k[0:GROUP, 0:P], kind[:, k, :], c.ident[:])
                    pe.wait_ge(s["in_x"][k], (lap + 1) * 16)
                    for f in range(2):
                        last = pe.transpose(ps_x[:, f * P:(f + 1) * P], x[:, k, f * P:(f + 1) * P], c.ident[:])
                    last.then_inc(s["turned"], 1)

                def project(j, k, lap):
                    p = k % 2
                    pe.wait_ge(s["kt"], j + 1)
                    pe.wait_ge(s["in_g"][k], (lap + 1) * 16)
                    pe.matmul(ps_w[:, 0:D + 1], kind_t[0:R2, p, :], tail_w[0:R2, :], start=True, stop=True)
                    pe.wait_ge(s["xt"], j + 1)
                    for f in range(2):
                        last = pe.matmul(ps_h[0:R2, 0:P], head_w[:, f, 0:R2], x_t[:, p, f * P:(f + 1) * P],
                                         start=(f == 0), stop=(f == 1))
                    last.then_inc(s["hw_done"], 1)

                def scores(j, k, lap):
                    p = k % 2
                    pe.wait_ge(s["minus"], j) if not isinstance(j, int) or j > 0 else None
                    pe.matmul(ps_e[:, 0:P], mask[:, k, :], c.ident_b[:], start=True, stop=False)
                    pe.wait_ge(s["ht"], j + 1)
                    pe.matmul(ps_e[:, 0:P], head_t[0:R2, p, :], kind_t[0:R2, p, :], start=False, stop=False)
                    pe.wait_ge(s["diag"], j + 1)
                    pe.matmul(ps_e[:, 0:P], c.ones[:], diag[:, p, :], start=False, stop=True).then_inc(s["e_done"], 1)

                def transpose(j, k, lap):
                    pe.wait_ge(s["expo"], j + 1)
                    pe.transpose(ps_t[:, 0:P], expo[:, k % 4, 0:P], c.ident[:]).then_inc(s["t_done"], 1)

                def aggregate(j, k, lap):
                    pe.wait_ge(s["expo_t"], j + 1)
                    if not isinstance(j, int) or j > 0:
                        pe.wait_ge(s["agg"], j)
                    pe.matmul(ps_g[:, 0:D], expo_t[:, k % 2, :], gathered[:, k, 0:D], start=True, stop=True)\
                        .then_inc(s["agg_done"], 1)

                steps = [(scores, 4), (project, 5), (turn, 6), (aggregate, 2), (transpose, 3)]
                groups = load_groups(pe, graph)
                for n in range(-6, 0):
                    for step, ahead in steps:
                        if n + ahead >= 0:
                            step(*at(0, n + ahead))
                with pe.Fori(0, groups) as g:
                    for k in range(RING):
                        for step, ahead in steps:
                            step(*at(g, k + ahead))


class Weights:
    def __init__(self, sb):
        self.l0 = sb("l0_w", [P, 4, D], F32)
        self.gamma, self.beta = sb("gamma", [P, D], F32), sb("beta", [P, D], F32)
        self.root = [sb(f"root{k}", [P, 2, D], F32) for k in range(2)]
        self.table = [sb(f"blocks{k}", [K3, 4 * D], BF16) for k in range(2)]
        self.bias = [sb(f"l1_bias{k}", [P, D], F32) for k in range(2)]
        self.head = sb("head_w", [P, 2, GROUP], F32)
        self.tail = sb("tail_w", [GROUP, D + 1], F32)
        self.l3 = [sb(f"l3_w{k}", [P, 2, D], F32) for k in range(2)]
        self.l3_bias = sb("l3_bias", [P, D], F32)
        self.eps = sb("eps", [P, 1], F32)
        self.shift = sb("shift", [P, 1], F32)


def load_weights(nc, c, w, a):
    with Phase(nc, "weights") as ph:
        full = [ph.sb(f"full{k}", [K3, 4 * D], F32) for k in range(2)]
        rest = [ph.sb(f"rest{k}", [K3, 4 * D], F32) for k in range(2)]
        piece = [ph.sb(f"piece{k}", [K3, 4 * D], BF16) for k in range(2)]
        fc = ph.sb("fc", [P, 2, 2 * D + 1], F32)
        rel = ph.sb("rel", [P, 2, R2], F32)
        bias2 = ph.sb("bias2", [P, D], F32)
        ps_h = ph.ps("h", [P, 2 * D])
        ps_t = ph.ps("t", [P, 2 * D])
        s_in, s_zero, s_v, s_fc = ph.sem("in"), ph.sem("zero"), ph.sem("v"), ph.sem("fc")
        with nc.Block() as block:
            @block.sync
            def _(sp):
                n = 0
                halves = "(b p) o -> p b o"
                for dst, src in ((w.l0[:], a["L0_gnn_W"].rearrange(halves, p=P)),
                                 (w.root[0][:], a["L1_gnn_root1"].rearrange(halves, p=P)),
                                 (w.root[1][:], a["L1_gnn_root2"].rearrange(halves, p=P)),
                                 (w.l3[0][:], a["L3_gnn_W1"].rearrange(halves, p=P)),
                                 (w.l3[1][:], a["L3_gnn_W2"].rearrange(halves, p=P)),
                                 (fc[:, :, 0:2 * D], a["L2_gnn_fc_w"].rearrange(halves, p=P)),
                                 (rel[:], a["L2_gnn_relation_emb"].rearrange(halves, p=P)),
                                 (w.gamma[:], a["L0_gnn_gamma"].partition_broadcast(P)),
                                 (w.beta[:], a["L0_gnn_beta"].partition_broadcast(P)),
                                 (w.bias[0][:], a["L1_gnn_bias1"].partition_broadcast(P)),
                                 (w.bias[1][:], a["L1_gnn_bias2"].partition_broadcast(P)),
                                 (w.l3_bias[:], a["L3_gnn_b1"].partition_broadcast(P)),
                                 (bias2[:], a["L3_gnn_b2"].partition_broadcast(P))):
                    sp.dma_start(dst, src).then_inc(s_in, 16)
                    n += 16
                with nc.allow_non_contiguous_dma(reason="256 values once"):
                    sp.dma_start(fc[:, :, 2 * D:], a["L2_gnn_fc_b"].rearrange("(b p o) -> p b o", p=P, o=1)).then_inc(s_in, 16)
                n += 16
                sp.wait_ge(s_zero, 1)
                for k in range(2):
                    for part in range(3):
                        sp.dma_start(full[k][part * GROUP:part * GROUP + R1, :], a[f"L1_gnn_W{k + 1}"]).then_inc(s_in, 16)
                        n += 16
                assert n == 20 * 16
                sp.wait_ge(s_in, n)

            @block.vector
            def _(dve):
                chain = Chain(dve, s_v)
                for k in range(2):
                    chain.step(dve.memset(full[k][:], 0.0))
                dve.memset(w.eps[:], EPS).then_inc(s_zero, 1)
                dve.memset(w.shift[:], float(np.log(2.0) * LN_SCALE / 2))
                dve.wait_ge(s_in, 20 * 16)
                for k in range(2):
                    source = full[k]
                    for part in range(3):
                        rows = slice(part * GROUP, (part + 1) * GROUP)
                        chain.step(dve.tensor_copy(piece[k][:], source[:]))
                        chain.step(dve.tensor_copy(w.table[k][rows, :], piece[k][rows, :]))
                        chain.step(dve.tensor_tensor(rest[k][:], source[:], piece[k][:], ALU.subtract))
                        source = rest[k]
                chain.step(dve.tensor_tensor(w.l3_bias[:], w.l3_bias[:], bias2[:], ALU.add))
                dve.wait_ge(s_fc, 1)
                for f in range(2):
                    chain.step(dve.tensor_copy(w.head[:, f, 0:R2], ps_h[:, f * GROUP:f * GROUP + R2]))
                chain.step(dve.tensor_copy(w.tail[0:R2, :], ps_t[0:R2, 0:D + 1]))

            @block.tensor
            def _(pe):
                pe.wait_ge(s_in, 20 * 16)
                for f in range(2):
                    for b in range(2):
                        pe.matmul(ps_h[:, f * GROUP:f * GROUP + R2], fc[:, b, f * P:(f + 1) * P], rel[:, b, :],
                                  start=(b == 0), stop=(b == 1))
                for b in range(2):
                    last = pe.matmul(ps_t[0:R2, 0:D + 1], rel[:, b, :], fc[:, b, D:], start=(b == 0), stop=(b == 1))
                last.then_inc(s_fc, 1)


def build(nc, a, out):
    def dram(name, shape, dt=F32):
        return nc.dram_tensor(name, shape, dt).ap()

    with ExitStack() as ctx:
        def sb(name, shape, dt):
            return ctx.enter_context(nc.sbuf_tensor(name, shape, dt))

        c, w = Constants(sb), Weights(sb)
        graphs = [Graph(sb, "by_src"), Graph(sb, "by_dst")]
        item_records = [dram(f"item_records{o}", (P * ITEMS, 4)) for o in range(2)]
        item_rows = [(dram(f"rows_i{o}", (3, ITEMS), I32), dram(f"rows_f{o}", (ITEMS,))) for o in range(2)]
        node_rows = dram("node_rows", (ITEMS, P), F16)
        x1, h, x2, z, x3 = (dram(n, (ALL_ROWS, D)) for n in ("x1", "h", "x2", "z", "x3"))
        make_constants(nc, c)
        with ExitStack() as prep:
            def sb_prep(name, shape, dt):
                return prep.enter_context(nc.sbuf_tensor(name, shape, dt))
            for g, n in zip(graphs, ("src", "dst")):
                g.prepare(sb_prep, n)
            sort_edges(nc, c, [a[n] for n in ("src", "dst", "edge_type_16", "edge_type_24", "edge_weight")],
                       graphs, item_records)
            make_items(nc, c, graphs, item_records, item_rows)
        load_weights(nc, c, w, a)
        by_src, by_dst = graphs
        count_edges(nc, c, by_dst, node_rows)
        mean_layer(nc, c, by_src, w.l0, w.gamma, w.beta, w.eps, a["x"], x1)
        relation_layer(nc, c, by_dst, "l1a", w.root[0], w.table[0], w.bias[0], w.eps, x1, h)
        relation_layer(nc, c, by_dst, "l1b", w.root[1], w.table[1], w.bias[1], w.eps, h, x2, residual=x1)
        attention_hop(nc, c, by_src, "l2a", w.head, w.tail, w.shift, x2, z)
        attention_hop(nc, c, by_src, "l2b", w.head, w.tail, w.shift, z, x3, residual=x2)
        interaction_layer(nc, c, by_dst, w.l3[0], w.l3[1], w.l3_bias, w.eps, x3, out)


def laid_out(inputs):
    a = {k: np.asarray(v) for k, v in inputs.items()}
    x = np.zeros((ALL_ROWS, D), np.float32)
    x[:N_NODES] = a["x"]
    a["x"] = x
    for k in ("L0_gnn_W", "L2_gnn_relation_emb", "L3_gnn_W1", "L3_gnn_W2"):
        a[k] = a[k].T
    for k in ("L1_gnn_W1", "L1_gnn_W2"):
        a[k] = a[k].transpose(0, 2, 1, 3).reshape(R1, 4 * D)
    return {k: np.ascontiguousarray(v) for k, v in a.items()}


def kernel(**inputs):
    import concourse.bacc as bacc
    from concourse.bass_utils import run_bass_kernel_spmd

    nc = bacc.Bacc("TRN2", target_bir_lowering=False, num_devices=1)
    arrays = {f"in_{k}": v for k, v in laid_out(inputs).items()}
    aps = {k[3:]: nc.dram_tensor(k, v.shape, mybir.dt.from_np(v.dtype), kind="ExternalInput").ap()
           for k, v in arrays.items()}
    out = nc.dram_tensor("out", (ALL_ROWS, D), F32, kind="ExternalOutput").ap()
    build(nc, aps, out)
    r = run_bass_kernel_spmd(nc, [arrays], core_ids=[0])
    return r.results[0]["out"][:N_NODES]
```

```python
from contextlib import ExitStack

import numpy as np

import concourse.bass as bass
from concourse import mybir

F32 = mybir.dt.float32
BF16 = mybir.dt.bfloat16
F16 = mybir.dt.float16
I32 = mybir.dt.int32
ALU = mybir.AluOpType
ACT = mybir.ActivationFunctionType
AX = mybir.AxisListType

P = 128
N_NODES, D, N_EDGES = 50000, 256, 25000
TILES = -(-N_NODES // P)
ROWS = TILES * P
RING = 8
ALL_ROWS = ROWS + RING * P
PAIRS = RING // 2
EP, EC = 125, 200
MAX_ITEMS = TILES + N_EDGES // P
ITEM_CHUNKS = -(-(MAX_ITEMS + 3 * RING) // P)
ITEMS = ITEM_CHUNKS * P
R1, R2 = 16, 24
GROUP = 32
K3 = 3 * GROUP
EPS = 1e-5
FAR = 1 << 20
assert EP * EC == N_EDGES and max(R1, R2) < GROUP
OTHER, NODE, KIND, WEIGHT = range(4)
LOAD, STORE, LAST = range(3)


class Graph:

    def __init__(self, sb, name):
        self.meta = sb(f"{name}_meta", [P, ITEMS, 4], F32)
        self.keep = sb(f"{name}_keep", [P, ITEMS], F32)
        self.share = sb(f"{name}_share", [P, ITEMS], F32)
        self.table = sb(f"{name}_table", [1, 3, ITEMS], I32)
        self.groups = sb(f"{name}_groups", [1, 1], I32)


    def prepare(self, sb, name):
        self.buckets = {k: sb(f"{name}_{k}", [P, TILES + 1], I32 if k.startswith("int") else F32)
                        for k in ("count", "end", "base", "seed", "int", "int2")}


class Phase:

    def __init__(self, nc, name):
        self.nc, self.name, self.sems, self.ctx = nc, name, [], ExitStack()

    def __enter__(self):
        self.ctx.__enter__()
        return self

    def sem(self, name):
        s = self.ctx.enter_context(self.nc.semaphore(f"{self.name}_{name}"))
        self.sems.append(s)
        return s

    def pool_dma_sem(self, name):
        return self.nc.alloc_semaphore(f"{self.name}_{name}")

    def sb(self, name, shape, dt):
        return self.ctx.enter_context(self.nc.sbuf_tensor(f"{self.name}_{name}", shape, dt))

    def ps(self, name, shape, dt=F32):
        return self.ctx.enter_context(self.nc.psum_tensor(f"{self.name}_ps_{name}", shape, dt))

    def __exit__(self, *error):
        if error[0] is None:
            for s in self.sems:
                self.nc.gpsimd.sem_clear(s)
            self.nc.all_engine_barrier()
        return self.ctx.__exit__(*error)


def row_of(eng, graph, field, item):
    return eng.value_load(graph.table[0:1, field, bass.ds(item, 1)], min_val=0, max_val=ALL_ROWS - P)


def load_groups(eng, graph):
    return eng.value_load(graph.groups[0:1, 0:1], min_val=1, max_val=-(-MAX_ITEMS // RING))


def move_tiles(sp, graph, s, tiles, source, result, target, later=(), lead=0):
    streams = [(tiles, source, s["in_x"], s[s["x_done"]], lead)] + list(later)
    leads = sorted({stream[4] for stream in streams})
    regs = {n: [sp.alloc_register(f"{s['name']}_row_{n}_{k}") for k in range(RING)] for n in ["store"] + leads}

    def rows_of(n, field, first_item):
        sp.load(regs[n], graph.table[0:1, field, bass.ds(first_item, RING)])
        return [sp.snap(r, min_val=0, max_val=ALL_ROWS - P) for r in regs[n]]

    def load(stream, row, slot, used=None):
        buffer, origin, loaded, done, _ = stream
        if used is not None:
            sp.wait_ge(done, used)
        sp.dma_start(buffer[:, slot, :], origin[bass.ds(row, P), :]).then_inc(loaded[slot], 16)

    sp.wait_ge(s["zeroed"], 2)
    for slot in range(RING):
        sp.dma_start(target[ROWS + slot * P:ROWS + (slot + 1) * P, :], result[:, slot, :]).then_inc(s["stored"][slot], 16)
    rows = rows_of("store", LOAD, 0)
    for k in range(RING):
        for stream in streams:
            load(stream, rows[k], k)
    groups = load_groups(sp, graph)
    for stream in streams:
        for ahead in range(0, stream[4], RING):
            rows = rows_of("store", LOAD, ahead + RING)
            for k in range(min(RING, stream[4] - ahead)):
                load(stream, rows[k], k, ahead + k + 1)
    with sp.Fori(0, groups) as g:
        rows = rows_of("store", STORE, g * RING)
        next_rows = {n: rows_of(n, LOAD, (g + 1) * RING + n) for n in leads}
        for k in range(RING):
            item = g * RING + k
            for stream in streams:
                n = stream[4]
                if n:
                    load(stream, next_rows[n][k], (k + n) % RING, item + (n + 1))
            sp.wait_ge(s["out_ready"], item + 1)
            sp.dma_start(target[bass.ds(rows[k], P), :], result[:, k, :]).then_inc(s["stored"][k], 16)
            for stream in streams:
                if not stream[4]:
                    load(stream, next_rows[0][k], k, item + 1)
    for slot in range(RING):
        sp.wait_ge(s["stored"][slot], (groups + 1) * 16)
        sp.sem_inc(s["passed"], 1)
        for stream in streams:
            sp.wait_ge(stream[2][slot], (groups + 1 + (stream[4] - slot + RING - 1) // RING) * 16)
            sp.sem_inc(s["passed"], 1)


def gather_rows(pool, graph, s, index, gathered, source, extra=0, more=None):
    limit = pool.alloc_register(f"limit_{s['name']}")
    pool.reg_mov(limit, N_NODES - 1)
    for slot in range(RING):
        pool.memset(gathered[:, slot, :], 0.0).then_inc(s["g_zeroed"], 1)
    pool.wait_ge(s["g_zeroed"], RING)
    if gathered.shape[2] > D:
        for slot in range(RING):
            pool.memset(gathered[:, slot, D:], 1.0).then_inc(s["g_zeroed"], 1)
        pool.wait_ge(s["g_zeroed"], 2 * RING)

    def gather(item, slot):
        pool.tensor_copy(index[:, slot, :], graph.meta[:, bass.ds(item, 1), OTHER].bitcast(I32))\
            .then_inc(s["index_copied"], 1)
        pool.wait_ge(s["index_copied"], item + 1)
        pool.sem_inc(s["passed"], 1)
        pool.indirect_dma_start(gathered[:, slot, 0:D], None, source[0:N_NODES, :],
                                bass.IndirectOffsetOnAxis(ap=index[:, slot, :], axis=0),
                                bounds_check=limit, oob_is_err=False).then_inc(s["in_g"][slot], 16)

    for k in range(RING):
        gather(k, k)
    groups = load_groups(pool, graph)
    if more:
        step, ahead = more
        for n in range(ahead):
            step(Pair(0, n))
    with pool.Fori(0, groups) as g:
        for k in range(RING):
            item, slot = g * RING + k, k
            pool.wait_ge(s[s["g_last"]], item + 1)
            pool.sem_inc(s["passed"], 1)
            gather(item + RING, slot)
            if more and k % 2:
                step(Pair(g, k // 2 + ahead))
    for slot in range(extra):
        pool.wait_ge(s[s["g_last"]], groups * RING + slot + 1)
        pool.sem_inc(s["passed"], 1)
        gather((groups + 1) * RING + slot, slot)
    for slot in range(RING):
        pool.wait_ge(s["in_g"][slot], (groups + 1 + (slot < extra)) * 16)
        pool.sem_inc(s["passed"], 1)


def ring_sems(ph, x_done, g_done="g_done", residual=False):
    s = {k: ph.sem(k) for k in ("zeroed", "out_ready", "passed", "g_zeroed", "index_copied")}
    s["in_x"] = [ph.sem(f"in_x{k}") for k in range(RING)]
    s["in_g"] = [ph.pool_dma_sem(f"in_g{k}") for k in range(RING)]
    s["stored"] = [ph.sem(f"stored{k}") for k in range(RING)]
    if residual:
        s["in_res"] = [ph.sem(f"in_res{k}") for k in range(RING)]
        s["res_done"] = ph.sem("res_done")
    s["name"], s["x_done"], s["g_last"] = ph.name, x_done, g_done
    return s


class Chain:

    def __init__(self, eng, sem):
        self.eng, self.sem, self.count = eng, sem, 0

    def step(self, instruction):
        self.count += 1
        instruction.then_inc(self.sem, 1)
        self.eng.wait_ge(self.sem, self.count)


class Constants:
    def __init__(self, sb):
        self.iota16 = sb("iota16", [P, TILES + 1], F16)
        self.iota = sb("iota", [P, TILES + 1], F32)
        self.iota_kind = sb("iota_kind", [P, K3], F16)
        self.item_id = sb("item_id", [P, ITEM_CHUNKS], F32)
        self.spare_i = sb("spare_i", [P, ITEM_CHUNKS], I32)
        self.spare = sb("spare", [P, ITEM_CHUNKS], F32)
        self.ones_row = sb("ones_row", [P, TILES + 1], F32)
        self.zero_row = sb("zero_row", [P, TILES + 1], BF16)
        self.ones = sb("ones", [P, P], F32)
        self.ones_b = sb("ones_b", [P, P], BF16)
        self.zeros_b = sb("zeros_b", [P, P], BF16)
        self.ident = sb("ident", [P, P], F32)
        self.ident_b = sb("ident_b", [P, P], BF16)
        self.before = sb("before", [P, P], BF16)
        self.not_before = sb("not_before", [P, P], BF16)


def make_constants(nc, c):
    with Phase(nc, "const") as ph:
        made, numbered, spared = ph.sem("made"), ph.sem("numbered"), ph.sem("spared")
        with nc.Block() as block:
            @block.vector
            def _(dve):
                chain = Chain(dve, spared)
                dve.wait_ge(numbered, 1)
                chain.step(dve.tensor_single_scalar(c.spare_i[:], c.spare_i[:], RING - 1, op=ALU.bitwise_and))
                chain.step(dve.tensor_scalar(c.spare[:], c.spare_i[:], float(P), float(ROWS), ALU.mult, ALU.add))

            @block.gpsimd
            def _(pool):
                chain = Chain(pool, made)
                loose = dict(allow_small_or_imprecise_dtypes=True, channel_multiplier=0)
                pool.iota(c.iota16[:], [[1, TILES + 1]], 0, **loose)
                pool.iota(c.iota[:], [[1, TILES + 1]], 0, **loose)
                pool.iota(c.iota_kind[:], [[0, 3], [1, GROUP]], 0, **loose)
                pool.iota(c.item_id[:], [[P, ITEM_CHUNKS]], 0, channel_multiplier=1,
                          allow_small_or_imprecise_dtypes=True)
                chain.step(pool.iota(c.spare_i[:], [[P, ITEM_CHUNKS]], 0, channel_multiplier=1))
                pool.sem_inc(numbered, 1)
                for t in (c.ident, c.ident_b, c.before, c.zeros_b, c.zero_row):
                    chain.step(pool.memset(t[:], 0.0))
                for t in (c.ones, c.ones_b, c.not_before, c.ones_row):
                    chain.step(pool.memset(t[:], 1.0))
                for t in (c.ident, c.ident_b):
                    chain.step(pool.affine_select(out=t[:], in_=t[:], compare_op=ALU.not_equal, fill=1.0, base=0,
                                                  pattern=[[-1, P]], channel_multiplier=1))
                chain.step(pool.affine_select(out=c.before[:], in_=c.before[:], compare_op=ALU.is_ge, fill=1.0,
                                              base=0, pattern=[[-1, P]], channel_multiplier=1))
                chain.step(pool.affine_select(out=c.not_before[:], in_=c.not_before[:], compare_op=ALU.is_ge,
                                              fill=0.0, base=0, pattern=[[-1, P]], channel_multiplier=1))


def sort_edges(nc, c, arrays, graphs, item_records):
    src, dst, kind16, kind24, weight = arrays
    HALF = RING // 2
    with Phase(nc, "sort") as ph:
        raw = ph.sb("raw", [EP, 4, EC], I32)
        wt = ph.sb("wt", [EP, EC], F32)
        rec = ph.sb("rec", [EP, 2, EC, 4], F32)
        bucket_i = ph.sb("bucket_i", [EP, 2, EC], I32)
        local_i = ph.sb("local_i", [EP, 2, EC], I32)
        bucket = ph.sb("bucket", [EP, 2, EC + 1], F32)
        rank_f = ph.sb("rank_f", [EP, 2, 2, HALF], F32)
        rank_i = ph.sb("rank_i", [EP, 2, 2, HALF], I32)
        item_i = ph.sb("item_i", [EP, 2, 2, HALF], I32)
        lane_i = ph.sb("lane_i", [EP, 2, 2, HALF], I32)
        place = ph.sb("place", [EP, 2, 2, HALF], I32)
        onehot = ph.sb("onehot", [P, 2, RING, TILES + 1], BF16)
        junk = ph.sb("junk", [P, 2, TILES + 1], F32)
        slot_rec = ph.sb("slot_rec", [EP, 2, 2, HALF, 4], F32)
        hist = [ph.ps(f"hist{o}", [P, TILES + 1]) for o in range(2)]
        rank = [ph.ps(f"rank{o}", [P, TILES + 1]) for o in range(2)]
        s_in, s_dve, s_keys = ph.sem("in"), ph.sem("dve"), ph.sem("keys")
        s_hot, s_hist, s_start = ph.sem("hot"), ph.sem("hist"), ph.sem("start")
        s_hot2, s_rank, s_read, s_empty = ph.sem("hot2"), ph.sem("rank"), ph.sem("read"), ph.sem("empty")
        s_int, s_split, s_placed = ph.sem("int"), ph.sem("split"), ph.sem("placed")
        s_staged, s_freed, s_passed, s_rec, s_pads = (ph.sem(n) for n in ("staged", "freed", "passed", "rec", "pads"))
        s_out = [ph.pool_dma_sem(f"out{h}") for h in range(2)]
        out_per_half = 2 * HALF * 16

        def flat(t):
            return t[:].rearrange("p o c -> p (o c)")

        with nc.Block() as block:
            @block.sync
            def _(sp):
                for k, a in enumerate((src, dst, kind16, kind24)):
                    sp.dma_start(raw[:, k, :], a.rearrange("(p c) -> p c", p=EP)).then_inc(s_in, 16)
                sp.dma_start(wt[:], weight.rearrange("(p c) -> p c", p=EP)).then_inc(s_in, 16)
                sp.wait_ge(s_empty, 4)
                for o in range(2):
                    sp.dma_start(item_records[o].rearrange("(p i) f -> p i f", p=P), graphs[o].meta[:])\
                        .then_inc(s_pads, 16)
                sp.wait_ge(s_pads, 32)

            @block.vector
            def _(dve):
                chain = Chain(dve, s_dve)
                dve.memset(bucket[:, :, EC:], 0.0)
                dve.wait_ge(s_in, 80)
                for o in range(2):
                    chain.step(dve.tensor_single_scalar(bucket_i[:, o, :], raw[:, o, :], 7, op=ALU.logical_shift_right))
                    dve.tensor_copy(bucket[:, o, 0:EC], bucket_i[:, o, :]).then_inc(s_keys, 1)
                    chain.step(dve.tensor_single_scalar(local_i[:, o, :], raw[:, o, :], P - 1, op=ALU.bitwise_and))
                    dve.tensor_copy(rec[:, o, :, OTHER].bitcast(I32), raw[:, 1 - o, :])
                    dve.tensor_copy(rec[:, o, :, NODE], local_i[:, o, :])
                dve.tensor_copy(rec[:, 1, :, KIND], raw[:, 2, :])
                dve.tensor_copy(rec[:, 0, :, KIND], raw[:, 3, :])
                for o in range(2):
                    chain.step(dve.tensor_copy(rec[:, o, :, WEIGHT], wt[:]))
                dve.drain().then_inc(s_rec, 1)
                dve.wait_ge(s_keys, 2)

                def make(column, k, sem):
                    for o in range(2):
                        a = dve.snap(column + o * (EC + 1)) if not isinstance(column, int) else column + o * (EC + 1)
                        dve.tensor_scalar(onehot[0:EP, o, k, :], c.iota16[0:EP, :], flat(bucket)[:, bass.ds(a, 1)], None,
                                          ALU.is_equal).then_inc(sem, 1)

                with dve.Fori(0, EC // RING) as g:
                    for k in range(RING):
                        dve.wait_ge(s_hist, (g * RING + k) * 2 + 2)
                        make(g * RING + k, k, s_hot)
                dve.wait_ge(s_hist, 2 * (EC + RING))
                for o in range(2):
                    b = graphs[o].buckets
                    chain.step(dve.tensor_scalar(b["int"][:], hist[o][:], float(P - 1), None, ALU.add))
                    chain.step(dve.tensor_single_scalar(b["int2"][:], b["int"][:], 7, op=ALU.logical_shift_right))
                    chain.step(dve.tensor_scalar(b["count"][:], b["int2"][:], 1.0, None, ALU.max))
                    chain.step(dve.tensor_tensor_scan(b["end"][:], c.ones_row[:], b["count"][:], 0.0, ALU.mult, ALU.add))
                    chain.step(dve.tensor_tensor(b["base"][:], b["end"][:], b["count"][:], ALU.subtract))
                    chain.step(dve.tensor_scalar(b["seed"][:], b["base"][:], float(P), None, ALU.mult))
                dve.drain().then_inc(s_start, 1)

                make(0, 0, s_hot2)
                with dve.Fori(0, EC // RING) as g:
                    for half in range(2):
                        step = g * 2 + half
                        for q in range(HALF):
                            k = half * HALF + q
                            column = g * RING + k
                            make(column + 1, (k + 1) % RING, s_hot2)
                            for o in range(2):
                                a = dve.snap(column + o * (EC + 1))
                                dve.wait_ge(s_rank, column * 2 + (o + 1))
                                dve.scalar_tensor_tensor(junk[0:EP, o, :], c.iota[0:EP, :], flat(bucket)[:, bass.ds(a, 1)],
                                                         rank[o][0:EP, :], ALU.is_equal, ALU.mult,
                                                         accum_out=rank_f[:, half, o, q:q + 1]).then_inc(s_read, 1)
                                dve.wait_ge(s_read, column * 2 + (o + 1))
                        dve.tensor_copy(rank_i[:, half], rank_f[:, half]).then_inc(s_int, 1)
                        dve.wait_ge(s_int, step + 1)
                        dve.tensor_single_scalar(item_i[:, half], rank_i[:, half], 7, op=ALU.logical_shift_right)
                        dve.tensor_single_scalar(lane_i[:, half], rank_i[:, half], P - 1, op=ALU.bitwise_and)\
                            .then_inc(s_split, 1)
                        dve.wait_ge(s_freed, step + 1)
                        dve.wait_ge(s_split, step + 1)
                        dve.scalar_tensor_tensor(place[:, half], lane_i[:, half], float(ITEMS), item_i[:, half],
                                                 ALU.mult, ALU.add).then_inc(s_placed, 1)

            @block.scalar
            def _(act):
                act.wait_ge(s_rec, 1)
                with act.Fori(0, EC // RING) as g:
                    for half in range(2):
                        act.wait_ge(s_freed, g * 2 + half + 1)
                        act.sem_inc(s_passed, 1)
                        column = act.snap(g * RING + half * HALF)
                        act.copy(slot_rec[:, half], rec[:, :, bass.ds(column, HALF), :]).then_inc(s_staged, 1)

            @block.tensor
            def _(pe):
                pe.wait_ge(s_keys, 2)
                for _ in range(RING):
                    for o in range(2):
                        pe.matmul(hist[o][:], c.zeros_b[0:EP, :], c.zero_row[0:EP, :], start=True, stop=True)\
                            .then_inc(s_hist, 1)
                with pe.Fori(0, EC // RING) as g:
                    for k in range(RING):
                        for o in range(2):
                            pe.wait_ge(s_hot, (g * RING + k) * 2 + (o + 1))
                            pe.matmul(hist[o][:], c.ones_b[0:EP, :], onehot[0:EP, o, k, :], start=False, stop=True,
                                      skip_group_check=True).then_inc(s_hist, 1)
                pe.wait_ge(s_start, 1)
                for o in range(2):
                    pe.matmul(rank[o][0:EP, :], c.ones[0:1, 0:EP], graphs[o].buckets["seed"][0:1, :],
                              start=True, stop=True)
                with pe.Fori(0, EC // RING) as g:
                    for k in range(RING):
                        column = g * RING + k
                        for o in range(2):
                            pe.wait_ge(s_hot2, column * 2 + (o + 1))
                            pe.matmul(rank[o][0:EP, :], c.before[0:EP, 0:EP], onehot[0:EP, o, k, :], start=False,
                                      stop=True, skip_group_check=True).then_inc(s_rank, 1)
                        for o in range(2):
                            pe.wait_ge(s_read, column * 2 + (o + 1))
                            pe.matmul(rank[o][0:EP, :], c.not_before[0:EP, 0:EP], onehot[0:EP, o, k, :], start=False,
                                      stop=True, skip_group_check=True)

            @block.gpsimd
            def _(pool):
                for g in graphs:
                    pool.memset(g.meta[:, :, KIND:], 0.0).then_inc(s_empty, 1)
                    pool.memset(g.meta[:, :, NODE], -1.0)
                    pool.memset(g.meta[:, :, OTHER].bitcast(I32), FAR).then_inc(s_empty, 1)
                pool.sem_inc(s_freed, 2)
                pool.wait_ge(s_pads, 32)
                pool.sem_inc(s_passed, 1)

                def scatter(step, half):
                    pool.wait_ge(s_staged, step + 1)
                    pool.sem_inc(s_passed, 1)
                    pool.wait_ge(s_placed, step + 1)
                    pool.sem_inc(s_passed, 1)
                    for q in range(HALF):
                        for o in range(2):
                            pool.indirect_dma_start(item_records[o][:],
                                                    bass.IndirectOffsetOnAxis(ap=place[:, half, o, q:q + 1], axis=0),
                                                    slot_rec[:, half, o, q, :], None).then_inc(s_out[half], 16)

                def free(half, lap):
                    pool.wait_ge(s_out[half], lap * out_per_half)
                    pool.sem_inc(s_freed, 1)

                scatter(0, 0)
                with pool.Fori(0, EC // RING - 1) as g:
                    scatter(g * 2 + 1, 1)
                    free(0, g + 1)
                    scatter(g * 2 + 2, 0)
                    free(1, g + 1)
                scatter(2 * (EC // RING) - 1, 1)
                for half in range(2):
                    free(half, EC // RING)


def make_items(nc, c, graphs, item_records, item_rows):
    with Phase(nc, "items") as ph:
        ints = ph.sb("ints", [P, 2, 3, ITEM_CHUNKS], I32)
        vals = ph.sb("vals", [P, 2, 4, ITEM_CHUNKS], F32)
        tile_id = ph.sb("tile_id", [P, 2, ITEM_CHUNKS], F32)
        base = ph.sb("base", [P, ITEM_CHUNKS], F32)
        end = ph.sb("end", [P, ITEM_CHUNKS], F32)
        tmp = ph.sb("tmp", [P, ITEM_CHUNKS], F32)
        tmp2 = ph.sb("tmp2", [P, ITEM_CHUNKS], F32)
        junk = ph.sb("junk", [P, TILES + 1], F32)
        gi = ph.sb("gi", [P, 2], I32)
        s_v, s_tab, s_out, s_in = ph.sem("v"), ph.sem("tab"), ph.sem("out"), ph.sem("in")
        KEEP = 3
        with nc.Block() as block:
            @block.vector
            def _(dve):
                chain = Chain(dve, s_v)
                for o in range(2):
                    b = graphs[o].buckets
                    n = TILES
                    for q in range(ITEM_CHUNKS):
                        item = c.item_id[:, q:q + 1]
                        chain.step(dve.tensor_scalar(junk[:, 0:n], b["end"][:, 0:n], item, 0.0, ALU.is_le, ALU.add,
                                                     accum_out=tile_id[:, o, q:q + 1]))
                        for what, out in (("base", base), ("end", end)):
                            chain.step(dve.scalar_tensor_tensor(junk[:, 0:n], c.iota[:, 0:n], tile_id[:, o, q:q + 1],
                                                                b[what][:, 0:n], ALU.is_equal, ALU.mult,
                                                                accum_out=out[:, q:q + 1]))
                    v = vals[:, o]
                    chain.step(dve.tensor_tensor(tmp[:], c.item_id[:], base[:], ALU.subtract))
                    chain.step(dve.tensor_scalar(v[:, KEEP, :], tmp[:], 0.0, None, ALU.not_equal))
                    chain.step(dve.tensor_scalar(v[:, LOAD, :], tile_id[:, o, :], float(TILES - 1), float(P), ALU.min, ALU.mult))
                    chain.step(dve.tensor_scalar(v[:, LAST, :], end[:], -1.0, 0.0, ALU.add, ALU.max))
                    chain.step(dve.tensor_tensor(tmp[:], end[:], c.item_id[:], ALU.subtract))
                    chain.step(dve.tensor_scalar(tmp[:], tmp[:], 1.0, None, ALU.is_equal))
                    chain.step(dve.tensor_tensor(tmp2[:], v[:, LOAD, :], c.spare[:], ALU.subtract))
                    chain.step(dve.tensor_tensor(tmp2[:], tmp2[:], tmp[:], ALU.mult))
                    chain.step(dve.tensor_tensor(v[:, STORE, :], tmp2[:], c.spare[:], ALU.add))
                    chain.step(dve.tensor_copy(ints[:, o, :, :], v[:, 0:3, :]))
                    chain.step(dve.tensor_scalar(gi[:, o:o + 1], b["end"][:, n - 1:n], float(RING - 1), None, ALU.add))
                    chain.step(dve.tensor_single_scalar(graphs[o].groups[0:1, 0:1], gi[0:1, o:o + 1], RING.bit_length() - 1,
                                                        op=ALU.logical_shift_right))
                dve.drain().then_inc(s_tab, 1)

            @block.sync
            def _(sp):
                for o in range(2):
                    sp.dma_start(graphs[o].meta[:], item_records[o].rearrange("(p i) f -> p i f", p=P)).then_inc(s_in, 16)
                sp.wait_ge(s_tab, 1)
                with nc.allow_non_contiguous_dma(reason="small tables turned once"):
                    for o in range(2):
                        rows_i, rows_f = item_rows[o]
                        for f in range(3):
                            sp.dma_start(rows_i[f].rearrange("(q p) -> p q", p=P), ints[:, o, f, :]).then_inc(s_out, 16)
                        sp.dma_start(rows_f.rearrange("(q p) -> p q", p=P), vals[:, o, KEEP, :]).then_inc(s_out, 16)
                sp.wait_ge(s_out, 128)
                for o in range(2):
                    g = graphs[o]
                    rows_i, rows_f = item_rows[o]
                    sp.dma_start(g.table[:], rows_i.rearrange("(a f) i -> a f i", a=1)).then_inc(s_in, 16)
                    sp.dma_start(g.keep[:], rows_f.partition_broadcast(P)).then_inc(s_in, 16)
                sp.wait_ge(s_in, 96)


def pass_wait(eng, s, sem, value):
    eng.wait_ge(sem, value)
    eng.sem_inc(s["passed"], 1)


def one_hot(dve, c, graph, out, item, weight, sem):
    dve.tensor_scalar(out, c.iota[:, 0:P], graph.meta[:, bass.ds(item, 1), NODE],
                      weight, ALU.is_equal, ALU.mult).then_inc(sem, 1)


class Pair:

    def __init__(self, group, n):
        self.number = group * PAIRS + n
        self.item = group * RING + 2 * n
        self.slot = 2 * n % RING
        self.lap = group + n // PAIRS
        self.both = slice(self.slot, self.slot + 2)

    def each(self):
        return [(self.item + q, self.slot + q) for q in range(2)]

    def wait(self, eng, sem):
        eng.wait_ge(sem, self.number + 1)

    def wait_items(self, eng, sem):
        eng.wait_ge(sem, self.item + 2)


def run_pairs(eng, graph, steps):
    groups = load_groups(eng, graph)
    for n in range(-max(ahead for _, ahead in steps), 0):
        for step, ahead in steps:
            if n + ahead >= 0:
                step(Pair(0, n + ahead))
    with eng.Fori(0, groups) as g:
        for n in range(PAIRS):
            for step, ahead in steps:
                step(Pair(g, n + ahead))


class Norm:

    def __init__(self, ph, name, eps):
        self.sum, self.minus_mean, self.squares, self.sd, self.scale, self.bias = (
            ph.sb(f"{name}_{k}", [P, RING], F32) for k in ("sum", "minus_mean", "squares", "sd", "scale", "bias"))
        self.junk = ph.sb(f"{name}_junk", [P, 2, D], F32)
        self.centred, self.squared, self.rooted, self.scaled, self.shifted = (
            ph.sem(f"{name}_{k}") for k in ("centred", "squared", "rooted", "scaled", "shifted"))
        self.eps = eps

    def centre(self, dve, pair):
        dve.tensor_scalar(self.minus_mean[:, pair.both], self.sum[:, pair.both], -1.0 / D, None, ALU.mult)\
            .then_inc(self.centred, 1)

    def square(self, act, pair, values):
        pair.wait(act, self.centred)
        for _, k in pair.each():
            act.activation(self.junk[:, k % 2, :], values[:, k, :], ACT.Square, bias=self.minus_mean[:, k:k + 1],
                           accum_out=self.squares[:, k:k + 1]).then_inc(self.squared, 1)

    def spread(self, act, pair, values):
        self.square(act, pair, values)
        pair.wait_items(act, self.squared)
        act.activation(self.sd[:, pair.both], self.squares[:, pair.both], ACT.Sqrt, scale=1.0 / D, bias=self.eps[:])\
            .then_inc(self.rooted, 1)

    def invert(self, dve, pair):
        pair.wait(dve, self.rooted)
        dve.reciprocal(self.scale[:, pair.both], self.sd[:, pair.both]).then_inc(self.scaled, 1)

    def shift(self, dve, pair):
        pair.wait(dve, self.scaled)
        dve.tensor_tensor(self.bias[:, pair.both], self.minus_mean[:, pair.both], self.scale[:, pair.both], ALU.mult)\
            .then_inc(self.shifted, 1)

    def apply(self, act, s, pair, result, values, scale=None):
        pass_wait(act, s, self.shifted, pair.number + 1)
        for _, k in pair.each():
            act.wait_ge(s["stored"][k], (pair.lap + 1) * 16)
            act.activation(result[:, k, :], values[:, k, :], ACT.Identity,
                           scale=(self.scale if scale is None else scale)[:, k:k + 1], bias=self.bias[:, k:k + 1]).then_inc(s["out_ready"], 1)


def mean_layer(nc, c, graph, w, gamma, beta, eps, x_in, x_out):
    with Phase(nc, "l0") as ph:
        x, gathered, agg_t, x_t, products, scaled, shifted, summed, result = (
            ph.sb(k, [P, RING, D], F32) for k in ("x", "gathered", "agg_t", "x_t", "products", "scaled", "shifted",
                                                  "summed", "result"))
        index = ph.sb("index", [P, RING, 1], I32)
        hot = ph.sb("hot", [P, RING, P], F32)
        ps_a = [ph.ps(f"a{k}", [P, 2 * D])[:, 0:D] for k in range(2)]
        ps_x = [ph.ps(f"x{k}", [P, 2 * D])[:, 0:D] for k in range(2)]
        ps_b = [ph.ps(f"b{k}", [P, 2 * D])[:, 0:D] for k in range(4)]
        s = ring_sems(ph, "summed", "a_done")
        for k in ("turned", "made", "a_done", "acc", "xt", "b_done", "products", "scaled", "shifted", "summed"):
            s[k] = ph.sem(k)
        inner, outer = Norm(ph, "inner", eps), Norm(ph, "outer", eps)
        with nc.Block() as block:
            @block.sync
            def _(sp):
                move_tiles(sp, graph, s, x, x_in, result, x_out, lead=2)

            @block.gpsimd
            def _(pool):
                gather_rows(pool, graph, s, index, gathered, x_in, extra=2)

            @block.vector
            def _(dve):
                def make(pair):
                    for j, k in pair.each():
                        one_hot(dve, c, graph, hot[:, k, :], j, graph.meta[:, bass.ds(j, 1), WEIGHT], s["made"])

                def accumulate(pair):
                    for j, k in pair.each():
                        pass_wait(dve, s, s["a_done"], j + 1)
                        dve.wait_ge(s["acc"], j + 1)
                        dve.scalar_tensor_tensor(agg_t[:, k, :], agg_t[:, (k - 1) % RING, :],
                                                 graph.keep[:, bass.ds(j, 1)], ps_a[k % 2], ALU.mult, ALU.add)\
                            .then_inc(s["acc"], 1)
                        one_hot(dve, c, graph, hot[:, (k + 2) % RING, :], j + 2, graph.meta[:, bass.ds(j + 2, 1), WEIGHT],
                                s["made"])

                def centre_inner(pair):
                    pair.wait_items(dve, s["products"])
                    inner.centre(dve, pair)

                def combine(pair):
                    for j, k in pair.each():
                        dve.scalar_tensor_tensor(scaled[:, k, :], products[:, k, :], inner.minus_mean[:, k:k + 1],
                                                 gamma[:], ALU.add, ALU.mult).then_inc(s["scaled"], 1)
                    pair.wait(dve, inner.scaled)
                    for j, k in pair.each():
                        dve.wait_ge(s["scaled"], j + 1)
                        dve.scalar_tensor_tensor(shifted[:, k, :], scaled[:, k, :], inner.scale[:, k:k + 1], beta[:],
                                                 ALU.mult, ALU.add).then_inc(s["shifted"], 1)
                    for j, k in pair.each():
                        dve.wait_ge(s["shifted"], j + 1)
                        dve.scalar_tensor_tensor(summed[:, k, :], shifted[:, k, :], 0.0, x[:, k, :], ALU.max, ALU.add,
                                                 accum_out=outer.sum[:, k:k + 1]).then_inc(s["summed"], 1)

                def centre_outer(pair):
                    pair.wait_items(dve, s["summed"])
                    outer.centre(dve, pair)

                dve.memset(agg_t[:], 0.0).then_inc(s["zeroed"], 1)
                dve.memset(result[:], 0.0).then_inc(s["zeroed"], 1)
                dve.wait_ge(s["zeroed"], 2)
                dve.sem_inc(s["acc"], 1)
                make(Pair(0, 0))
                run_pairs(dve, graph, ((lambda p: inner.invert(dve, p), 1), (centre_inner, 2), (combine, 1),
                                       (lambda p: outer.invert(dve, p), 0), (lambda p: outer.shift(dve, p), 0),
                                       (accumulate, 5), (centre_outer, 1)))

            @block.scalar
            def _(act):
                def evacuate(pair):
                    for j, k in pair.each():
                        act.wait_ge(s["turned"], j + 1)
                        act.copy(x_t[:, k, :], ps_x[k % 2]).then_inc(s["xt"], 1)

                def take(pair):
                    for j, k in pair.each():
                        act.wait_ge(s["b_done"], j + 1)
                        act.activation(products[:, k, :], ps_b[k % 4], ACT.Identity, accum_out=inner.sum[:, k:k + 1])\
                            .then_inc(s["products"], 1)

                run_pairs(act, graph, ((lambda p: outer.spread(act, p, summed), 0),
                                       (lambda p: inner.spread(act, p, products), 2), (evacuate, 4), (take, 3),
                                       (lambda p: outer.apply(act, s, p, result, summed), 0)))

            @block.tensor
            def _(pe):
                def gather_sum(pair):
                    for j, k in pair.each():
                        pe.wait_ge(s["in_g"][k], (pair.lap + 1) * 16)
                        pe.wait_ge(s["made"], j + 1)
                        for f in range(2):
                            last = pe.matmul(ps_a[k % 2][:, f * P:(f + 1) * P], gathered[:, k, f * P:(f + 1) * P],
                                             hot[:, k, :], start=True, stop=True)
                        last.then_inc(s["a_done"], 1)

                def turn(pair):
                    for j, k in pair.each():
                        pe.wait_ge(s["in_x"][k], (pair.lap + 1) * 16)
                        for f in range(2):
                            last = pe.transpose(ps_x[k % 2][:, f * P:(f + 1) * P], x[:, k, f * P:(f + 1) * P], c.ident[:])
                        last.then_inc(s["turned"], 1)

                def product(pair):
                    for j, k in pair.each():
                        pe.wait_ge(s["acc"], j + 2)
                        pe.wait_ge(s["xt"], j + 1)
                        for i in range(4):
                            left = agg_t if i < 2 else x_t
                            last = pe.matmul(ps_b[k % 4], left[:, k, i % 2 * P:(i % 2 + 1) * P], w[:, i, :],
                                             start=(i == 0), stop=(i == 3))
                        last.then_inc(s["b_done"], 1)

                run_pairs(pe, graph, ((product, 3), (turn, 4), (gather_sum, 5)))


def count_edges(nc, c, graph, node_rows):
    HALF = RING // 2
    with Phase(nc, "count") as ph:
        hot = ph.sb("hot", [P, RING, P], BF16)
        kind = ph.sb("kind", [P, RING, R1], BF16)
        window = ph.sb("window", [P, R1, ITEMS], F32)
        total = ph.sb("total", [P, R1, ITEMS], F32)
        names = ph.sb("names", [P, ITEM_CHUNKS, P], F16)
        row = ph.sb("row", [P, 2, RING, P], F16)
        hot_t = ph.sb("hot_t", [P, 2, RING, P], F32)
        kind2 = ph.sb("kind2", [P, 2, RING, R1], F32)
        own = ph.sb("own", [P, 2, RING, R1], F32)
        ps_c = [ph.ps(f"c{h}", [P, 2 * D])[:, 0:HALF * R1] for h in range(2)]
        ps_n = ph.ps("n", [P, 2 * D])[:, 0:P]
        ps_e = [ph.ps(f"e{h}", [P, 2 * D])[:, 0:RING * R1] for h in range(2)]
        s = {k: ph.sem(k) for k in ("made", "counted", "taken", "zeroed", "passed", "turned", "named", "named_out",
                                    "summed", "hot_t", "kind2", "looked", "own", "shared", "chain", "last")}
        row_in = [ph.sem(f"row{h}") for h in range(2)]
        with nc.Block() as block:
            @block.sync
            def _(sp):
                sp.wait_ge(s["named"], ITEM_CHUNKS)
                sp.dma_start(node_rows.rearrange("(q p) n -> p q n", p=P), names[:]).then_inc(s["named_out"], 16)
                sp.wait_ge(s["named_out"], 16)
                groups = load_groups(sp, graph)
                for h in range(2):
                    sp.dma_start(row[:, h], node_rows[h * RING:(h + 1) * RING, :].partition_broadcast(P))\
                        .then_inc(row_in[h], 16)
                with sp.Fori(0, (groups + 1) // 2) as pair:
                    for h in range(2):
                        first = sp.snap((pair + 1) * 2 * RING + h * RING, min_val=0, max_val=ITEMS - RING)
                        sp.wait_ge(s["hot_t"], pair * 2 + (h + 1))
                        sp.dma_start(row[:, h], node_rows[bass.ds(first, RING), :].partition_broadcast(P))\
                            .then_inc(row_in[h], 16)
                for h in range(2):
                    sp.wait_ge(row_in[h], ((groups + 1) // 2 + 1) * 16)
                    sp.sem_inc(s["passed"], 1)

            @block.vector
            def _(dve):
                def kinds(out, item, n):
                    return dve.tensor_tensor(out, graph.meta[:, bass.ds(item, n), KIND].unsqueeze(2).broadcast_to([P, n, R1]),
                                             c.iota[:, 0:R1].unsqueeze(1).broadcast_to([P, n, R1]), ALU.is_equal)

                def make(item, half):
                    for q in range(HALF):
                        dve.tensor_scalar(hot[:, half * HALF + q, :], c.iota16[:, 0:P],
                                          graph.meta[:, bass.ds(item + q, 1), NODE], None, ALU.is_equal)
                    kinds(kind[:, half * HALF:(half + 1) * HALF, :], item, HALF).then_inc(s["made"], 1)

                dve.memset(window[:], 0.0).then_inc(s["zeroed"], 1)
                dve.memset(graph.share[:], 1.0).then_inc(s["chain"], 1)
                groups = load_groups(dve, graph)
                make(0, 0)
                make(HALF, 1)
                with dve.Fori(0, groups) as g:
                    for half in range(2):
                        pass_wait(dve, s, s["counted"], g * 2 + half + 1)
                        make((g + 1) * RING + half * HALF, half)
                dve.wait_ge(s["taken"], groups * 2 + 2)
                dve.sem_inc(s["passed"], 1)
                dve.wait_ge(s["chain"], 1)
                for r in range(R1):
                    last = dve.tensor_tensor_scan(total[:, r, :], graph.keep[:], window[:, r, :], 0.0, ALU.mult, ALU.add)
                last.then_inc(s["summed"], 1)

                def look(j, g, h, lap):
                    dve.wait_ge(row_in[h], (lap + 1) * 16)
                    dve.sem_inc(s["passed"], 1)
                    dve.tensor_scalar(hot_t[:, h], row[:, h], c.item_id[:, 0:1], None, ALU.is_equal).then_inc(s["hot_t"], 1)
                    kinds(kind2[:, h], j, RING).then_inc(s["kind2"], 1)

                def take(j, g, h):
                    dve.wait_ge(s["looked"], g + 1)
                    dve.tensor_tensor(own[:, h], kind2[:, h], ps_e[h].rearrange("p (k r) -> p k r", r=R1), ALU.mult)\
                        .then_inc(s["own"], 1)
                    pass_wait(dve, s, s["own"], g + 1)
                    dve.tensor_reduce(graph.share[:, bass.ds(j, RING)], own[:, h], AX.X, ALU.add).then_inc(s["shared"], 1)

                look(0, 0, 0, 0)
                dve.wait_ge(s["kind2"], 1)
                with dve.Fori(0, (groups + 1) // 2) as pair:
                    for h in range(2):
                        g = pair * 2 + h
                        look((g + 1) * RING, g + 1, 1 - h, pair + h)
                        take(g * RING, g, h)
                        dve.wait_ge(s["kind2"], g + 2)
                dve.drain().then_inc(s["last"], 1)
                dve.wait_ge(s["last"], 1)
                dve.tensor_scalar(graph.share[:], graph.share[:], 1.0, None, ALU.max).then_inc(s["chain"], 1)
                dve.wait_ge(s["chain"], 2)
                dve.reciprocal(graph.share[:], graph.share[:])

            @block.scalar
            def _(act):
                for q in range(ITEM_CHUNKS):
                    act.wait_ge(s["turned"], q + 1)
                    act.copy(names[:, q, :], ps_n).then_inc(s["named"], 1)
                groups = load_groups(act, graph)
                act.wait_ge(s["zeroed"], 1)
                act.sem_inc(s["taken"], 2)
                with act.Fori(0, groups) as g:
                    for half in range(2):
                        pass_wait(act, s, s["counted"], g * 2 + half + 1)
                        act.copy(window[:, :, bass.ds(g * RING + half * HALF, HALF)],
                                 ps_c[half].rearrange("p (k r) -> p r k", r=R1)).then_inc(s["taken"], 1)

            @block.tensor
            def _(pe):
                for q in range(ITEM_CHUNKS):
                    if q:
                        pe.wait_ge(s["named"], q)
                    pe.transpose(ps_n, graph.meta[:, q * P:(q + 1) * P, NODE], c.ident[:]).then_inc(s["turned"], 1)
                groups = load_groups(pe, graph)
                with pe.Fori(0, groups) as g:
                    for half in range(2):
                        pe.wait_ge(s["made"], g * 2 + half + 1)
                        pe.wait_ge(s["taken"], g * 2 + half + 1)
                        for q in range(HALF):
                            k = half * HALF + q
                            last = pe.matmul(ps_c[half][:, q * R1:(q + 1) * R1], hot[:, k, :], kind[:, k, :],
                                             start=True, stop=True)
                        last.then_inc(s["counted"], 1)
                regs = [pe.alloc_register(f"last{k}") for k in range(RING)]
                pe.wait_ge(s["summed"], 1)
                with pe.Fori(0, (groups + 1) // 2) as pair:
                    for h in range(2):
                        g = pair * 2 + h
                        pe.load(regs, graph.table[0:1, LAST, bass.ds(g * RING, RING)])
                        pass_wait(pe, s, s["hot_t"], g + 1)
                        for k in range(RING):
                            item = pe.snap(regs[k], min_val=0, max_val=ITEMS - 1)
                            last = pe.matmul(ps_e[h][:, k * R1:(k + 1) * R1], hot_t[:, h, k, :],
                                             total[:, :, bass.ds(item, 1)].rearrange("p r k -> p (r k)"), start=True, stop=True)
                        last.then_inc(s["looked"], 1)


def relation_layer(nc, c, graph, name, root, table, bias, eps, x_in, x_out, residual=None):
    with Phase(nc, name) as ph:
        x, gathered, x_t, total, biased, result = (
            ph.sb(k, [P, RING, D], F32) for k in ("x", "gathered", "x_t", "total", "biased", "result"))
        res, summed = (None, None) if residual is None else (ph.sb(k, [P, RING, D], F32) for k in ("res", "summed"))
        index = ph.sb("index", [P, RING, 1], I32)
        hot = ph.sb("hot", [P, RING, P], F32)
        kind = ph.sb("kind", [P, RING, K3], BF16)
        first = ph.sb("first", [P, RING], F32)
        kind_t = ph.sb("kind_t", [K3, RING, P], BF16)
        part = ph.sb("part", [P, 2, 4, D], F32)
        message = ph.sb("message", [P, 4, 2, D], F32)
        ps_x = ph.ps("x", [P, 2, D])
        ps_k = ph.ps("k", [P, 4 * D], BF16)
        ps_w = [ph.ps(f"w{k}", [P, 4 * D]) for k in range(2)]
        ps_b = [ph.ps(f"b{k}", [P, 2, D]) for k in range(2)]
        s = ring_sems(ph, "turned", "multiplied", residual is not None)
        for k in ("made_kind", "made_hot", "turned", "xt", "kt", "w_done", "multiplied", "message", "b_done", "total",
                  "biased", "summed"):
            s[k] = ph.sem(k)
        norm = Norm(ph, "norm", eps) if residual is not None else None
        with nc.Block() as block:
            @block.sync
            def _(sp):
                later = () if residual is None else ((res, residual, s["in_res"], s["res_done"], 4),)
                move_tiles(sp, graph, s, x, x_in, result, x_out, later, lead=6)

            @block.gpsimd
            def _(pool):
                def add_bias(pair):
                    for j, k in pair.each():
                        pool.wait_ge(s["stored"][k], (pair.lap + 1) * 16)
                        pool.sem_inc(s["passed"], 1)
                        if residual is None:
                            pool.wait_ge(s["total"], j + 2)
                            pool.sem_inc(s["passed"], 1)
                            pool.tensor_tensor(biased[:, k, :], total[:, k, :], bias[:], ALU.add).then_inc(s["biased"], 1)
                        else:
                            pool.wait_ge(s["in_res"][k], (pair.lap + 1) * 16)
                            pool.sem_inc(s["passed"], 1)
                            pool.tensor_tensor(biased[:, k, :], res[:, k, :], bias[:], ALU.add).then_inc(s["res_done"], 1)

                gather_rows(pool, graph, s, index, gathered, x_in, more=(add_bias, 0 if residual is None else 2))

            @block.vector
            def _(dve):
                def make_kind(pair):
                    dve.tensor_scalar(first[:, pair.both], graph.keep[:, bass.ds(pair.item, 2)], -1.0, 1.0, ALU.mult, ALU.add)
                    for j, k in pair.each():
                        dve.tensor_scalar(kind[:, k, :], c.iota_kind[:], graph.meta[:, bass.ds(j, 1), KIND], None,
                                          ALU.is_equal).then_inc(s["made_kind"], 1)

                def make_hot(pair):
                    for j, k in pair.each():
                        one_hot(dve, c, graph, hot[:, k, :], j, graph.share[:, bass.ds(j, 1)], s["made_hot"])

                def ready(pair):
                    if not isinstance(pair.number, int) or pair.number > 0:
                        pass_wait(dve, s, s["message"], pair.item)

                def multiply(pair, q):
                    j, k = pair.each()[q]
                    dve.wait_ge(s["in_g"][k], (pair.lap + 1) * 16)
                    dve.wait_ge(s["w_done"], j + 1)
                    rows = gathered[:, k, :].rearrange("p (b i) -> p i b", i=4).unsqueeze(3).broadcast_to([P, 4, 64, 4])
                    dve.tensor_tensor(part[:, k % 2].rearrange("p i (b o) -> p i b o", o=4), rows,
                                      ps_w[k % 2][:].rearrange("p (i b o) -> p i b o", i=4, o=4), ALU.mult)\
                        .then_inc(s["multiplied"], 1)

                def add_parts(pair):
                    for j, k in pair.each():
                        dve.wait_ge(s["multiplied"], j + 1)
                        dve.tensor_tensor(message[:, k % 4], part[:, k % 2, 0:2, :], part[:, k % 2, 2:4, :], ALU.add)\
                            .then_inc(s["message"], 1)

                def add_up(pair, q):
                    j, k = pair.each()[q]
                    if q == 0:
                        pass_wait(dve, s, s["b_done"], pair.number + 1)
                    dve.wait_ge(s["total"], j + 1)
                    dve.scalar_tensor_tensor(total[:, k, :], total[:, (k - 1) % RING, :],
                                             graph.keep[:, bass.ds(j, 1)], ps_b[k // 2 % 2][:, k % 2, :],
                                             ALU.mult, ALU.add).then_inc(s["total"], 1)

                def add_residual(pair):
                    pass_wait(dve, s, s["res_done"], pair.item + 2)
                    for j, k in pair.each():
                        dve.wait_ge(s["total"], j + 2)
                        dve.scalar_tensor_tensor(summed[:, k, :], total[:, k, :], 1.0, biased[:, k, :], ALU.mult, ALU.add,
                                                 accum_out=norm.sum[:, k:k + 1]).then_inc(s["summed"], 1)

                def centre(pair):
                    pair.wait_items(dve, s["summed"])
                    norm.centre(dve, pair)

                dve.memset(total[:], 0.0).then_inc(s["zeroed"], 1)
                dve.memset(result[:], 0.0).then_inc(s["zeroed"], 1)
                dve.wait_ge(s["zeroed"], 2)
                dve.sem_inc(s["total"], 1)
                steps = [(ready, 3), (lambda p: add_up(p, 0), 1), (lambda p: multiply(p, 0), 3), (lambda p: add_up(p, 1), 1),
                         (lambda p: multiply(p, 1), 3)]
                if residual is None:
                    steps += [(make_hot, 3), (add_parts, 3), (make_kind, 6)]
                else:
                    steps += [(add_residual, 1), (make_hot, 3), (add_parts, 3), (lambda p: norm.invert(dve, p), 0),
                              (make_kind, 6), (lambda p: norm.shift(dve, p), 0), (centre, 1)]
                run_pairs(dve, graph, steps)

            @block.scalar
            def _(act):
                def evacuate(pair):
                    pair.wait_items(act, s["turned"])
                    act.copy(kind_t[:, pair.both, :], ps_k[0:K3, 0:2 * P].rearrange("p (k n) -> p k n", n=P))\
                        .then_inc(s["kt"], 1)
                    for j, k in pair.each():
                        act.activation(x_t[:, k, :], ps_x[:, k % 2, :], ACT.Copy, scale=first[:, k:k + 1])\
                            .then_inc(s["xt"], 1)

                def relu(pair):
                    for j, k in pair.each():
                        act.wait_ge(s["stored"][k], (pair.lap + 1) * 16)
                        act.wait_ge(s["biased"], j + 1)
                        act.activation(result[:, k, :], biased[:, k, :], ACT.Relu).then_inc(s["out_ready"], 1)

                if residual is None:
                    run_pairs(act, graph, ((evacuate, 5), (relu, 0)))
                else:
                    run_pairs(act, graph, ((lambda p: norm.spread(act, p, summed), 0), (evacuate, 5),
                                           (lambda p: norm.apply(act, s, p, result, summed), 0)))

            @block.tensor
            def _(pe):
                def turn(pair):
                    if not isinstance(pair.number, int) or pair.number > 0:
                        pe.wait_ge(s["xt"], pair.item)
                    for j, k in pair.each():
                        pe.wait_ge(s["made_kind"], j + 1)
                        pe.transpose(ps_k[0:K3, k % 2 * P:(k % 2 + 1) * P], kind[:, k, :], c.ident_b[:])
                        pe.wait_ge(s["in_x"][k], (pair.lap + 1) * 16)
                        for f in range(2):
                            last = pe.transpose(ps_x[:, k % 2, f * P:(f + 1) * P], x[:, k, f * P:(f + 1) * P], c.ident[:])
                        last.then_inc(s["turned"], 1)

                def blocks(pair):
                    pair.wait(pe, s["kt"])
                    for j, k in pair.each():
                        if not isinstance(pair.number, int) or pair.number > 0:
                            pe.wait_ge(s["multiplied"], j - 1)
                        for h in range(2):
                            last = pe.matmul(ps_w[k % 2][:, h * 2 * D:(h + 1) * 2 * D], kind_t[:, k, :],
                                             table[:, h * 2 * D:(h + 1) * 2 * D], start=True, stop=True)
                        last.then_inc(s["w_done"], 1)

                def products(pair):
                    pair.wait_items(pe, s["made_hot"])
                    pair.wait_items(pe, s["message"])
                    for j, k in pair.each():
                        sums = ps_b[k // 2 % 2][:, k % 2, :]
                        for f in range(2):
                            pe.matmul(sums, x_t[:, k, f * P:(f + 1) * P], root[:, f, :], start=(f == 0), stop=False)
                        for i in range(2):
                            last = pe.matmul(sums, hot[:, k, :], message[:, k % 4, i, :], start=False, stop=(i == 1))
                    last.then_inc(s["b_done"], 1)

                run_pairs(pe, graph, ((products, 2), (turn, 5), (blocks, 4)))


def interaction_layer(nc, c, graph, w1, w2, bias, eps, x_in, x_out):
    with Phase(nc, "l3") as ph:
        x, gathered, agg_t, x_t, mix_t, biased, leaky, summed, result = (
            ph.sb(k, [P, RING, D], F32) for k in ("x", "gathered", "agg_t", "x_t", "mix_t", "biased", "leaky", "summed",
                                                  "result"))
        index = ph.sb("index", [P, RING, 1], I32)
        hot = ph.sb("hot", [P, RING, P], F32)
        squares = ph.sb("squares", [P, 2, D], F32)
        square_sum, length, guarded, inverse = (ph.sb(k, [P, RING], F32) for k in ("square_sum", "length", "guarded",
                                                                                   "inverse"))
        ps_a = [ph.ps(f"a{k}", [P, 2 * D])[:, 0:D] for k in range(2)]
        ps_x = [ph.ps(f"x{k}", [P, 2 * D])[:, 0:D] for k in range(2)]
        ps_b = [ph.ps(f"b{k}", [P, 2 * D])[:, 0:D] for k in range(4)]
        s = ring_sems(ph, "summed", "a_done")
        for k in ("made", "turned", "a_done", "acc", "xt", "mix", "b_done", "biased", "leaky", "squared", "rooted",
                  "guarded", "inverted", "summed"):
            s[k] = ph.sem(k)
        norm = Norm(ph, "norm", eps)
        with nc.Block() as block:
            @block.sync
            def _(sp):
                move_tiles(sp, graph, s, x, x_in, result, x_out, lead=2)

            @block.gpsimd
            def _(pool):
                gather_rows(pool, graph, s, index, gathered, x_in, extra=2)

            @block.vector
            def _(dve):
                def make(pair):
                    for j, k in pair.each():
                        one_hot(dve, c, graph, hot[:, k, :], j, graph.meta[:, bass.ds(j, 1), WEIGHT], s["made"])

                def accumulate(pair):
                    for j, k in pair.each():
                        pass_wait(dve, s, s["a_done"], j + 1)
                        dve.wait_ge(s["acc"], j + 1)
                        dve.scalar_tensor_tensor(agg_t[:, k, :], agg_t[:, (k - 1) % RING, :],
                                                 graph.keep[:, bass.ds(j, 1)], ps_a[k % 2], ALU.mult, ALU.add)\
                            .then_inc(s["acc"], 1)
                        one_hot(dve, c, graph, hot[:, (k + 2) % RING, :], j + 2, graph.meta[:, bass.ds(j + 2, 1), WEIGHT],
                                s["made"])

                def mix(pair):
                    pair.wait_items(dve, s["xt"])
                    for j, k in pair.each():
                        dve.wait_ge(s["acc"], j + 2)
                        dve.scalar_tensor_tensor(mix_t[:, k, :], x_t[:, k, :], 1.0, agg_t[:, k, :], ALU.add, ALU.mult)\
                            .then_inc(s["mix"], 1)

                def activate(pair):
                    for j, k in pair.each():
                        dve.wait_ge(s["b_done"], j + 1)
                        dve.tensor_tensor(biased[:, k, :], ps_b[k % 4], bias[:], ALU.add).then_inc(s["biased"], 1)
                    for j, k in pair.each():
                        dve.wait_ge(s["biased"], j + 1)
                        dve.scalar_tensor_tensor(leaky[:, k, :], biased[:, k, :], 0.2, biased[:, k, :], ALU.mult, ALU.max)\
                            .then_inc(s["leaky"], 1)

                def guard(pair):
                    pair.wait(dve, s["rooted"])
                    dve.tensor_scalar(guarded[:, pair.both], length[:, pair.both], 1e-12, None, ALU.max)\
                        .then_inc(s["guarded"], 1)

                def invert(pair):
                    pair.wait(dve, s["guarded"])
                    dve.reciprocal(inverse[:, pair.both], guarded[:, pair.both]).then_inc(s["inverted"], 1)

                def add(pair):
                    pair.wait(dve, s["inverted"])
                    for j, k in pair.each():
                        dve.scalar_tensor_tensor(summed[:, k, :], leaky[:, k, :], inverse[:, k:k + 1], x[:, k, :],
                                                 ALU.mult, ALU.add, accum_out=norm.sum[:, k:k + 1]).then_inc(s["summed"], 1)

                def centre(pair):
                    pair.wait_items(dve, s["summed"])
                    norm.centre(dve, pair)

                dve.memset(agg_t[:], 0.0).then_inc(s["zeroed"], 1)
                dve.memset(result[:], 0.0).then_inc(s["zeroed"], 1)
                dve.wait_ge(s["zeroed"], 2)
                dve.sem_inc(s["acc"], 1)
                make(Pair(0, 0))
                run_pairs(dve, graph, ((guard, 1), (mix, 3), (invert, 1), (activate, 2), (add, 1),
                                       (lambda p: norm.invert(dve, p), 0), (lambda p: norm.shift(dve, p), 0),
                                       (accumulate, 5), (centre, 1)))

            @block.scalar
            def _(act):
                def evacuate(pair):
                    for j, k in pair.each():
                        act.wait_ge(s["turned"], j + 1)
                        act.copy(x_t[:, k, :], ps_x[k % 2]).then_inc(s["xt"], 1)

                def measure(pair):
                    for j, k in pair.each():
                        act.wait_ge(s["leaky"], j + 1)
                        act.activation(squares[:, k % 2, :], leaky[:, k, :], ACT.Square, accum_out=square_sum[:, k:k + 1])\
                            .then_inc(s["squared"], 1)
                    pair.wait_items(act, s["squared"])
                    act.activation(length[:, pair.both], square_sum[:, pair.both], ACT.Sqrt).then_inc(s["rooted"], 1)

                run_pairs(act, graph, ((lambda p: norm.spread(act, p, summed), 0), (measure, 2), (evacuate, 4),
                                       (lambda p: norm.apply(act, s, p, result, summed), 0)))

            @block.tensor
            def _(pe):
                def gather_sum(pair):
                    for j, k in pair.each():
                        pe.wait_ge(s["in_g"][k], (pair.lap + 1) * 16)
                        pe.wait_ge(s["made"], j + 1)
                        for f in range(2):
                            last = pe.matmul(ps_a[k % 2][:, f * P:(f + 1) * P], gathered[:, k, f * P:(f + 1) * P],
                                             hot[:, k, :], start=True, stop=True)
                        last.then_inc(s["a_done"], 1)

                def turn(pair):
                    for j, k in pair.each():
                        pe.wait_ge(s["in_x"][k], (pair.lap + 1) * 16)
                        for f in range(2):
                            last = pe.transpose(ps_x[k % 2][:, f * P:(f + 1) * P], x[:, k, f * P:(f + 1) * P], c.ident[:])
                        last.then_inc(s["turned"], 1)

                def product(pair):
                    pair.wait_items(pe, s["xt"])
                    for j, k in pair.each():
                        for i in range(2):
                            pe.matmul(ps_b[k % 4], x_t[:, k, i * P:(i + 1) * P], w1[:, i, :], start=(i == 0), stop=False)
                    for j, k in pair.each():
                        pe.wait_ge(s["mix"], j + 1)
                        for i in range(2):
                            last = pe.matmul(ps_b[k % 4], mix_t[:, k, i * P:(i + 1) * P], w2[:, i, :], start=False,
                                             stop=(i == 1))
                        last.then_inc(s["b_done"], 1)

                run_pairs(pe, graph, ((product, 3), (turn, 4), (gather_sum, 5)))


MASK = -1e30
FLOOR = -1e29
TINY = 1e-24
LN_SCALE = 16


class InverseRoot:

    def __init__(self, ph, name):
        self.v, self.log, self.y, self.a, self.b, self.root = (
            ph.sb(f"{name}_{k}", [P, RING], F32) for k in ("v", "log", "y", "a", "b", "root"))
        self.have_v, self.logged, self.first, self.s_a, self.s_b, self.done = (
            ph.sem(f"{name}_{k}") for k in ("have_v", "logged", "first", "s_a", "s_b", "done"))

    def guess(self, act, shift, pair):
        pair.wait(act, self.have_v)
        act.activation(self.log[:, pair.both], self.v[:, pair.both], ACT.Ln, scale=float(2 ** LN_SCALE)).then_inc(self.logged, 1)
        pair.wait(act, self.logged)
        act.activation(self.y[:, pair.both], self.log[:, pair.both], ACT.Exp, scale=-0.5, bias=shift[:])\
            .then_inc(self.first, 1)

    def square(self, dve, pair):
        pair.wait(dve, self.first)
        dve.tensor_tensor(self.a[:, pair.both], self.y[:, pair.both], self.y[:, pair.both], ALU.mult).then_inc(self.s_a, 1)

    def weigh(self, dve, pair):
        pair.wait(dve, self.s_a)
        dve.scalar_tensor_tensor(self.b[:, pair.both], self.a[:, pair.both], -0.5, self.v[:, pair.both], ALU.mult, ALU.mult)\
            .then_inc(self.s_b, 1)

    def improve(self, dve, pair):
        pair.wait(dve, self.s_b)
        dve.scalar_tensor_tensor(self.root[:, pair.both], self.b[:, pair.both], 1.5, self.y[:, pair.both], ALU.add, ALU.mult)\
            .then_inc(self.done, 1)


def attention_hop(nc, c, graph, name, head_w, tail_w, shift, x_in, x_out, residual=None):
    last_hop = residual is not None
    r = 2 if last_hop else 0
    Q = 4
    with Phase(nc, name) as ph:
        x, x_again, agg, y, result = (ph.sb(k, [P, RING, D], F32) for k in ("x", "x_again", "agg", "y", "result"))
        res, summed = (ph.sb(k, [P, RING, D], F32) for k in ("res", "summed")) if last_hop else (None, None)
        gathered = ph.sb("gathered", [P, RING, D + 1], F32)
        index = ph.sb("index", [P, RING, 1], I32)
        kind = ph.sb("kind", [P, RING, GROUP], F32)
        mask = ph.sb("mask", [P, RING, P], BF16)
        kind_t = ph.sb("kind_t", [GROUP, RING, P], F32)
        x_t = ph.sb("x_t", [P, Q, D], F32)
        head_t = ph.sb("head_t", [GROUP, Q, P], F32)
        tail = ph.sb("tail", [P, RING], F32)
        junk = ph.sb("junk", [P, 2, D + 1], F32)
        diag = ph.sb("diag", [P, Q, P], F32)
        fifth = ph.sb("fifth", [P, Q, P], F32)
        minus = ph.sb("minus", [P, Q, P + 1], F32)
        top, top_leaky, minus_max, scale_old, fresh, denom, guarded, inverse, total_sq, sums = (
            ph.sb(k, [P, RING], F32) for k in ("top", "top_leaky", "minus_max", "scale_old", "fresh", "denom", "guarded",
                                               "inverse", "total_sq", "sums"))
        expo = ph.sb("expo", [P, RING, P + 1], F32)
        expo_t = ph.sb("expo_t", [P, Q, P], F32)
        squares = ph.sb("squares", [P, 2, D], F32)
        restart = ph.sb("restart", [P, ITEMS], F32)
        ps_x = ph.ps("x", [P, 2, D])
        ps_kh = ph.ps("kh", [P, 2, 2, P])
        ps_w = [ph.ps(f"w{k}", [P, 2 * D]) for k in range(2)]
        ps_e = [ph.ps(f"e{k}", [P, 4, P]) for k in range(2)]
        ps_t = ph.ps("t", [P, 4, P])
        ps_g = ph.ps("g", [P, 2, D])
        s = ring_sems(ph, "turned", "agg_done", last_hop)
        for k in ("made", "turned", "evacuated", "projected", "ht", "tail", "diag", "e_done", "fifth", "minus", "top",
                  "leaky", "old", "mm", "expo", "t_done", "expo_t", "agg_done", "c1", "c2", "den", "agg", "guarded",
                  "inverted", "y", "squared", "summed"):
            s[k] = ph.sem(k)
        in_again = [ph.sem(f"in_again{k}") for k in range(RING)]
        inv = InverseRoot(ph, "inv")
        if last_hop:
            norm, inv2 = Norm(ph, "norm", None), InverseRoot(ph, "inv2")
        with nc.Block() as block:
            @block.sync
            def _(sp):
                later = [(x_again, x_in, in_again, s["y"], 2 * r)]
                if last_hop:
                    later.append((res, residual, s["in_res"], s["summed"], 0))
                move_tiles(sp, graph, s, x, x_in, result, x_out, later, lead=10 + 2 * r)

            @block.gpsimd
            def _(pool):
                gather_rows(pool, graph, s, index, gathered, x_in, extra=2 * r + 2)

            @block.vector
            def _(dve):
                def make(j, k):
                    dve.tensor_scalar(kind[:, k, :], c.iota16[:, 0:GROUP], graph.meta[:, bass.ds(j, 1), KIND], None,
                                      ALU.is_equal)
                    dve.tensor_scalar(mask[:, k, :], c.iota16[:, 0:P], graph.meta[:, bass.ds(j, 1), NODE], MASK,
                                      ALU.not_equal, ALU.mult).then_inc(s["made"], 1)

                def score(pair):
                    pass_wait(dve, s, s["projected"], pair.number + 1)
                    for j, k in pair.each():
                        dve.wait_ge(s["in_g"][k], (pair.lap + 1) * 16)
                        dve.sem_inc(s["passed"], 1)
                        dve.tensor_tensor_reduce(out=junk[:, k % 2], in0=gathered[:, k, :], in1=ps_w[k % 2][:, 0:D + 1],
                                                 scale=1.0, scalar=0.0, op0=ALU.mult, op1=ALU.add,
                                                 accum_out=tail[:, k:k + 1]).then_inc(s["tail"], 1)

                def diagonal(pair):
                    for j, k in pair.each():
                        dve.wait_ge(s["tail"], j + 1)
                        dve.tensor_scalar(diag[:, k % Q, :], c.ident[:], tail[:, k:k + 1], None, ALU.mult)\
                            .then_inc(s["diag"], 1)

                def maximum(pair):
                    q = slice(pair.slot % Q, pair.slot % Q + 2)
                    scores = ps_e[pair.slot // 2 % 2][:, 0:2, :]
                    pair.wait(dve, s["fifth"])
                    dve.tensor_reduce(top[:, pair.both], scores, AX.X, ALU.max).then_inc(s["top"], 1)
                    dve.scalar_tensor_tensor(minus[:, q, 0:P], scores, -1.0, fifth[:, q, :], ALU.mult, ALU.min)\
                        .then_inc(s["minus"], 1)
                    pair.wait(dve, s["top"])
                    dve.scalar_tensor_tensor(top_leaky[:, pair.both], top[:, pair.both], 0.2, top[:, pair.both], ALU.mult,
                                             ALU.max).then_inc(s["leaky"], 1)

                def old_maximum(j, k):
                    pass_wait(dve, s, s["mm"], j + 1)
                    dve.scalar_tensor_tensor(minus[:, k % Q, P:P + 1], minus_max[:, (k - 1) % RING:(k - 1) % RING + 1],
                                             graph.keep[:, bass.ds(j, 1)], restart[:, bass.ds(j, 1)], ALU.mult, ALU.add)\
                        .then_inc(s["old"], 1)

                def new_maximum(pair, j, k):
                    pass_wait(dve, s, s["leaky"], pair.number + 1)
                    dve.wait_ge(s["old"], j + 1)
                    dve.scalar_tensor_tensor(minus_max[:, k:k + 1], top_leaky[:, k:k + 1], -1.0, minus[:, k % Q, P:P + 1],
                                             ALU.mult, ALU.min).then_inc(s["mm"], 1)

                def rescale(pair):
                    corr = expo[:, pair.both, P]
                    pair.wait_items(dve, s["expo"])
                    dve.tensor_tensor(scale_old[:, pair.both], corr, graph.keep[:, bass.ds(pair.item, 2)], ALU.mult)\
                        .then_inc(s["c1"], 1)
                    dve.tensor_tensor(fresh[:, pair.both], sums[:, pair.both], corr, ALU.subtract).then_inc(s["c2"], 1)

                def ready_to_add(pair):
                    pass_wait(dve, s, s["c2"], pair.number + 1)
                    pass_wait(dve, s, s["agg_done"], pair.item + 2)
                    for j, k in pair.each():
                        pass_wait(dve, s, in_again[k], (pair.lap + 1) * 16)

                def add_up(j, k):
                    before = (k - 1) % RING
                    pass_wait(dve, s, s["agg"], j + 1)
                    dve.scalar_tensor_tensor(denom[:, k:k + 1], denom[:, before:before + 1], scale_old[:, k:k + 1],
                                             fresh[:, k:k + 1], ALU.mult, ALU.add).then_inc(s["den"], 1)
                    dve.scalar_tensor_tensor(agg[:, k, :], agg[:, before, :], scale_old[:, k:k + 1],
                                             ps_g[:, k % 2, :], ALU.mult, ALU.add).then_inc(s["agg"], 1)

                def guard(pair):
                    pair.wait_items(dve, s["den"])
                    dve.tensor_scalar(guarded[:, pair.both], denom[:, pair.both], 1e-30, None, ALU.max)\
                        .then_inc(s["guarded"], 1)

                def invert(pair):
                    pair.wait(dve, s["guarded"])
                    dve.reciprocal(inverse[:, pair.both], guarded[:, pair.both]).then_inc(s["inverted"], 1)

                def ready_to_add_self(pair):
                    pass_wait(dve, s, s["inverted"], pair.number + 1)

                def add_self(j, k):
                    dve.wait_ge(s["agg"], j + 2)
                    dve.scalar_tensor_tensor(y[:, k, :], agg[:, k, :], inverse[:, k:k + 1], x_again[:, k, :], ALU.mult,
                                             ALU.add).then_inc(s["y"], 1)

                def have_square(pair):
                    pair.wait_items(dve, s["squared"])
                    dve.tensor_scalar(inv.v[:, pair.both], total_sq[:, pair.both], TINY, None, ALU.max).then_inc(inv.have_v, 1)

                def add_residual(pair):
                    pass_wait(dve, s, inv.done, pair.number + 1)
                    for j, k in pair.each():
                        dve.wait_ge(s["in_res"][k], (pair.lap + 1) * 16)
                        dve.scalar_tensor_tensor(summed[:, k, :], y[:, k, :], inv.root[:, k:k + 1], res[:, k, :],
                                                 ALU.mult, ALU.add, accum_out=norm.sum[:, k:k + 1]).then_inc(s["summed"], 1)

                def centre(pair):
                    pair.wait_items(dve, s["summed"])
                    norm.centre(dve, pair)

                def have_variance(pair):
                    pair.wait_items(dve, norm.squared)
                    dve.tensor_scalar(inv2.v[:, pair.both], norm.squares[:, pair.both], 1.0 / D, EPS, ALU.mult, ALU.add)\
                        .then_inc(inv2.have_v, 1)

                def shift_bias(pair):
                    pair.wait(dve, inv2.done)
                    dve.tensor_tensor(norm.bias[:, pair.both], norm.minus_mean[:, pair.both], inv2.root[:, pair.both],
                                      ALU.mult).then_inc(norm.shifted, 1)

                for buffer in (agg, denom, minus_max):
                    dve.memset(buffer[:], 0.0)
                dve.tensor_scalar(restart[:], graph.keep[:], FLOOR, -FLOOR, ALU.mult, ALU.add).then_inc(s["zeroed"], 1)
                dve.memset(result[:], 0.0).then_inc(s["zeroed"], 1)
                dve.wait_ge(s["zeroed"], 2)
                dve.sem_inc(s["mm"], 1)
                dve.sem_inc(s["agg"], 1)
                first, second = (lambda pair: pair.each()[0]), (lambda pair: pair.each()[1])
                steps = [(lambda p: inv2.square(dve, p), 0)] if last_hop else []
                steps += [(lambda p: inv.square(dve, p), r), (rescale, r + 2)]
                steps += [(lambda p: inv2.weigh(dve, p), 0)] if last_hop else []
                steps += [(lambda p: inv.weigh(dve, p), r), (score, r + 5)]
                steps += [(lambda p: inv2.improve(dve, p), 0)] if last_hop else []
                steps += [(lambda p: inv.improve(dve, p), r), (diagonal, r + 5)]
                steps += [(shift_bias, 0), (add_residual, r)] if last_hop else []
                steps += [(have_square, r + 1)] + ([(have_variance, r - 1)] if last_hop else [])
                steps += [(ready_to_add, r + 2), (lambda p: add_up(*first(p)), r + 2), (maximum, r + 4),
                          (lambda p: add_up(*second(p)), r + 2), (lambda p: make(*first(p)), r + 8), (guard, r + 2),
                          (lambda p: old_maximum(*first(p)), r + 4), (invert, r + 2),
                          (lambda p: new_maximum(p, *first(p)), r + 4), (ready_to_add_self, r + 2),
                          (lambda p: add_self(*first(p)), r + 2), (lambda p: old_maximum(*second(p)), r + 4),
                          (lambda p: add_self(*second(p)), r + 2), (lambda p: new_maximum(p, *second(p)), r + 4)]
                steps += [(centre, r)] if last_hop else []
                steps += [(lambda p: make(*second(p)), r + 8)]
                run_pairs(dve, graph, steps)

            @block.scalar
            def _(act):
                def exponentials(pair):
                    for j, k in pair.each():
                        act.wait_ge(s["mm"], j + 2)
                        act.activation(expo[:, k, :], minus[:, k % Q, :], ACT.Exp, scale=-1.0,
                                       bias=minus_max[:, k:k + 1], accum_out=sums[:, k:k + 1]).then_inc(s["expo"], 1)

                def leak(pair):
                    q = slice(pair.slot % Q, pair.slot % Q + 2)
                    pair.wait(act, s["e_done"])
                    act.activation(fifth[:, q, :], ps_e[pair.slot // 2 % 2][:, 0:2, :], ACT.Copy, scale=-0.2)\
                        .then_inc(s["fifth"], 1)

                def measure(pair):
                    for j, k in pair.each():
                        act.wait_ge(s["y"], j + 1)
                        act.activation(squares[:, k % 2, :], y[:, k, :], ACT.Square, accum_out=total_sq[:, k:k + 1])\
                            .then_inc(s["squared"], 1)

                def turned_exponentials(pair):
                    q = slice(pair.slot % Q, pair.slot % Q + 2)
                    pair.wait(act, s["t_done"])
                    act.copy(expo_t[:, q, :], ps_t[:, 0:2, :]).then_inc(s["expo_t"], 1)

                def heads(pair):
                    q = slice(pair.slot % Q, pair.slot % Q + 2)
                    pair.wait(act, s["projected"])
                    act.copy(head_t[0:R2, q, :], ps_kh[0:R2, 1]).then_inc(s["ht"], 1)

                def evacuate(pair):
                    q = slice(pair.slot % Q, pair.slot % Q + 2)
                    pair.wait_items(act, s["turned"])
                    act.copy(x_t[:, q, :], ps_x[:])
                    act.copy(kind_t[:, pair.both, :], ps_kh[0:GROUP, 0]).then_inc(s["evacuated"], 1)

                def scale_rows(pair):
                    pass_wait(act, s, inv.done, pair.number + 1)
                    for _, k in pair.each():
                        act.wait_ge(s["stored"][k], (pair.lap + 1) * 16)
                        act.activation(result[:, k, :], y[:, k, :], ACT.Copy, scale=inv.root[:, k:k + 1])\
                            .then_inc(s["out_ready"], 1)

                act.preload_act_table_set("natural_log_exp_and_others")
                steps = [(leak, r + 4), (measure, r + 1)]
                steps += [(lambda p: norm.square(act, p, summed), r - 1)] if last_hop else []
                steps += [(turned_exponentials, r + 3), (lambda p: inv.guess(act, shift, p), r + 1)]
                steps += [(lambda p: inv2.guess(act, shift, p), r - 1)] if last_hop else []
                steps += [(heads, r + 6), (evacuate, r + 7)]
                steps += [(lambda p: norm.apply(act, s, p, result, summed, inv2.root), 0)] if last_hop else [(scale_rows, 0)]
                steps += [(exponentials, r + 4)]
                run_pairs(act, graph, steps)

            @block.tensor
            def _(pe):
                def turn(pair):
                    dynamic = not isinstance(pair.number, int)
                    if dynamic or pair.number > 0:
                        pe.wait_ge(s["evacuated"], pair.number)
                    if dynamic or pair.number > 1:
                        pe.wait_ge(s["ht"], pair.number - 1)
                    for j, k in pair.each():
                        pe.wait_ge(s["made"], j + 1)
                        pe.transpose(ps_kh[0:GROUP, 0, k % 2, :], kind[:, k, :], c.ident[:])
                        pe.wait_ge(s["in_x"][k], (pair.lap + 1) * 16)
                        for f in range(2):
                            last = pe.transpose(ps_x[:, k % 2, f * P:(f + 1) * P], x[:, k, f * P:(f + 1) * P], c.ident[:])
                        last.then_inc(s["turned"], 1)

                def project(pair):
                    q = slice(pair.slot % Q, pair.slot % Q + 2)
                    if not isinstance(pair.number, int) or pair.number > 0:
                        pe.wait_ge(s["tail"], pair.item)
                    pair.wait(pe, s["evacuated"])
                    for j, k in pair.each():
                        pe.matmul(ps_w[k % 2][:, 0:D + 1], kind_t[0:R2, k, :], tail_w[0:R2, :], start=True, stop=True)
                    for j, k in pair.each():
                        for f in range(2):
                            last = pe.matmul(ps_kh[0:R2, 1, k % 2, :], head_w[:, f, 0:R2], x_t[:, k % Q, f * P:(f + 1) * P],
                                             start=(f == 0), stop=(f == 1))
                    last.then_inc(s["projected"], 1)

                def scores(pair):
                    pair.wait(pe, s["ht"])
                    for j, k in pair.each():
                        out = ps_e[k // 2 % 2][:, k % 2, :]
                        pe.matmul(out, mask[:, k, :], c.ident_b[:], start=True, stop=False)
                        pe.matmul(out, head_t[0:R2, k % Q, :], kind_t[0:R2, k, :], start=False, stop=False)
                        pe.wait_ge(s["diag"], j + 1)
                        last = pe.matmul(out, c.ones[:], diag[:, k % Q, :], start=False, stop=True)
                    last.then_inc(s["e_done"], 1)

                def transpose(pair):
                    for j, k in pair.each():
                        pe.wait_ge(s["expo"], j + 1)
                        last = pe.transpose(ps_t[:, k % 2, :], expo[:, k, 0:P], c.ident[:])
                    last.then_inc(s["t_done"], 1)

                def aggregate(pair):
                    pair.wait(pe, s["expo_t"])
                    pe.wait_ge(s["agg"], pair.item + 1)
                    for j, k in pair.each():
                        pe.wait_ge(s["in_g"][k], (pair.lap + 1) * 16)
                        pe.matmul(ps_g[:, k % 2, :], expo_t[:, k % Q, :], gathered[:, k, 0:D], start=True, stop=True)\
                            .then_inc(s["agg_done"], 1)

                run_pairs(pe, graph, ((aggregate, r + 2), (transpose, r + 3), (turn, r + 7), (project, r + 6),
                                      (scores, r + 5)))


class Weights:
    def __init__(self, sb):
        self.l0 = sb("l0_w", [P, 4, D], F32)
        self.gamma, self.beta = sb("gamma", [P, D], F32), sb("beta", [P, D], F32)
        self.root = [sb(f"root{k}", [P, 2, D], F32) for k in range(2)]
        self.table = [sb(f"blocks{k}", [K3, 4 * D], BF16) for k in range(2)]
        self.bias = [sb(f"l1_bias{k}", [P, D], F32) for k in range(2)]
        self.head = sb("head_w", [P, 2, GROUP], F32)
        self.tail = sb("tail_w", [GROUP, D + 1], F32)
        self.l3 = [sb(f"l3_w{k}", [P, 2, D], F32) for k in range(2)]
        self.l3_bias = sb("l3_bias", [P, D], F32)
        self.eps = sb("eps", [P, 1], F32)
        self.shift = sb("shift", [P, 1], F32)


def load_weights(nc, c, w, a):
    with Phase(nc, "weights") as ph:
        full = [ph.sb(f"full{k}", [K3, 4 * D], F32) for k in range(2)]
        rest = [ph.sb(f"rest{k}", [K3, 4 * D], F32) for k in range(2)]
        piece = [ph.sb(f"piece{k}", [K3, 4 * D], BF16) for k in range(2)]
        fc = ph.sb("fc", [P, 2, 2 * D + 1], F32)
        rel = ph.sb("rel", [P, 2, R2], F32)
        bias2 = ph.sb("bias2", [P, D], F32)
        ps_h = ph.ps("h", [P, 2 * D])
        ps_t = ph.ps("t", [P, 2 * D])
        s_in, s_zero, s_v, s_fc = ph.sem("in"), ph.sem("zero"), ph.sem("v"), ph.sem("fc")
        with nc.Block() as block:
            @block.sync
            def _(sp):
                n = 0
                halves = "(b p) o -> p b o"
                for dst, src in ((w.l0[:], a["L0_gnn_W"].rearrange(halves, p=P)),
                                 (w.root[0][:], a["L1_gnn_root1"].rearrange(halves, p=P)),
                                 (w.root[1][:], a["L1_gnn_root2"].rearrange(halves, p=P)),
                                 (w.l3[0][:], a["L3_gnn_W1"].rearrange(halves, p=P)),
                                 (w.l3[1][:], a["L3_gnn_W2"].rearrange(halves, p=P)),
                                 (fc[:, :, 0:2 * D], a["L2_gnn_fc_w"].rearrange(halves, p=P)),
                                 (rel[:], a["L2_gnn_relation_emb"].rearrange(halves, p=P)),
                                 (w.gamma[:], a["L0_gnn_gamma"].partition_broadcast(P)),
                                 (w.beta[:], a["L0_gnn_beta"].partition_broadcast(P)),
                                 (w.bias[0][:], a["L1_gnn_bias1"].partition_broadcast(P)),
                                 (w.bias[1][:], a["L1_gnn_bias2"].partition_broadcast(P)),
                                 (w.l3_bias[:], a["L3_gnn_b1"].partition_broadcast(P)),
                                 (bias2[:], a["L3_gnn_b2"].partition_broadcast(P))):
                    sp.dma_start(dst, src).then_inc(s_in, 16)
                    n += 16
                with nc.allow_non_contiguous_dma(reason="256 values once"):
                    sp.dma_start(fc[:, :, 2 * D:], a["L2_gnn_fc_b"].rearrange("(b p o) -> p b o", p=P, o=1)).then_inc(s_in, 16)
                n += 16
                sp.wait_ge(s_zero, 1)
                for k in range(2):
                    for part in range(3):
                        sp.dma_start(full[k][part * GROUP:part * GROUP + R1, :], a[f"L1_gnn_W{k + 1}"]).then_inc(s_in, 16)
                        n += 16
                assert n == 20 * 16
                sp.wait_ge(s_in, n)

            @block.vector
            def _(dve):
                chain = Chain(dve, s_v)
                for k in range(2):
                    chain.step(dve.memset(full[k][:], 0.0))
                dve.memset(w.eps[:], EPS).then_inc(s_zero, 1)
                dve.memset(w.shift[:], float(np.log(2.0) * LN_SCALE / 2))
                dve.wait_ge(s_in, 20 * 16)
                for k in range(2):
                    source = full[k]
                    for part in range(3):
                        rows = slice(part * GROUP, (part + 1) * GROUP)
                        chain.step(dve.tensor_copy(piece[k][:], source[:]))
                        chain.step(dve.tensor_copy(w.table[k][rows, :], piece[k][rows, :]))
                        chain.step(dve.tensor_tensor(rest[k][:], source[:], piece[k][:], ALU.subtract))
                        source = rest[k]
                chain.step(dve.tensor_tensor(w.l3_bias[:], w.l3_bias[:], bias2[:], ALU.add))
                dve.wait_ge(s_fc, 1)
                for f in range(2):
                    chain.step(dve.tensor_copy(w.head[:, f, 0:R2], ps_h[:, f * GROUP:f * GROUP + R2]))
                chain.step(dve.tensor_copy(w.tail[0:R2, :], ps_t[0:R2, 0:D + 1]))

            @block.tensor
            def _(pe):
                pe.wait_ge(s_in, 20 * 16)
                for f in range(2):
                    for b in range(2):
                        pe.matmul(ps_h[:, f * GROUP:f * GROUP + R2], fc[:, b, f * P:(f + 1) * P], rel[:, b, :],
                                  start=(b == 0), stop=(b == 1))
                for b in range(2):
                    last = pe.matmul(ps_t[0:R2, 0:D + 1], rel[:, b, :], fc[:, b, D:], start=(b == 0), stop=(b == 1))
                last.then_inc(s_fc, 1)


def build(nc, a, out):
    def dram(name, shape, dt=F32):
        return nc.dram_tensor(name, shape, dt).ap()

    with ExitStack() as ctx:
        def sb(name, shape, dt):
            return ctx.enter_context(nc.sbuf_tensor(name, shape, dt))

        c, w = Constants(sb), Weights(sb)
        graphs = [Graph(sb, "by_src"), Graph(sb, "by_dst")]
        item_records = [dram(f"item_records{o}", (P * ITEMS, 4)) for o in range(2)]
        item_rows = [(dram(f"rows_i{o}", (3, ITEMS), I32), dram(f"rows_f{o}", (ITEMS,))) for o in range(2)]
        node_rows = dram("node_rows", (ITEMS, P), F16)
        x1, h, x2, z, x3 = (dram(n, (ALL_ROWS, D)) for n in ("x1", "h", "x2", "z", "x3"))
        make_constants(nc, c)
        with ExitStack() as prep:
            def sb_prep(name, shape, dt):
                return prep.enter_context(nc.sbuf_tensor(name, shape, dt))
            for g, n in zip(graphs, ("src", "dst")):
                g.prepare(sb_prep, n)
            sort_edges(nc, c, [a[n] for n in ("src", "dst", "edge_type_16", "edge_type_24", "edge_weight")],
                       graphs, item_records)
            make_items(nc, c, graphs, item_records, item_rows)
        load_weights(nc, c, w, a)
        by_src, by_dst = graphs
        count_edges(nc, c, by_dst, node_rows)
        mean_layer(nc, c, by_src, w.l0, w.gamma, w.beta, w.eps, a["x"], x1)
        relation_layer(nc, c, by_dst, "l1a", w.root[0], w.table[0], w.bias[0], w.eps, x1, h)
        relation_layer(nc, c, by_dst, "l1b", w.root[1], w.table[1], w.bias[1], w.eps, h, x2, residual=x1)
        attention_hop(nc, c, by_src, "l2a", w.head, w.tail, w.shift, x2, z)
        attention_hop(nc, c, by_src, "l2b", w.head, w.tail, w.shift, z, x3, residual=x2)
        interaction_layer(nc, c, by_dst, w.l3[0], w.l3[1], w.l3_bias, w.eps, x3, out)


def laid_out(inputs):
    a = {k: np.asarray(v) for k, v in inputs.items()}
    x = np.zeros((ALL_ROWS, D), np.float32)
    x[:N_NODES] = a["x"]
    a["x"] = x
    for k in ("L0_gnn_W", "L2_gnn_relation_emb", "L3_gnn_W1", "L3_gnn_W2"):
        a[k] = a[k].T
    for k in ("L1_gnn_W1", "L1_gnn_W2"):
        a[k] = a[k].transpose(0, 2, 1, 3).reshape(R1, 4 * D)
    return {k: np.ascontiguousarray(v) for k, v in a.items()}


def kernel(**inputs):
    import concourse.bacc as bacc
    from concourse.bass_utils import run_bass_kernel_spmd

    nc = bacc.Bacc("TRN2", target_bir_lowering=False, num_devices=1)
    arrays = {f"in_{k}": v for k, v in laid_out(inputs).items()}
    aps = {k[3:]: nc.dram_tensor(k, v.shape, mybir.dt.from_np(v.dtype), kind="ExternalInput").ap()
           for k, v in arrays.items()}
    out = nc.dram_tensor("out", (ALL_ROWS, D), F32, kind="ExternalOutput").ap()
    build(nc, aps, out)
    r = run_bass_kernel_spmd(nc, [arrays], core_ids=[0])
    return r.results[0]["out"][:N_NODES]
```
